# Optimizing a Trainium2 kernel written in Bass

```python
import numpy as np
import jax
import jax.numpy as jnp

def _softmax(x, axis=-1):
    return jax.nn.softmax(x, axis=axis)

def _gelu(x):
    return jax.nn.gelu(x, approximate=True)

def _silu(x):
    return jax.nn.silu(x)

def _sigmoid(x):
    return jax.nn.sigmoid(x)

def _layernorm(x, axis=-1, eps=1e-05):
    m = jnp.mean(x, axis=axis, keepdims=True)
    v = jnp.var(x, axis=axis, keepdims=True)
    return (x - m) / jnp.sqrt(v + eps)

def _scatter_add(tgt, idx, src, axis=0):
    return tgt.at[idx].add(src)

def _segment_sum(src, seg, n):
    return jax.ops.segment_sum(src, seg, n)
kernel_name = 'mk_sandwich_d1_jaxref_r4_f4a655'

def setup_inputs(seed: int=0):
    np.random.seed(seed)
    _w = jnp.asarray

    def _L0_attn_setup():
        import jax, jax.numpy as jnp
        import numpy as np
        D_MODEL, D_STATE, D_CONV, EXPAND = (256, 16, 4, 2)
        D_INNER = EXPAND * D_MODEL
        EPS = 1e-06

        def _forward(x, norm_w, in_proj_w, conv_w, dt_w, dt_b, A_log, B_w, C_w, D_skip, out_proj_w):
            Bsz, T, _ = x.shape
            xn = x * jax.lax.rsqrt(jnp.mean(x * x, axis=-1, keepdims=True) + EPS) * norm_w
            xg = xn @ in_proj_w
            x_inner, gate = jnp.split(xg, 2, axis=-1)
            x_inner = x_inner * jax.nn.silu(gate)
            xc = jax.lax.conv_general_dilated(x_inner.transpose(0, 2, 1), conv_w, window_strides=(1,), padding=[(D_CONV - 1, 0)], feature_group_count=D_INNER, dimension_numbers=('NCH', 'OIH', 'NCH')).transpose(0, 2, 1)
            dt = jax.nn.softplus(xc @ dt_w + dt_b)
            A = -jnp.exp(A_log)
            Bm = xc @ B_w
            Cm = xc @ C_w
            A_bar = jnp.exp(dt[..., None] * A)
            B_bar = dt[..., None] * Bm[:, :, None, :]

            def step(h, inp):
                a_t, b_t, xc_t, c_t = inp
                h = a_t * h + b_t * xc_t[..., None]
                y = jnp.einsum('bds,bs->bd', h, c_t) + D_skip * xc_t
                return (h, y)
            h0 = jnp.zeros((Bsz, D_INNER, D_STATE), x.dtype)
            xs = (A_bar.transpose(1, 0, 2, 3), B_bar.transpose(1, 0, 2, 3), xc.transpose(1, 0, 2), Cm.transpose(1, 0, 2))
            _, ys = jax.lax.scan(step, h0, xs)
            out = ys.transpose(1, 0, 2) @ out_proj_w
            return out
        key = jax.random.key(seed)
        ks = jax.random.split(key, 8)
        B, T = (2, 256)
        s = lambda fan_in: 1.0 / np.sqrt(fan_in)
        x = jax.random.normal(ks[0], (B, T, D_MODEL), dtype=jnp.float32)
        norm_w = jnp.ones((D_MODEL,), jnp.float32)
        in_proj_w = jax.random.normal(ks[1], (D_MODEL, 2 * D_INNER), jnp.float32) * s(D_MODEL)
        conv_w = jax.random.normal(ks[2], (D_INNER, 1, D_CONV), jnp.float32) * s(D_CONV)
        dt_w = jax.random.normal(ks[3], (D_INNER, D_INNER), jnp.float32) * s(D_INNER)
        dt_b = jnp.zeros((D_INNER,), jnp.float32)
        A_log = jnp.log(jnp.broadcast_to(jnp.arange(1, D_STATE + 1, dtype=jnp.float32), (D_INNER, D_STATE)))
        B_w = jax.random.normal(ks[4], (D_INNER, D_STATE), jnp.float32) * s(D_INNER)
        C_w = jax.random.normal(ks[5], (D_INNER, D_STATE), jnp.float32) * s(D_INNER)
        D_skip = jnp.ones((D_INNER,), jnp.float32)
        out_proj_w = jax.random.normal(ks[6], (D_INNER, D_MODEL), jnp.float32) * s(D_INNER)
        return {'x': x, 'norm_w': norm_w, 'in_proj_w': in_proj_w, 'conv_w': conv_w, 'dt_w': dt_w, 'dt_b': dt_b, 'A_log': A_log, 'B_w': B_w, 'C_w': C_w, 'D_skip': D_skip, 'out_proj_w': out_proj_w}
    _L0_attn_in = _L0_attn_setup()

    def _L0_ffn_setup():
        import jax, jax.numpy as jnp
        import numpy as np
        B, S = (4, 128)
        H = 256
        I = 704
        E = 8
        K = 2
        IS = 352
        key = jax.random.key(seed)
        ks = jax.random.split(key, 8)

        def init(k, shape, fan_in):
            return (jax.random.normal(k, shape, jnp.float32) / np.sqrt(fan_in)).astype(jnp.float32)
        return {'hidden_states': jax.random.normal(ks[0], (B, S, H), jnp.float32), 'gate_w': init(ks[1], (H, E), H), 'Wg': init(ks[2], (E, H, I), H), 'Wu': init(ks[3], (E, H, I), H), 'Wd': init(ks[4], (E, I, H), I), 'Sg': init(ks[5], (H, IS), H), 'Su': init(ks[6], (H, IS), H), 'Sd': init(ks[7], (IS, H), IS)}
    _L0_ffn_in = _L0_ffn_setup()
    _d = {'L0_attn_x': _L0_attn_in['x'], 'L0_attn_norm_w': _L0_attn_in['norm_w'], 'L0_attn_in_proj_w': _L0_attn_in['in_proj_w'], 'L0_attn_conv_w': _L0_attn_in['conv_w'], 'L0_attn_dt_w': _L0_attn_in['dt_w'], 'L0_attn_dt_b': _L0_attn_in['dt_b'], 'L0_attn_A_log': _L0_attn_in['A_log'], 'L0_attn_B_w': _L0_attn_in['B_w'], 'L0_attn_C_w': _L0_attn_in['C_w'], 'L0_attn_D_skip': _L0_attn_in['D_skip'], 'L0_attn_out_proj_w': _L0_attn_in['out_proj_w'], 'L0_ffn_gate_w': _L0_ffn_in['gate_w'], 'L0_ffn_Wg': _L0_ffn_in['Wg'], 'L0_ffn_Wu': _L0_ffn_in['Wu'], 'L0_ffn_Wd': _L0_ffn_in['Wd'], 'L0_ffn_Sg': _L0_ffn_in['Sg'], 'L0_ffn_Su': _L0_ffn_in['Su'], 'L0_ffn_Sd': _L0_ffn_in['Sd']}
    _x0 = _d['L0_attn_x']
    _d['L0_attn_x'] = jax.random.normal(jax.random.fold_in(jax.random.key(seed), 1), (4, 1024, 256), dtype=_x0.dtype)
    del _x0
    return _d

def reference(L0_attn_x, L0_attn_norm_w, L0_attn_in_proj_w, L0_attn_conv_w, L0_attn_dt_w, L0_attn_dt_b, L0_attn_A_log, L0_attn_B_w, L0_attn_C_w, L0_attn_D_skip, L0_attn_out_proj_w, L0_ffn_gate_w, L0_ffn_Wg, L0_ffn_Wu, L0_ffn_Wd, L0_ffn_Sg, L0_ffn_Su, L0_ffn_Sd):

    def _L0_attn_ref(x, norm_w, in_proj_w, conv_w, dt_w, dt_b, A_log, B_w, C_w, D_skip, out_proj_w):
        import jax, jax.numpy as jnp
        import numpy as np
        D_MODEL, D_STATE, D_CONV, EXPAND = (256, 16, 4, 2)
        D_INNER = EXPAND * D_MODEL
        EPS = 1e-06

        def _forward(x, norm_w, in_proj_w, conv_w, dt_w, dt_b, A_log, B_w, C_w, D_skip, out_proj_w):
            Bsz, T, _ = x.shape
            xn = x * jax.lax.rsqrt(jnp.mean(x * x, axis=-1, keepdims=True) + EPS) * norm_w
            xg = xn @ in_proj_w
            x_inner, gate = jnp.split(xg, 2, axis=-1)
            x_inner = x_inner * jax.nn.silu(gate)
            xc = jax.lax.conv_general_dilated(x_inner.transpose(0, 2, 1), conv_w, window_strides=(1,), padding=[(D_CONV - 1, 0)], feature_group_count=D_INNER, dimension_numbers=('NCH', 'OIH', 'NCH')).transpose(0, 2, 1)
            dt = jax.nn.softplus(xc @ dt_w + dt_b)
            A = -jnp.exp(A_log)
            Bm = xc @ B_w
            Cm = xc @ C_w
            A_bar = jnp.exp(dt[..., None] * A)
            B_bar = dt[..., None] * Bm[:, :, None, :]

            def step(h, inp):
                a_t, b_t, xc_t, c_t = inp
                h = a_t * h + b_t * xc_t[..., None]
                y = jnp.einsum('bds,bs->bd', h, c_t) + D_skip * xc_t
                return (h, y)
            h0 = jnp.zeros((Bsz, D_INNER, D_STATE), x.dtype)
            xs = (A_bar.transpose(1, 0, 2, 3), B_bar.transpose(1, 0, 2, 3), xc.transpose(1, 0, 2), Cm.transpose(1, 0, 2))
            _, ys = jax.lax.scan(step, h0, xs)
            out = ys.transpose(1, 0, 2) @ out_proj_w
            return out
        return _forward(x, norm_w, in_proj_w, conv_w, dt_w, dt_b, A_log, B_w, C_w, D_skip, out_proj_w)

    def _L0_ffn_ref(hidden_states, gate_w, Wg, Wu, Wd, Sg, Su, Sd):
        import jax, jax.numpy as jnp
        import numpy as np
        B, S = (4, 128)
        H = 256
        I = 704
        E = 8
        K = 2
        IS = 352
        b, s, h = hidden_states.shape
        x = hidden_states.reshape(-1, h)
        T = x.shape[0]
        logits = x @ gate_w
        top_v, top_i = jax.lax.top_k(logits, K)
        top_p = jax.nn.softmax(top_v, axis=-1)
        combine = jnp.zeros((T, E), x.dtype).at[jnp.arange(T)[:, None], top_i].add(top_p)
        g = jnp.einsum('th,ehi->tei', x, Wg)
        u = jnp.einsum('th,ehi->tei', x, Wu)
        d = jnp.einsum('tei,eih->teh', jax.nn.silu(g) * u, Wd)
        expert_out = jnp.einsum('te,teh->th', combine, d)
        shared = jax.nn.silu(x @ Sg) * (x @ Su) @ Sd
        return (expert_out + shared).reshape(b, s, h)
    x = L0_attn_x
    x = x + _layernorm(_L0_attn_ref(_layernorm(x, axis=-1), L0_attn_norm_w, L0_attn_in_proj_w, L0_attn_conv_w, L0_attn_dt_w, L0_attn_dt_b, L0_attn_A_log, L0_attn_B_w, L0_attn_C_w, L0_attn_D_skip, L0_attn_out_proj_w), axis=-1)
    x = x + _layernorm(_L0_ffn_ref(_layernorm(x, axis=-1), L0_ffn_gate_w, L0_ffn_Wg, L0_ffn_Wu, L0_ffn_Wd, L0_ffn_Sg, L0_ffn_Su, L0_ffn_Sd), axis=-1)
    return x

_drawn_inputs = setup_inputs


def setup_inputs(seed=0):
    import zlib

    import numpy as np

    out = dict(_drawn_inputs(seed))
    spreads = {'L0_attn_norm_w': (1.0, 0.2), 'L0_attn_dt_b': (0.0, 0.1), 'L0_attn_D_skip': (1.0, 0.2)}
    factors = {}
    for name, (base, spread) in spreads.items():
        noise = np.random.default_rng([zlib.crc32(name.encode()), seed]).standard_normal(out[name].shape)
        drawn = base * np.exp(spread * noise) if base else spread * noise
        out[name] = jnp.asarray(drawn.astype(out[name].dtype))
    for name, factor in factors.items():
        out[name] = (out[name] * factor).astype(out[name].dtype)
    return out
```

```python
from collections import defaultdict
from contextlib import ExitStack

import numpy as np
import concourse.bass as bass
from concourse import mybir

F32 = mybir.dt.float32
I32 = mybir.dt.int32
U32 = mybir.dt.uint32
ALU = mybir.AluOpType
ACT = mybir.ActivationFunctionType
AX = mybir.AxisListType
POOL = mybir.EngineType.Pool
SYNC = mybir.EngineType.SP

P = 128
DM = 256
DI = 512
NS = 16
TAPS = 4
E = 8
TOPK = 2
FI = 704
SI = 352
NTOK = 4096
CH = 512
NCH = NTOK // CH
J = CH // P
KD = DM // P
ND = DI // P
SLOTS = NS * ND
CAP = NTOK + P
NT = NTOK * TOPK // P + E - 1
EPS_LN = 1e-5
EPS_RMS = 1e-6
SIT = [(t * P, min(P, SI - t * P)) for t in range((SI + P - 1) // P)]
FIT = [(t * P, min(P, FI - t * P)) for t in range((FI + P - 1) // P)]
FH = FI // 2
BU = {"A0": 2 + ND + ND, "A1": 1 + ND + ND, "A2": 9, "A3": 9}


class Chunk:

    def __init__(self, add, reg=None):
        self.add, self.reg = add, reg

    def shift(self, by):
        return Chunk(self.add + by, self.reg)

    def times(self, n, plus=0):
        if self.reg is None:
            return self.add * n + plus
        return self.reg * (2 * n) + (self.add * n + plus)


def wait(eng, sem, per, c, k):
    v = c.times(per, k + 1)
    if isinstance(v, int) and v <= 0:
        return
    eng.wait_ge(sem, v)
    if not isinstance(v, int) and eng.engine in (POOL, SYNC):
        eng.nop(nofuse=True)


def then(eng, ins):
    eng.drain()


def build(nc, x, norm_w, in_proj_w, conv_w, dt_w, dt_b, A_log, B_w, C_w, D_skip, out_proj_w,
          gate_w, Wg, Wu, Wd, Sg, Su, Sd, out):
    x_rows = x.rearrange("b t d -> (b t) d")
    out_rows = out.rearrange("b t d -> (b t) d")

    x1_d = nc.dram_tensor("x1_scratch", (NTOK, DM), F32).ap()
    sh_d = nc.dram_tensor("shared_scratch", (NTOK, DM), F32).ap()
    xs_d = nc.dram_tensor("expert_in_scratch", (E * CAP, DM), F32).ap()
    ys_d = nc.dram_tensor("expert_out_scratch", (NT * P, DM), F32).ap()

    with ExitStack() as top:
        def sem(name):
            return top.enter_context(nc.semaphore(name))

        def sbp(name, shape, dt=F32):
            return top.enter_context(nc.sbuf_tensor(name, shape, dt))

        ident = sbp("ident", [P, P])
        base = sbp("base", [P, E])
        posi = sbp("posi", [P, NTOK // P, TOPK], U32)
        posa = sbp("posa", [P, NTOK // P, TOPK])
        expa = sbp("expa", [P, NTOK // P, TOPK])
        gat = sbp("gat", [P, NTOK // P, TOPK])
        padi = sbp("padi", [P, E], U32)
        tab = sbp("tab", [1, 2, NT + 1], I32)

        phase1(nc, sem, x_rows, norm_w, in_proj_w, conv_w, dt_w, dt_b, A_log, B_w, C_w, D_skip,
               out_proj_w, gate_w, Sg, Su, Sd, x1_d, sh_d, xs_d, ident, base, posi, posa, expa, gat, padi, tab)
        phase2(nc, sem, Wg, Wu, Wd, x1_d, sh_d, xs_d, ys_d, out_rows, ident, posi, gat, tab)


def phase1(nc, sem, x_rows, norm_w, in_proj_w, conv_w, dt_w, dt_b, A_log, B_w, C_w, D_skip,
           out_proj_w, gate_w, Sg, Su, Sd, x1_d, sh_d, xs_d, ident, base, posi, posa, expa, gat, padi, tab):
    with ExitStack() as ctx:
        def sb(name, shape, dt=F32):
            return ctx.enter_context(nc.sbuf_tensor(name, shape, dt))

        def bank(name):
            return ctx.enter_context(nc.psum_tensor(name, [P, 512], F32))

        w_in = sb("w_in", [P, KD, 2 * DI])
        w_dt = sb("w_dt", [P, ND, DI])
        w_bc = sb("w_bc", [P, ND, 2 * NS])
        w_out = sb("w_out", [P, ND, DM])
        w_cv = sb("w_cv", [P, ND, TAPS])
        w_nm = sb("w_nm", [P, KD])
        b_dt = sb("b_dt", [P, ND])
        a_log = sb("a_log", [P, ND, NS])
        a_exp = sb("a_exp", [P, ND, NS])
        a_neg = sb("a_neg", [P, ND, NS])
        dskip = sb("dskip", [P, ND])
        w_gt = sb("w_gt", [P, KD, E])
        w_sg = sb("w_sg", [P, KD, SI])
        w_su = sb("w_su", [P, KD, SI])
        w_sd = sb("w_sd", [P, len(SIT), DM])
        ones = sb("ones", [P, P])
        below = sb("below", [P, P])
        iota_e = sb("iota_e", [P, E])
        iota_i = sb("iota_i", [P, E], I32)
        capi = sb("capi", [P, E], I32)
        xp = sb("xp", [P, J, DM])
        st = sb("st", [P, J, 6])
        mv = sb("mv", [P, J, 2])
        va = sb("va", [P, J])
        r0 = sb("r0", [P, J])
        tn = sb("tn", [P, J])
        nmr = sb("nmr", [P, J])
        xn = sb("xn", [P, J, DM])
        xnT = sb("xnT", [P, KD, CH])
        sg = sb("sg", [P, 2, CH])
        xin = sb("xin", [P, ND, TAPS - 1 + CH])
        xc = [sb(f"xc{i}", [P, ND, CH]) for i in range(2)]
        dt = [sb(f"dt{i}", [P, ND, CH]) for i in range(2)]
        uT = [sb(f"uT{i}", [P, J, DI]) for i in range(2)]
        bc = [sb(f"bc{i}", [P, J, 2 * NS]) for i in range(2)]
        rl = sb("rl", [P, 2, CH])
        uu = sb("uu", [P, 2, CH])
        ub = sb("ub", [P, 2, J, DI])
        NA = 4
        ab = sb("ab", [P, NA, CH])
        hh = sb("hh", [P, 2, ND, CH])
        hl = sb("hl", [P, NS, ND])
        yT = [sb(f"yT{i}", [P, J, DI]) for i in range(2)]
        xr = sb("xr", [P, J, DM])
        st2 = sb("st2", [P, J, 6])
        mv2 = sb("mv2", [P, J, 2])
        va2 = sb("va2", [P, J])
        r2 = sb("r2", [P, J])
        tn2 = sb("tn2", [P, J])
        nmr2 = sb("nmr2", [P, J])
        on = sb("on", [P, J, DM])
        xf = sb("xf", [P, J, DM])
        xfT = sb("xfT", [P, KD, CH])
        lg = sb("lg", [P, J, E])
        mx = sb("mx", [P, J, E])
        ix = sb("ix", [P, J, E], U32)
        ixf = sb("ixf", [P, J, TOPK])
        oh = sb("oh", [P, TOPK, J, E])
        mm_ = sb("mm_", [P, J, E])
        dif = sb("dif", [P, J])
        e2 = sb("e2", [P, J])
        e2p = sb("e2p", [P, J])
        p1 = sb("p1", [P, J])
        pos8 = sb("pos8", [P, J, E])
        prd = sb("prd", [P, TOPK, J, E])
        posf = sb("posf", [P, J, TOPK])
        posl = sb("posl", [P, J, TOPK], U32)
        sgs = sb("sgs", [P, 2, CH])
        hs = sb("hs", [P, len(SIT), CH])
        sh = sb("sh", [P, J, DM])
        cnt = sb("cnt", [P, E])
        cnti = sb("cnti", [P, E], I32)
        nti = sb("nti", [P, E], I32)
        ntf = sb("ntf", [P, E])
        one8 = sb("one8", [P, E])
        cum = sb("cum", [P, E])
        tot = sb("tot", [1, 1])
        off = sb("off", [P, E])
        capf = sb("capf", [P, E])
        adj = sb("adj", [P, NTOK // P * TOPK])
        tii = sb("tii", [1, NT + 1], I32)
        tif = sb("tif", [1, NT + 1])
        ge = sb("ge", [1, NT + 1])
        te = sb("te", [1, NT + 1])
        tp = sb("tp", [1, NT + 1])
        iop = sb("iop", [P, 1], I32)
        iopf = sb("iopf", [P, 1])
        padf = sb("padf", [P, E])
        zro = sb("zro", [P, DM])

        bB = [bank("bB0"), bank("bB1")]
        bH = [bank("bH0"), bank("bH1")]
        A = {n: bank(n) for n in ("A0", "A1", "A2", "A3")}
        full = {n: sem(f"full_{n}") for n in A}
        free = {n: sem(f"free_{n}") for n in A}

        s_w = sem("s_w"); s_c = sem("s_c"); s_id = sem("s_id"); s_cst = sem("s_cst"); s_an = sem("s_an")
        s_x = sem("s_x"); s_p0v = sem("s_p0v"); s_p0r = sem("s_p0r"); s_p0n = sem("s_p0n"); s_xn = sem("s_xn")
        s_t0 = sem("s_t0"); s_xc = sem("s_xc"); s_ln = sem("s_ln"); s_dt = sem("s_dt"); s_u = sem("s_u")
        s_ub = sem("s_ub"); s_b = sem("s_b"); s_a = sem("s_a"); s_scan = sem("s_scan")
        s_ht = sem("s_ht"); s_y = sem("s_y"); s_hl = sem("s_hl")
        s_xr = sem("s_xr"); s_o1 = sem("s_o1"); s_o2 = sem("s_o2"); s_o3 = sem("s_o3"); s_x1 = sem("s_x1")
        s_l1 = sem("s_l1"); s_l2 = sem("s_l2"); s_l3 = sem("s_l3"); s_xf = sem("s_xf"); s_x1s = sem("s_x1s")
        s_m = sem("s_m"); s_e2 = sem("s_e2"); s_pos = sem("s_pos"); s_sc = sem("s_sc"); s_shs = sem("s_shs")
        s_pad = sem("s_pad"); s_padd = sem("s_padd")

        SP_, PE_, AC_, DV_, PO_ = "sync", "tensor", "scalar", "vector", "gpsimd"

        def fullw(eng, b, c, k):
            wait(eng, full[b], BU[b], c, k)

        def freew(eng, b, c, k):
            wait(eng, free[b], BU[b], c, k)

        def rsqrt_tail(e, r, v, t):
            then(e, e.tensor_tensor(t[:], r[:], r[:], ALU.mult))
            then(e, e.tensor_tensor(t[:], t[:], v[:], ALU.mult))
            then(e, e.tensor_scalar(t[:], t[:], -0.5, 1.5, ALU.mult, ALU.add))
            then(e, e.tensor_tensor(r[:], r[:], t[:], ALU.mult))

        def pre(c, par):
            s = defaultdict(list)

            def add(slot, eng, fn):
                s[(slot, eng)].append(fn)

            def load_x(e):
                wait(e, s_xn, J, c.shift(-1), J - 1)
                e.dma_start(xp[:], x_rows[bass.ds(c.times(CH), CH), :].rearrange("(j p) d -> p j d", p=P)).then_inc(s_x, 16)
            add(0, SP_, load_x)

            def stats(e):
                wait(e, s_x, 16, c, 15)
                for j in range(J):
                    then(e, e.bn_stats(st[:, j, :], xp[:, j, :]))
                for j in range(J):
                    then(e, e.bn_aggr(mv[:, j, :], st[:, j, :]))
                wait(e, s_p0r, 1, c.shift(-1), 0)
                e.tensor_scalar(va[:], mv[:, :, 1], 1.0 + EPS_RMS, EPS_LN * EPS_RMS, ALU.mult, ALU.add).then_inc(s_p0v, 1)
            add(2, DV_, stats)

            def root(e):
                wait(e, s_p0v, 1, c, 0)
                wait(e, s_xn, J, c.shift(-1), J - 1)
                then(e, e.activation(r0[:], va[:], ACT.Ln))
                e.activation(r0[:], r0[:], ACT.Exp, scale=-0.5).then_inc(s_p0r, 1)
            add(3, AC_, root)

            def newton(e):
                wait(e, s_p0r, 1, c, 0)
                wait(e, s_p0v, 1, c, 0)
                rsqrt_tail(e, r0, va, tn)
                e.scalar_tensor_tensor(out=nmr[:], in0=mv[:, :, 0], scalar=-1.0, in1=r0[:], op0=ALU.mult, op1=ALU.mult).then_inc(s_p0n, 1)
            add(5, DV_, newton)

            def norm(e):
                wait(e, s_p0n, 1, c, 0)
                fullw(e, "A1", c.shift(-1), 0)
                for j in range(J):
                    e.tensor_scalar(xn[:, j, :], xp[:, j, :], r0[:, j:j + 1], nmr[:, j:j + 1], ALU.mult, ALU.add).then_inc(s_xn, 1)
            add(6, PO_, norm)

            def turn_x(k):
                def f(e):
                    b = ("A0", "A1")[k]
                    wait(e, s_xn, J, c, J - 1)
                    freew(e, b, c, -1)
                    for j in range(J):
                        i = e.transpose(A[b][:, j * P:(j + 1) * P], xn[:, j, k * P:(k + 1) * P], ident[:])
                    i.then_inc(full[b], 1)
                return f

            def keep_x(k):
                def f(e):
                    b = ("A0", "A1")[k]
                    fullw(e, b, c, 0)
                    e.copy(xnT[:, k, :], A[b][:]).then_inc(free[b], 1)
                return f
            for k in range(KD):
                add(9 + k, PE_, turn_x(k))
                add(11 + k, AC_, keep_x(k))

            def p1_pe(d):
                def f(e):
                    for b, off in (("A0", DI), ("A1", 0)):
                        freew(e, b, c, d)
                        if d == 0:
                            freew(e, "A1", c, 0)
                        for k in range(KD):
                            i = e.matmul(A[b][:], w_in[:, k, off + d * P:off + (d + 1) * P], xnT[:, k, :], start=(k == 0), stop=(k == KD - 1))
                        i.then_inc(full[b], 1)
                return f

            def p1_act(d):
                def f(e):
                    fullw(e, "A0", c, 1 + d)
                    freew(e, "A1", c, 1 + d - 2)
                    e.activation(sg[:, d % 2, :], A["A0"][:], ACT.Silu).then_inc(free["A0"], 1)
                return f

            def p1_dve(d):
                def f(e):
                    wait(e, s_xc, ND, c.shift(-1), d)
                    if par:
                        then(e, e.tensor_copy(xin[:, d, 0:TAPS - 1], xin[:, d, CH:CH + TAPS - 1]))
                    else:
                        then(e, e.memset(xin[:, d, 0:TAPS - 1], 0.0))
                    freew(e, "A0", c, 1 + d)
                    fullw(e, "A1", c, 1 + d)
                    e.tensor_tensor(xin[:, d, TAPS - 1:], sg[:, d % 2, :], A["A1"][:], ALU.mult).then_inc(free["A1"], 1)
                return f

            def tap0(d):
                def f(e):
                    freew(e, "A1", c, 1 + d)
                    fullw(e, "A3", c.shift(-2), 2)
                    e.tensor_scalar(xc[par][:, d, :], xin[:, d, 0:CH], w_cv[:, d, 0:1], 1.0, ALU.mult, ALU.mult).then_inc(s_t0, 1)
                return f

            def taps(d):
                def f(e):
                    wait(e, s_t0, ND, c, d)
                    for k in range(1, TAPS):
                        i = e.scalar_tensor_tensor(out=xc[par][:, d, :], in0=xin[:, d, k:k + CH], scalar=w_cv[:, d, k:k + 1],
                                                   in1=xc[par][:, d, :], op0=ALU.mult, op1=ALU.add)
                        if k < TAPS - 1:
                            then(e, i)
                    i.then_inc(s_xc, 1)
                return f
            for d in range(ND):
                t = 17 + 4 * d
                add(t, PE_, p1_pe(d))
                add(t + 1, AC_, p1_act(d))
                add(t + 2, DV_, p1_dve(d))
                add(t + 3, PO_, tap0(d))
                add(t + 5, DV_, taps(d))

            def bc_pe(e):
                wait(e, s_xc, ND, c, ND - 1)
                freew(e, "A0", c, ND)
                for j in range(J):
                    for k in range(ND):
                        i = e.matmul(A["A0"][:, j * 2 * NS:(j + 1) * 2 * NS], xc[par][:, k, j * P:(j + 1) * P], w_bc[:, k, :],
                                     start=(k == 0), stop=(k == ND - 1))
                i.then_inc(full["A0"], 1)
            add(36, PE_, bc_pe)

            def bc_act(e):
                fullw(e, "A0", c, 1 + ND)
                wait(e, s_ub, SLOTS, c.shift(-2), SLOTS - 1)
                wait(e, s_y, SLOTS, c.shift(-2), SLOTS - 1)
                e.copy(bc[par][:].rearrange("p j s -> p (j s)"), A["A0"][:, 0:J * 2 * NS]).then_inc(free["A0"], 1)
            add(37, AC_, bc_act)

            def dt_pe(m):
                def f(e):
                    wait(e, s_xc, ND, c, ND - 1)
                    freew(e, "A1", c, ND + m)
                    for k in range(ND):
                        i = e.matmul(A["A1"][:], w_dt[:, k, m * P:(m + 1) * P], xc[par][:, k, :], start=(k == 0), stop=(k == ND - 1))
                    i.then_inc(full["A1"], 1)
                return f

            def dt_act(m):
                def f(e):
                    fullw(e, "A1", c, 1 + ND + m)
                    wait(e, s_dt, ND, c, m - 2)
                    e.activation(rl[:, m % 2, :], A["A1"][:], ACT.Relu, bias=b_dt[:, m:m + 1])
                    e.activation(dt[par][:, m, :], A["A1"][:], ACT.Abs, bias=b_dt[:, m:m + 1]).then_inc(free["A1"], 1)
                    freew(e, "A1", c, 1 + ND + m)
                    then(e, e.activation(dt[par][:, m, :], dt[par][:, m, :], ACT.Exp, scale=-1.0))
                    e.activation(dt[par][:, m, :], dt[par][:, m, :], ACT.Ln, bias=1.0).then_inc(s_ln, 1)
                return f

            def dt_pool(m):
                def f(e):
                    wait(e, s_ln, ND, c, m)
                    e.tensor_tensor(dt[par][:, m, :], dt[par][:, m, :], rl[:, m % 2, :], ALU.add).then_inc(s_dt, 1)
                    wait(e, s_dt, ND, c, m)
                    fullw(e, "A0", c, 2 + ND + m - 2)
                    wait(e, s_xc, ND, c, m)
                    e.tensor_tensor(uu[:, m % 2, :], dt[par][:, m, :], xc[par][:, m, :], ALU.mult).then_inc(s_u, 1)
                return f

            def ut_pe(m):
                def f(e):
                    wait(e, s_u, ND, c, m)
                    freew(e, "A0", c, 1 + ND + m)
                    for j in range(J):
                        i = e.transpose(A["A0"][:, j * P:(j + 1) * P], uu[:, m % 2, j * P:(j + 1) * P], ident[:])
                    i.then_inc(full["A0"], 1)
                return f

            def ut_act(m):
                def f(e):
                    fullw(e, "A0", c, 2 + ND + m)
                    e.copy(uT[par][:, :, m * P:(m + 1) * P], A["A0"][:].rearrange("p (j q) -> p j q", j=J)).then_inc(free["A0"], 1)
                return f
            for m in range(ND):
                t = 37 + 5 * m
                add(t, PE_, dt_pe(m))
                add(t + 1, AC_, dt_act(m))
                add(t + 3, PO_, dt_pool(m))
                add(t + 6, PE_, ut_pe(m))
                add(t + 7, AC_, ut_act(m))
            return s

        def post(c, par):
            s = defaultdict(list)

            def add(slot, eng, fn):
                s[(slot, eng)].append(fn)
            B2 = ("A2", "A3")

            def load_r(e):
                e.dma_start(xr[:], x_rows[bass.ds(c.times(CH), CH), :].rearrange("(j p) d -> p j d", p=P)).then_inc(s_xr, 16)
            add(1, SP_, load_r)

            def yb_pe(d):
                def f(e):
                    b = B2[d % 2]
                    wait(e, s_y, SLOTS, c, SLOTS - 1)
                    if d >= 2:
                        freew(e, b, c, d // 2 - 1)
                    for j in range(J):
                        i = e.transpose(A[b][:, j * P:(j + 1) * P], yT[par][:, j, d * P:(d + 1) * P], ident[:])
                    i.then_inc(full[b], 1)
                return f

            def yb_dve(d):
                def f(e):
                    b = B2[d % 2]
                    fullw(e, b, c, d // 2)
                    e.scalar_tensor_tensor(out=xc[par][:, d, :], in0=xc[par][:, d, :], scalar=dskip[:, d:d + 1], in1=A[b][:],
                                           op0=ALU.mult, op1=ALU.add).then_inc(free[b], 1)
                return f
            for d in range(ND):
                add(5 + d, PE_, yb_pe(d))
                add(6 + d, DV_, yb_dve(d))

            def out_pe(q):
                def f(e):
                    b = B2[q]
                    freew(e, "A2", c, 1)
                    freew(e, "A3", c, 1)
                    for j in (2 * q, 2 * q + 1):
                        for k in range(ND):
                            i = e.matmul(A[b][:, (j % 2) * DM:(j % 2 + 1) * DM], xc[par][:, k, j * P:(j + 1) * P], w_out[:, k, :],
                                         start=(k == 0), stop=(k == ND - 1))
                    i.then_inc(full[b], 1)
                return f
            add(11, PE_, out_pe(0))
            add(12, PE_, out_pe(1))

            def o_stats(e):
                for j in range(J):
                    fullw(e, B2[j // 2], c, 2)
                    then(e, e.bn_stats(st2[:, j, :], A[B2[j // 2]][:, (j % 2) * DM:(j % 2 + 1) * DM]))
                for j in range(J):
                    then(e, e.bn_aggr(mv2[:, j, :], st2[:, j, :]))
                e.tensor_scalar(va2[:], mv2[:, :, 1], EPS_LN, None, ALU.add).then_inc(s_o1, 1)
            add(14, DV_, o_stats)

            def o_root(e):
                wait(e, s_o1, 1, c, 0)
                then(e, e.activation(r2[:], va2[:], ACT.Ln))
                e.activation(r2[:], r2[:], ACT.Exp, scale=-0.5).then_inc(s_o2, 1)
            add(15, AC_, o_root)

            def o_newton(e):
                wait(e, s_o2, 1, c, 0)
                wait(e, s_o1, 1, c, 0)
                rsqrt_tail(e, r2, va2, tn2)
                e.scalar_tensor_tensor(out=nmr2[:], in0=mv2[:, :, 0], scalar=-1.0, in1=r2[:], op0=ALU.mult, op1=ALU.mult).then_inc(s_o3, 1)
            add(16, DV_, o_newton)

            def o_norm(e):
                wait(e, s_o3, 1, c, 0)
                for j in range(J):
                    b = B2[j // 2]
                    i = e.activation(on[:, j, :], A[b][:, (j % 2) * DM:(j % 2 + 1) * DM], ACT.Identity,
                                     scale=r2[:, j:j + 1], bias=nmr2[:, j:j + 1])
                    if j % 2:
                        i.then_inc(free[b], 1)
            add(17, AC_, o_norm)

            def x1_pool(e):
                freew(e, "A2", c, 2)
                freew(e, "A3", c, 2)
                wait(e, s_xr, 16, c, 15)
                e.tensor_tensor(xr[:].rearrange("p j d -> p (j d)"), xr[:].rearrange("p j d -> p (j d)"),
                                on[:].rearrange("p j d -> p (j d)"), ALU.add).then_inc(s_x1, 1)
            add(19, PO_, x1_pool)

            def x1_store(e):
                wait(e, s_x1, 1, c, 0)
                e.dma_start(x1_d[bass.ds(c.times(CH), CH), :].rearrange("(j p) d -> p j d", p=P), xr[:]).then_inc(s_x1s, 16)
            add(20, SP_, x1_store)

            def l_stats(e):
                wait(e, s_x1, 1, c, 0)
                for j in range(J):
                    then(e, e.bn_stats(st2[:, j, :], xr[:, j, :]))
                freew(e, "A3", c, 2)
                e.nop(nofuse=True)
                for j in range(J):
                    then(e, e.bn_aggr(mv2[:, j, :], st2[:, j, :]))
                e.tensor_scalar(va2[:], mv2[:, :, 1], EPS_LN, None, ALU.add).then_inc(s_l1, 1)
            add(21, DV_, l_stats)

            def l_root(e):
                wait(e, s_l1, 1, c, 0)
                then(e, e.activation(r2[:], va2[:], ACT.Ln))
                e.activation(r2[:], r2[:], ACT.Exp, scale=-0.5).then_inc(s_l2, 1)
            add(22, AC_, l_root)

            def l_newton(e):
                wait(e, s_l2, 1, c, 0)
                wait(e, s_l1, 1, c, 0)
                rsqrt_tail(e, r2, va2, tn2)
                e.scalar_tensor_tensor(out=nmr2[:], in0=mv2[:, :, 0], scalar=-1.0, in1=r2[:], op0=ALU.mult, op1=ALU.mult).then_inc(s_l3, 1)
            add(23, DV_, l_newton)

            def l_norm(e):
                wait(e, s_l3, 1, c, 0)
                for j in range(J):
                    e.tensor_scalar(xf[:, j, :], xr[:, j, :], r2[:, j:j + 1], nmr2[:, j:j + 1], ALU.mult, ALU.add).then_inc(s_xf, 1)
            add(24, PO_, l_norm)

            def turn_f(k):
                def f(e):
                    b = B2[k]
                    wait(e, s_xf, J, c, J - 1)
                    freew(e, b, c, 2)
                    for j in range(J):
                        i = e.transpose(A[b][:, j * P:(j + 1) * P], xf[:, j, k * P:(k + 1) * P], ident[:])
                    i.then_inc(full[b], 1)
                return f

            def keep_f(k):
                def f(e):
                    fullw(e, B2[k], c, 3)
                    e.copy(xfT[:, k, :], A[B2[k]][:]).then_inc(free[B2[k]], 1)
                return f
            for k in range(KD):
                add(27 + k, PE_, turn_f(k))
                add(28 + k, AC_, keep_f(k))

            def lg_pe(e):
                freew(e, "A2", c, 3)
                freew(e, "A3", c, 3)
                for j in range(J):
                    for k in range(KD):
                        i = e.matmul(A["A2"][:, j * E:(j + 1) * E], xfT[:, k, j * P:(j + 1) * P], w_gt[:, k, :], start=(k == 0), stop=(k == KD - 1))
                i.then_inc(full["A2"], 1)
            add(30, PE_, lg_pe)

            def route(e):
                fullw(e, "A2", c, 4)
                e.tensor_copy(lg[:].rearrange("p j e -> p (j e)"), A["A2"][:, 0:J * E]).then_inc(free["A2"], 1)
                e.drain()
                for j in range(J):
                    then(e, e.max(mx[:, j, :], lg[:, j, :]))
                for j in range(J):
                    then(e, e.max_index(ix[:, j, :], mx[:, j, :], lg[:, j, :]))
                then(e, e.tensor_copy(ixf[:], ix[:, :, 0:TOPK]))
                for k in range(TOPK):
                    for j in range(J):
                        then(e, e.tensor_scalar(oh[:, k, j, :], iota_e[:], ixf[:, j, k:k + 1], None, ALU.is_equal))
                then(e, e.tensor_tensor(dif[:], mx[:, :, 1], mx[:, :, 0], ALU.subtract))
                e.tensor_tensor(mm_[:], oh[:, 0, :, :], oh[:, 1, :, :], ALU.add).then_inc(s_m, 1)
            add(32, DV_, route)

            def rank_pe(e):
                wait(e, s_m, 1, c, 0)
                freew(e, "A3", c, 3)
                for j in range(J):
                    e.matmul(A["A3"][:, j * E:(j + 1) * E], below[:], mm_[:, j, :], start=True, stop=(j == 0))
                    for q in range(j):
                        e.matmul(A["A3"][:, j * E:(j + 1) * E], ones[:], mm_[:, q, :], start=False, stop=(q == j - 1))
                for j in range(J):
                    i = e.matmul(A["A3"][:, J * E:(J + 1) * E], ones[:], mm_[:, j, :], start=(j == 0), stop=(j == J - 1))
                i.then_inc(full["A3"], 1)
            add(34, PE_, rank_pe)

            def e2_act(e):
                wait(e, s_m, 1, c, 0)
                e.activation(e2[:], dif[:], ACT.Exp).then_inc(s_e2, 1)
            add(34, AC_, e2_act)

            def place(e):
                fullw(e, "A3", c, 4)
                for j in range(J):
                    then(e, e.tensor_tensor(pos8[:, j, :], A["A3"][:, j * E:(j + 1) * E], base[:], ALU.add))
                e.tensor_tensor(base[:], base[:], A["A3"][:, J * E:(J + 1) * E], ALU.add).then_inc(free["A3"], 1)
                for k in range(TOPK):
                    then(e, e.tensor_tensor(prd[:, k, :, :], oh[:, k, :, :], pos8[:], ALU.mult))
                for k in range(TOPK):
                    then(e, e.tensor_reduce(posf[:, :, k], prd[:, k, :, :], AX.X, ALU.add))
                wait(e, s_e2, 1, c, 0)
                then(e, e.tensor_scalar(e2p[:], e2[:], 1.0, None, ALU.add))
                then(e, e.reciprocal(p1[:], e2p[:]))
                then(e, e.tensor_copy(gat[:, bass.ds(c.times(J), J), 0], p1[:]))
                e.tensor_tensor(gat[:, bass.ds(c.times(J), J), 1], e2[:], p1[:], ALU.mult)
                e.tensor_copy(posa[:, bass.ds(c.times(J), J), :], posf[:])
                e.tensor_copy(expa[:, bass.ds(c.times(J), J), :], ixf[:])
                e.tensor_copy(posl[:], posf[:]).then_inc(s_pos, 1)
            add(36, DV_, place)

            def scatter(e):
                wait(e, s_pos, 1, c, 0)
                for j in range(J):
                    for k in range(TOPK):
                        e.indirect_dma_start(out=xs_d, out_offset=bass.IndirectOffsetOnAxis(ap=posl[:, j, k:k + 1], axis=0),
                                             in_=xf[:, j, :], in_offset=None).then_inc(s_sc, 16)
            add(38, PO_, scatter)

            def sh_pe(t):
                def f(e):
                    i0, n = SIT[t]
                    for b, w in (("A2", w_sg), ("A3", w_su)):
                        freew(e, b, c, 4 + t)
                        for k in range(KD):
                            i = e.matmul(A[b][0:n, :], w[:, k, i0:i0 + n], xfT[:, k, :], start=(k == 0), stop=(k == KD - 1))
                        i.then_inc(full[b], 1)
                return f

            def sh_act(t):
                def f(e):
                    n = SIT[t][1]
                    fullw(e, "A2", c, 5 + t)
                    freew(e, "A3", c, 5 + t - 2)
                    e.activation(sgs[0:n, t % 2, :], A["A2"][0:n, :], ACT.Silu).then_inc(free["A2"], 1)
                return f

            def sh_dve(t):
                def f(e):
                    n = SIT[t][1]
                    freew(e, "A2", c, 5 + t)
                    fullw(e, "A3", c, 5 + t)
                    e.tensor_tensor(hs[0:n, t, :], sgs[0:n, t % 2, :], A["A3"][0:n, :], ALU.mult).then_inc(free["A3"], 1)
                return f
            for t in range(len(SIT)):
                add(39 + 3 * t, PE_, sh_pe(t))
                add(40 + 3 * t, AC_, sh_act(t))
                add(41 + 3 * t, DV_, sh_dve(t))

            def sd_pe(q):
                def f(e):
                    b = B2[q]
                    freew(e, "A3", c, 7)
                    freew(e, "A2", c, 7)
                    for j in (2 * q, 2 * q + 1):
                        for t, (i0, n) in enumerate(SIT):
                            i = e.matmul(A[b][:, (j % 2) * DM:(j % 2 + 1) * DM], hs[0:n, t, j * P:(j + 1) * P], w_sd[0:n, t, :],
                                         start=(t == 0), stop=(t == len(SIT) - 1))
                    i.then_inc(full[b], 1)
                return f

            def sd_act(q):
                def f(e):
                    b = B2[q]
                    fullw(e, b, c, 8)
                    e.copy(sh[:, 2 * q:2 * q + 2, :].rearrange("p j d -> p (j d)"), A[b][:]).then_inc(free[b], 1)
                return f
            for q in range(2):
                add(49 + q, PE_, sd_pe(q))
                add(51 + q, AC_, sd_act(q))

            def sh_store(e):
                freew(e, "A2", c, 8)
                freew(e, "A3", c, 8)
                e.dma_start(sh_d[bass.ds(c.times(CH), CH), :].rearrange("(j p) d -> p j d", p=P), sh[:]).then_inc(s_shs, 16)
            add(54, SP_, sh_store)

            def done_sp(e):
                wait(e, s_xf, J, c, J - 1)
                wait(e, s_x1s, 16, c, 15)
            add(60, SP_, done_sp)

            def done_act(e):
                wait(e, s_x1, 1, c, 0)
                wait(e, s_shs, 16, c, 15)
            add(60, AC_, done_act)

            def done_rows(e):
                wait(e, s_sc, 16 * J * TOPK, c, 16 * J * TOPK - 1)
                fullw(e, "A3", c, 3)
            add(60, PO_, done_rows)
            add(60, DV_, done_rows)

            def done_pe(e):
                freew(e, "A2", c, 8)
                freew(e, "A3", c, 8)
            add(60, PE_, done_pe)
            return s

        def main_act(e, c, par, k):
            n, d = divmod(k, ND)
            if n == 0:
                wait(e, s_dt, ND, c, d)
            wait(e, s_scan, SLOTS, c, k - NA)
            e.activation(ab[:, k % NA, :], dt[par][:, d, :], ACT.Exp, scale=a_neg[:, d, n:n + 1]).then_inc(s_a, 1)

        def main_pool(e, c, par, k):
            n, j = divmod(k, ND)
            if k == 0:
                freew(e, "A0", c, 1 + 2 * ND)
            if j == 0:
                wait(e, s_b, SLOTS, c, k - ND - 1)
            e.tensor_scalar(ub[:, n % 2, j, :], uT[par][:, j, :], bc[par][:, j, n:n + 1], 1.0, ALU.mult, ALU.mult).then_inc(s_ub, 1)

        def keep_last(e, c, n):
            wait(e, s_scan, SLOTS, c, n * ND + ND - 1)
            e.tensor_copy(hl[:, n, :], hh[:, n % 2, :, CH - 1]).then_inc(s_hl, 1)

        def main_pe(e, c, par, k, first, scan=True):
            n, d = divmod(k, ND)
            if scan:
                if d == 0:
                    wait(e, s_ub, SLOTS, c, n * ND + ND - 1)
                wait(e, s_scan, SLOTS, c, k - 2)
                for j in range(J):
                    i = e.transpose(bB[k % 2][:, j * P:(j + 1) * P], ub[:, n % 2, j, d * P:(d + 1) * P], ident[:])
                i.then_inc(s_b, 1)
            if not first:
                if d == 0:
                    wait(e, s_scan, SLOTS, c, k - 1)
                wait(e, s_y, SLOTS, c, k - ND - 2)
                for q in range(ND):
                    i = e.transpose(bH[d % 2][:, q * P:(q + 1) * P], hh[:, (n - 1) % 2, q, d * P:(d + 1) * P], ident[:])
                i.then_inc(s_ht, 1)

        def main_dve(e, c, par, k, first, scan=True):
            n, d = divmod(k, ND)
            if scan:
                wait(e, s_a, SLOTS, c, k)
                wait(e, s_b, SLOTS, c, k)
                if d == 0:
                    wait(e, s_ht, SLOTS, c, k - ND - 1)
                if par:
                    if k == 0:
                        e.wait_ge(s_hl, c.times(NS // 2, NS // 2))
                else:
                    if d == 0 and n >= 2:
                        e.wait_ge(s_hl, c.times(NS // 2, n - 1))
                e.tensor_tensor_scan(hh[:, n % 2, d, :], ab[:, k % NA, :], bB[k % 2][:], hl[:, n, d:d + 1] if par else 0.0,
                                     ALU.mult, ALU.add).then_inc(s_scan, 1)
            if not first:
                wait(e, s_ht, SLOTS, c, k - ND)
                if n == 0:
                    cm, yy = bc[1 - par][:, d, 2 * NS - 1:2 * NS], yT[1 - par]
                else:
                    cm, yy = bc[par][:, d, NS + n - 1:NS + n], yT[par]
                if n == 1:
                    if d == 0:
                        freew(e, "A0", c, 1 + ND)
                    e.tensor_scalar(yy[:, d, :], bH[d % 2][:], cm, None, ALU.mult).then_inc(s_y, 1)
                else:
                    wait(e, s_y, SLOTS, c, k - 2 * ND)
                    e.scalar_tensor_tensor(out=yy[:, d, :], in0=bH[d % 2][:], scalar=cm, in1=yy[:, d, :],
                                           op0=ALU.mult, op1=ALU.add).then_inc(s_y, 1)

        def chunk(e, name, c, par, first=False, last=False):
            side = []
            if not last:
                side.append(pre(c.shift(1), 1 - par))
            if not first:
                side.append(post(c.shift(-1), 1 - par))
            for k in range(SLOTS):
                f = first and k < ND
                if name == AC_:
                    main_act(e, c, par, k)
                elif name == PO_:
                    if k + ND < SLOTS:
                        main_pool(e, c, par, k + ND)
                    elif not last:
                        main_pool(e, c.shift(1), 1 - par, k + ND - SLOTS)
                elif name == PE_:
                    main_pe(e, c, par, k, f)
                elif name == DV_:
                    main_dve(e, c, par, k, f)
                if name == PO_ and par == 0 and k % ND == ND - 1 and k > ND:
                    keep_last(e, c, k // ND - 1)
                for s in side:
                    for fn in s[(k, name)]:
                        fn(e)
            if name == PO_ and par == 0:
                keep_last(e, c, NS - 1)
            if last:
                for d in range(ND):
                    if name == PE_:
                        main_pe(e, c.shift(1), 1 - par, d, False, scan=False)
                    if name == DV_:
                        main_dve(e, c.shift(1), 1 - par, d, False, scan=False)

        def run(e, name):
            s = pre(Chunk(0), 0)
            for k in range(SLOTS):
                for fn in s[(k, name)]:
                    fn(e)
            if name == PO_:
                for k in range(ND):
                    main_pool(e, Chunk(0), 0, k)
            chunk(e, name, Chunk(0), 0, first=True)
            with e.Fori(0, (NCH - 2) // 2) as i:
                chunk(e, name, Chunk(1, i), 1)
                chunk(e, name, Chunk(2, i), 0)
            chunk(e, name, Chunk(NCH - 1), 1, last=True)
            s = post(Chunk(NCH - 1), 1)
            for k in range(SLOTS):
                for fn in s[(k, name)]:
                    fn(e)

        def table(e):
            def link(i):
                then(e, i)
            freew(e, "A3", Chunk(NCH - 1), 4)
            link(e.tensor_copy(iopf[:], iop[:]))
            link(e.tensor_scalar(padf[:], base[:], iopf[:, 0:1], None, ALU.add))
            e.tensor_copy(padi[:], padf[:]).then_inc(s_pad, 1)
            link(e.tensor_scalar(capf[:], iota_e[:], float(CAP), None, ALU.mult))
            link(e.tensor_tensor(cnt[:], base[:], capf[:], ALU.subtract))
            link(e.tensor_scalar(cnti[:], cnt[:], float(P - 1), None, ALU.add))
            link(e.tensor_single_scalar(nti[:], cnti[:], P.bit_length() - 1, ALU.arith_shift_right))
            link(e.tensor_copy(ntf[:], nti[:]))
            link(e.tensor_tensor_scan(cum[:], one8[:], ntf[:], 0.0, ALU.mult, ALU.add))
            link(e.tensor_scalar(tot[:], cum[0:1, E - 1:E], -1.0, None, ALU.add))
            link(e.tensor_copy(tif[:], tii[:]))
            link(e.tensor_scalar(tif[:], tif[:], tot[:, 0:1], None, ALU.min))
            link(e.tensor_scalar(te[:], tif[:], 0.0, None, ALU.mult))
            link(e.tensor_copy(tp[:], tif[:]))
            for x_ in range(E - 1):
                link(e.tensor_scalar(ge[:], tif[:], cum[0:1, x_:x_ + 1], None, ALU.is_ge))
                link(e.tensor_tensor(te[:], te[:], ge[:], ALU.add))
                link(e.tensor_scalar(ge[:], ge[:], ntf[0:1, x_:x_ + 1], None, ALU.mult))
                link(e.tensor_tensor(tp[:], tp[:], ge[:], ALU.subtract))
            link(e.tensor_copy(tab[:, 0, :], te[:]))
            link(e.tensor_scalar(tp[:], tp[:], float(P), None, ALU.mult))
            link(e.tensor_scalar(te[:], te[:], float(CAP), None, ALU.mult))
            link(e.tensor_tensor(tp[:], te[:], tp[:], ALU.add))
            link(e.tensor_copy(tab[:, 1, :], tp[:]))
            link(e.tensor_tensor(off[:], cum[:], ntf[:], ALU.subtract))
            link(e.tensor_scalar(off[:], off[:], float(P), None, ALU.mult))
            link(e.tensor_tensor(off[:], off[:], capf[:], ALU.subtract))
            pa, ea = (t[:].rearrange("p t k -> p (t k)") for t in (posa, expa))
            for x_ in range(E):
                link(e.tensor_scalar(adj[:], ea, float(x_), off[:, x_:x_ + 1], ALU.is_equal, ALU.mult))
                link(e.tensor_tensor(pa, pa, adj[:], ALU.add))
            link(e.tensor_copy(posi[:].rearrange("p t k -> p (t k)"), pa))

        block = ctx.enter_context(nc.Block())

        NW = 16 + 2
        @block.sync
        def _(e):
            def ld(dst, src, **kw):
                e.dma_start(dst, src, **kw).then_inc(s_w, 16)
            ld(w_in[:], in_proj_w.rearrange("(k p) n -> p k n", p=P))
            ld(w_nm[:], norm_w.rearrange("(k p) -> p k", p=P), allow_slow_non_contiguous=True)
            ld(w_cv[:], conv_w.rearrange("(k p) a t -> p k (a t)", p=P))
            ld(w_dt[:], dt_w.rearrange("(k p) n -> p k n", p=P))
            ld(w_bc[:, :, 0:NS], B_w.rearrange("(k p) n -> p k n", p=P))
            ld(w_bc[:, :, NS:2 * NS], C_w.rearrange("(k p) n -> p k n", p=P))
            ld(b_dt[:], dt_b.rearrange("(k p) -> p k", p=P), allow_slow_non_contiguous=True)
            ld(a_log[:], A_log.rearrange("(k p) n -> p k n", p=P))
            ld(dskip[:], D_skip.rearrange("(k p) -> p k", p=P), allow_slow_non_contiguous=True)
            ld(w_out[:], out_proj_w.rearrange("(k p) n -> p k n", p=P))
            ld(w_gt[:], gate_w.rearrange("(k p) n -> p k n", p=P))
            ld(w_sg[:], Sg.rearrange("(k p) n -> p k n", p=P))
            ld(w_su[:], Su.rearrange("(k p) n -> p k n", p=P))
            for t, (i0, n) in enumerate(SIT):
                ld(w_sd[0:n, t, :], Sd[i0:i0 + n, :])
            run(e, SP_)
            e.wait_ge(s_x1s, 16 * NCH)
            e.wait_ge(s_shs, 16 * NCH)

        NWD = 13 + len(SIT)

        @block.gpsimd
        def _(e):
            def sel(t, op, fill, base_, pattern, cm):
                return e.affine_select(out=t, in_=t, compare_op=op, fill=fill, base=base_, pattern=pattern, channel_multiplier=cm)
            e.memset(ident[:], 0.0).then_inc(s_c, 1)
            e.memset(below[:], 1.0).then_inc(s_c, 1)
            e.memset(ones[:], 1.0).then_inc(s_c, 1)
            e.memset(zro[:], 0.0).then_inc(s_c, 1)
            e.memset(one8[:], 1.0).then_inc(s_c, 1)
            e.iota(iota_i[:], [[1, E]], base=0, channel_multiplier=0).then_inc(s_c, 1)
            e.iota(capi[:], [[CAP, E]], base=0, channel_multiplier=0).then_inc(s_c, 1)
            e.iota(iop[:], [[0, 1]], base=0, channel_multiplier=1).then_inc(s_c, 1)
            e.iota(tii[:], [[1, NT + 1]], base=0, channel_multiplier=0).then_inc(s_c, 1)
            e.wait_ge(s_c, 9)
            sel(ident[:], ALU.not_equal, 1.0, 0, [[-1, P]], 1).then_inc(s_id, 1)
            sel(below[:], ALU.is_gt, 0.0, 0, [[1, P]], -1).then_inc(s_id, 1)
            e.wait_ge(s_id, 2)
            e.wait_ge(s_cst, 3)
            run(e, PO_)
            e.wait_ge(s_pad, 1)
            for x_ in range(E):
                e.indirect_dma_start(out=xs_d, out_offset=bass.IndirectOffsetOnAxis(ap=padi[:, x_:x_ + 1], axis=0),
                                     in_=zro[:], in_offset=None).then_inc(s_padd, 16)
            e.wait_ge(s_padd, 16 * E)
            e.wait_ge(s_sc, 16 * J * TOPK * NCH)

        @block.scalar
        def _(e):
            e.wait_ge(s_w, 16 * NWD)
            e.activation(a_exp[:], a_log[:], ACT.Exp).then_inc(s_an, 1)
            e.wait_ge(s_an, 1)
            e.mul(a_neg[:], a_exp[:], -1.0).then_inc(s_an, 1)
            e.wait_ge(s_an, 2)
            run(e, AC_)

        @block.tensor
        def _(e):
            e.wait_ge(s_id, 2)
            e.wait_ge(s_cst, 3)
            run(e, PE_)

        @block.vector
        def _(e):
            e.wait_ge(s_c, 9)
            e.wait_ge(s_w, 16 * NWD)
            for k in range(KD):
                i = e.tensor_scalar(w_in[:, k, :], w_in[:, k, :], w_nm[:, k:k + 1], None, ALU.mult)
            i.then_inc(s_cst, 1)
            e.tensor_copy(iota_e[:], iota_i[:]).then_inc(s_cst, 1)
            e.tensor_copy(base[:], capi[:]).then_inc(s_cst, 1)
            e.wait_ge(s_cst, 3)
            run(e, DV_)
            table(e)



def phase2(nc, sem, Wg, Wu, Wd, x1_d, sh_d, xs_d, ys_d, out_rows, ident, posi, gat, tab):
    with ExitStack() as ctx:
        def sb(name, shape, dt=F32):
            return ctx.enter_context(nc.sbuf_tensor(name, shape, dt))

        def bank(name):
            return ctx.enter_context(nc.psum_tensor(name, [P, 512], F32))

        NF = len(FIT)
        w_g = sb("w_g", [P, E * KD * FI])
        w_u = sb("w_u", [P, E * KD * FI])
        w_d = sb("w_d", [P, E * NF * DM])
        xt = sb("xt", [P, 2, DM])
        xtT = sb("xtT", [P, 2, KD, P])
        sgm = sb("sgm", [P, 2, FI])
        hm = sb("hm", [P, 2, FI])
        hT = sb("hT", [P, 2, NF, P])
        yt = sb("yt", [P, 2, DM])

        bX = bank("bX"); bG = [bank("bG0"), bank("bG1")]; bU = [bank("bU0"), bank("bU1")]
        bHA = bank("bHA"); bHB = bank("bHB"); bD = bank("bD")

        s_wt = sem("s_wt")
        s_in = [sem("s_in0"), sem("s_in1")]
        s_tx = sem("s_tx"); s_kx = sem("s_kx"); s_g = sem("s_g"); s_gu = sem("s_gu"); s_si = sem("s_si"); s_h = sem("s_h")
        s_th = sem("s_th"); s_ka = sem("s_ka"); s_kb = sem("s_kb"); s_dn = sem("s_dn"); s_yt = sem("s_yt"); s_ys = sem("s_ys")
        NB4 = 4

        def after(e, s_, t, back=0, per=1):
            wait(e, s_, per, t.shift(-back), per - 1)

        def arrived(e, t, par):
            v = t.times(8, 16 - 8 * par)
            e.wait_ge(s_in[par], v)

        def tile_in(e, t, par):
            after(e, s_tx, t, 2)
            row = e.value_load(tab[0:1, 1, bass.ds(t.times(1), 1)], min_val=0, max_val=E * CAP - P)
            e.dma_start(xt[:, par, :], xs_d[bass.ds(row, P), :]).then_inc(s_in[par], 16)

        def tile_out(e, t, par):
            after(e, s_yt, t)
            after(e, s_ys, t, 1, 16)
            e.dma_start(ys_d[bass.ds(t.times(P), P), :], yt[:, par, :]).then_inc(s_ys, 16)

        def turn_in(e, t, par):
            arrived(e, t, par)
            after(e, s_kx, t, 1)
            for k in range(KD):
                i = e.transpose(bX[:, k * P:(k + 1) * P], xt[:, par, k * P:(k + 1) * P], ident[:])
            i.then_inc(s_tx, 1)

        def up(e, t, par):
            ex = e.value_load(tab[0:1, 0, bass.ds(t.times(1), 1)], min_val=0, max_val=E - 1)
            e.wait_ge(s_wt, ex * 64 + 64)
            e.nop(nofuse=True)
            after(e, s_kx, t)
            after(e, s_si, t, 1)
            for w, banks, s_ in ((w_g, bG, s_g), (w_u, bU, s_gu)):
                if w is w_u:
                    after(e, s_h, t, 1)
                for f in range(2):
                    for k in range(KD):
                        i = e.matmul(banks[f][:, 0:FH], xtT[:, par, k, :], w[:, bass.ds(ex * (KD * FI) + (k * FI + f * FH), FH)],
                                     start=(k == 0), stop=(k == KD - 1))
                i.then_inc(s_, 1)

        def turn_h(e, t, par):
            after(e, s_h, t)
            after(e, s_ka, t, 1)
            after(e, s_kb, t, 1)
            for q, (i0, n) in enumerate(FIT):
                b, o = (bHA, q) if q < NB4 else (bHB, q - NB4)
                i = e.transpose(b[0:n, o * P:(o + 1) * P], hm[:, par, i0:i0 + n], ident[:])
            i.then_inc(s_th, 1)

        def down(e, t, par):
            ex = e.value_load(tab[0:1, 0, bass.ds(t.times(1), 1)], min_val=0, max_val=E - 1)
            after(e, s_ka, t)
            after(e, s_kb, t)
            after(e, s_yt, t, 1)
            for q, (i0, n) in enumerate(FIT):
                i = e.matmul(bD[:, 0:DM], hT[0:n, par, q, :], w_d[0:n, bass.ds(ex * (NF * DM) + q * DM, DM)],
                             start=(q == 0), stop=(q == NF - 1))
            i.then_inc(s_dn, 1)

        def act_keep_x(e, t, par):
            after(e, s_tx, t)
            after(e, s_gu, t, 2)
            e.copy(xtT[:, par, :, :].rearrange("p k q -> p (k q)"), bX[:, 0:KD * P]).then_inc(s_kx, 1)

        def act_silu(e, t, par):
            after(e, s_g, t)
            after(e, s_h, t, 2)
            for f in range(2):
                i = e.activation(sgm[:, par, f * FH:(f + 1) * FH], bG[f][:, 0:FH], ACT.Silu)
            i.then_inc(s_si, 1)

        def act_keep_h(e, t, par):
            after(e, s_th, t)
            after(e, s_dn, t, 2)
            e.copy(hT[:, par, 0:NB4, :].rearrange("p k q -> p (k q)"), bHA[:]).then_inc(s_ka, 1)

        def dve_mul(e, t, par):
            after(e, s_si, t)
            after(e, s_gu, t)
            after(e, s_th, t, 2)
            for f in range(2):
                i = e.tensor_tensor(hm[:, par, f * FH:(f + 1) * FH], sgm[:, par, f * FH:(f + 1) * FH], bU[f][:, 0:FH], ALU.mult)
            i.then_inc(s_h, 1)

        def dve_keep_h(e, t, par):
            after(e, s_th, t)
            after(e, s_dn, t, 2)
            for q in range(NB4, NF):
                n = FIT[q][1]
                i = e.tensor_copy(hT[0:n, par, q, :], bHB[0:n, (q - NB4) * P:(q - NB4 + 1) * P])
            i.then_inc(s_kb, 1)

        def dve_keep_y(e, t, par):
            after(e, s_dn, t)
            after(e, s_ys, t, 2, 16)
            e.tensor_copy(yt[:, par, :], bD[:, 0:DM]).then_inc(s_yt, 1)

        def tiles(e, first, second, ahead):
            def step(t, p, more=True):
                first(e, t, p)
                if more:
                    ahead(e, t.shift(1), 1 - p)
                second(e, t.shift(-1), 1 - p)

            ahead(e, Chunk(0), 0)
            first(e, Chunk(0), 0)
            ahead(e, Chunk(1), 1)
            step(Chunk(1), 1)
            step(Chunk(2), 0)
            with e.Fori(0, (NT - 5) // 2) as i:
                step(Chunk(3, i), 1)
                step(Chunk(4, i), 0)
            step(Chunk(NT - 2), 1)
            step(Chunk(NT - 1), 0, more=False)
            second(e, Chunk(NT - 1), 0)

        def pe_second(e, t, p):
            turn_h(e, t, p)
            down(e, t, p)

        def dve_second(e, t, p):
            dve_keep_h(e, t, p)
            dve_keep_y(e, t, p)

        def none(e, t, p):
            pass

        UT = 2
        NU = NTOK // P // UT
        gidx = sb("gidx", [P, 2, UT, TOPK], U32)
        gwt = sb("gwt", [P, 2, UT, TOPK])
        yg = sb("yg", [P, 2, TOPK, UT, DM])
        x1u = sb("x1u", [P, 2, UT, DM])
        shu = sb("shu", [P, 2, UT, DM])
        ou = sb("ou", [P, 2, UT, DM])
        st = sb("st3", [P, UT, 6])
        mv = sb("mv3", [P, UT, 2])
        va = sb("va3", [P, UT])
        rr = sb("rr3", [P, 2, UT])
        tn = sb("tn3", [P, UT])
        nm = sb("nm3", [P, 2, UT])
        s_gi = sem("s_gi")
        s_yg = [sem("s_yg0"), sem("s_yg1")]
        s_xu = [sem("s_xu0"), sem("s_xu1")]
        s_f1 = sem("s_f1"); s_f2 = sem("s_f2"); s_f3 = sem("s_f3"); s_f4 = sem("s_f4"); s_f5 = sem("s_f5")
        s_out = [sem("s_out0"), sem("s_out1")]

        def by_parity(e, s_, per, u, par, back=0):
            h = per // 2
            v = u.times(h, per - h * par - per * back)
            if isinstance(v, int) and v <= 0:
                return
            e.wait_ge(s_, v)
            if not isinstance(v, int) and e.engine in (POOL, SYNC):
                e.nop(nofuse=True)

        def units(e, fn):
            for u in range(2):
                fn(e, Chunk(u), u)
            with e.Fori(0, (NU - 2) // 2) as i:
                fn(e, Chunk(2, i), 0)
                fn(e, Chunk(3, i), 1)

        def u_gather(e, u, par):
            wait(e, s_f1, 1, u.shift(-2), 0)
            e.tensor_copy(gidx[:, par, :, :], posi[:, bass.ds(u.times(UT), UT), :]).then_inc(s_gi, 1)
            e.tensor_copy(gwt[:, par, :, :], gat[:, bass.ds(u.times(UT), UT), :]).then_inc(s_gi, 1)
            wait(e, s_gi, 2, u, 1)
            for q in range(UT):
                for k in range(TOPK):
                    e.indirect_dma_start(out=yg[:, par, k, q, :], out_offset=None, in_=ys_d,
                                         in_offset=bass.IndirectOffsetOnAxis(ap=gidx[:, par, q, k:k + 1], axis=0)).then_inc(s_yg[par], 16)

        def u_load(e, u, par):
            wait(e, s_f5, 1, u.shift(-2), 0)
            rows = lambda d: d[bass.ds(u.times(UT * P), UT * P), :].rearrange("(j p) d -> p j d", p=P)
            e.dma_start(x1u[:, par, :, :], rows(x1_d)).then_inc(s_xu[par], 16)
            e.dma_start(shu[:, par, :, :], rows(sh_d)).then_inc(s_xu[par], 16)

        def u_store(e, u, par):
            wait(e, s_f5, 1, u, 0)
            rows = out_rows[bass.ds(u.times(UT * P), UT * P), :].rearrange("(j p) d -> p j d", p=P)
            e.dma_start(rows, x1u[:, par, :, :]).then_inc(s_out[par], 16)

        def u_sum(e, u, par):
            by_parity(e, s_yg[par], 16 * UT * TOPK, u, par)
            by_parity(e, s_xu[par], 32, u, par)
            wait(e, s_gi, 2, u, 1)
            for k in range(TOPK):
                for q in range(UT):
                    e.scalar_tensor_tensor(out=shu[:, par, q, :], in0=yg[:, par, k, q, :], scalar=gwt[:, par, q, k:k + 1],
                                           in1=shu[:, par, q, :], op0=ALU.mult, op1=ALU.add)
                e.drain()
            for q in range(UT):
                e.bn_stats(st[:, q, :], shu[:, par, q, :])
            e.drain()
            for q in range(UT):
                e.bn_aggr(mv[:, q, :], st[:, q, :])
            e.drain()
            e.tensor_scalar(va[:], mv[:, :, 1], EPS_LN, None, ALU.add).then_inc(s_f1, 1)

        def u_root(e, u, par):
            wait(e, s_f1, 1, u, 0)
            e.activation(rr[:, par, :], va[:], ACT.Ln)
            e.drain()
            e.activation(rr[:, par, :], rr[:, par, :], ACT.Exp, scale=-0.5).then_inc(s_f2, 1)

        def u_newton(e, u, par):
            wait(e, s_f2, 1, u, 0)
            r = rr[:, par, :]
            for ins in (lambda: e.tensor_tensor(tn[:], r, r, ALU.mult),
                        lambda: e.tensor_tensor(tn[:], tn[:], va[:], ALU.mult),
                        lambda: e.tensor_scalar(tn[:], tn[:], -0.5, 1.5, ALU.mult, ALU.add),
                        lambda: e.tensor_tensor(r, r, tn[:], ALU.mult)):
                ins()
                e.drain()
            e.scalar_tensor_tensor(out=nm[:, par, :], in0=mv[:, :, 0], scalar=-1.0, in1=r, op0=ALU.mult, op1=ALU.mult).then_inc(s_f3, 1)

        def u_norm(e, u, par):
            wait(e, s_f3, 1, u, 0)
            for q in range(UT):
                i = e.activation(ou[:, par, q, :], shu[:, par, q, :], ACT.Identity, scale=rr[:, par, q:q + 1], bias=nm[:, par, q:q + 1])
            i.then_inc(s_f4, 1)

        def u_add(e, u, par):
            wait(e, s_f4, 1, u, 0)
            e.tensor_tensor(x1u[:, par, :, :].rearrange("p j d -> p (j d)"), x1u[:, par, :, :].rearrange("p j d -> p (j d)"),
                            ou[:, par, :, :].rearrange("p j d -> p (j d)"), ALU.add).then_inc(s_f5, 1)

        block = ctx.enter_context(nc.Block())

        @block.sync
        def _(e):
            for x_ in range(E):
                n = NF - 1
                o = x_ * KD * FI
                e.dma_start(w_g[:, o:o + KD * FI].rearrange("p (k n) -> p k n", k=KD), Wg[x_].rearrange("(k p) n -> p k n", p=P)).then_inc(s_wt, 16)
                e.dma_start(w_u[:, o:o + KD * FI].rearrange("p (k n) -> p k n", k=KD), Wu[x_].rearrange("(k p) n -> p k n", p=P)).then_inc(s_wt, 16)
                o = x_ * NF * DM
                e.dma_start(w_d[:, o:o + n * DM].rearrange("p (k n) -> p k n", k=n), Wd[x_][0:n * P, :].rearrange("(k p) n -> p k n", p=P)).then_inc(s_wt, 16)
                e.dma_start(w_d[0:FI - n * P, o + n * DM:o + NF * DM], Wd[x_][n * P:FI, :]).then_inc(s_wt, 16)
                e.wait_ge(s_wt, 64 * (x_ + 1))
            u_load(e, Chunk(0), 0)
            u_load(e, Chunk(1), 1)

            def step(e, u, par):
                u_store(e, u, par)
                by_parity(e, s_out[par], 16, u, par)
                u_load(e, u.shift(2), par)
            with e.Fori(0, (NU - 2) // 2) as i:
                step(e, Chunk(0, i), 0)
                step(e, Chunk(1, i), 1)
            for k in (NU - 2, NU - 1):
                u_store(e, Chunk(k), k % 2)
            for p in range(2):
                e.wait_ge(s_out[p], 16 * NU // 2)

        @block.gpsimd
        def _(e):
            tiles(e, none, tile_out, tile_in)
            e.wait_ge(s_ys, 16 * NT)
            units(e, u_gather)

        @block.tensor
        def _(e):
            tiles(e, up, pe_second, turn_in)

        @block.scalar
        def _(e):
            tiles(e, act_silu, act_keep_h, act_keep_x)
            units(e, lambda e, u, par: (u_root(e, u, par), u_norm(e, u, par)))

        @block.vector
        def _(e):
            tiles(e, dve_mul, dve_second, none)
            units(e, lambda e, u, par: (u_sum(e, u, par), u_newton(e, u, par), u_add(e, u, par)))


_INS = ["L0_attn_x", "L0_attn_norm_w", "L0_attn_in_proj_w", "L0_attn_conv_w", "L0_attn_dt_w", "L0_attn_dt_b",
        "L0_attn_A_log", "L0_attn_B_w", "L0_attn_C_w", "L0_attn_D_skip", "L0_attn_out_proj_w",
        "L0_ffn_gate_w", "L0_ffn_Wg", "L0_ffn_Wu", "L0_ffn_Wd", "L0_ffn_Sg", "L0_ffn_Su", "L0_ffn_Sd"]


def kernel(**inputs):
    import numpy as _np
    import concourse.bacc as _bacc
    from concourse import mybir as _mybir
    from concourse.bass_utils import run_bass_kernel_spmd as _run

    nc = _bacc.Bacc("TRN2", target_bir_lowering=False, num_devices=1)
    arrays, args = {}, []
    for name in _INS:
        a = _np.ascontiguousarray(inputs[name])
        arrays[f"in_{name}_dram"] = a
        args.append(nc.dram_tensor(f"in_{name}_dram", a.shape, _mybir.dt.from_np(a.dtype), kind="ExternalInput").ap())
    args.append(nc.dram_tensor("out_0_dram", inputs["L0_attn_x"].shape, _mybir.dt.float32, kind="ExternalOutput").ap())
    build(nc, *args)
    r = _run(nc, [arrays], core_ids=[0])
    return r.results[0]["out_0_dram"]
```

```python
from collections import defaultdict
from contextlib import ExitStack

import numpy as np
import concourse.bass as bass
from concourse import mybir

F32 = mybir.dt.float32
I32 = mybir.dt.int32
U32 = mybir.dt.uint32
ALU = mybir.AluOpType
ACT = mybir.ActivationFunctionType
AX = mybir.AxisListType
POOL = mybir.EngineType.Pool
SYNC = mybir.EngineType.SP

P = 128
DM = 256
DI = 512
NS = 16
TAPS = 4
E = 8
TOPK = 2
FI = 704
SI = 352
NTOK = 4096
CH = 512
NCH = NTOK // CH
J = CH // P
KD = DM // P
ND = DI // P
SLOTS = NS * ND
CAP = NTOK + P
NT = NTOK * TOPK // P + E - 1
EPS_LN = 1e-5
EPS_RMS = 1e-6
SIT = [(t * P, min(P, SI - t * P)) for t in range((SI + P - 1) // P)]
FIT = [(t * P, min(P, FI - t * P)) for t in range((FI + P - 1) // P)]
FH = FI // 2
USES = {"A0": ("xnT0", "gate0", "gate2", "inner0", "inner2", "bT", "bc", "dt1", "dt3"),
        "A1": ("xnT1", "gate1", "gate3", "inner1", "inner3", "dt0", "dt2"),
        "A2": ("y0", "y2", "out0", "xfT0", "logit", "sg0", "sg2", "su1", "sd0"),
        "A3": ("y1", "y3", "out1", "xfT1", "rank", "sg1", "su0", "su2", "sd1")}
USE = {name: (b, k) for b, names in USES.items() for k, name in enumerate(names)}


PLAN = dict(
    stats=0, root=2, newton=3, norm=5, xT=[9, 11], xT_keep=[12, 12],
    gate=[15, 17, 19, 21], gate_keep=[18, 19, 21, 23], silu=24,
    inner=[23, 25, 27, 29], mul=[25, 25, 28, 31], tap0=[27, 28, 30, 31], taps=[27, 29, 32, 32],
    bT=33, bT_keep=36, bT_store=38, bc=37, bc_keep=37,
    dt=[34, 39, 41, 46], dt_act=[38, 42, 46, 51], dt_sum=[39, 44, 48, 52], dt_mul=[45, 49, 54, 57],
    y=[4, 4, 5, 6], y_keep=[3, 4, 5, 5], out=[6, 12], o_stats=15, o_root=16, o_newton=17, o_norm=18, x1=19, x1_store=13,
    l_stats=21, l_root=23, l_newton=25, l_norm=27, fT=[28, 28], fT_keep=[28, 29],
    logit=31, route=35, rank=37, e2=36, place=38, scatter=[39, 42, 43, 46],
    sg=[39, 40, 43], sg_keep=[41, 44, 44], sh_silu=46, su=[45, 47, 48], sh_mul=[47, 48, 49],
    sd=[56, 59], sd_keep=[58, 62], sh_store=63,
    step=1, ahead_act=1, ahead_pool=3)
LOGEXP = "natural_log_exp_and_others"


class Chunk:

    def __init__(self, add, reg=None, stride=2):
        self.add, self.reg, self.stride = add, reg, stride

    def shift(self, by):
        return Chunk(self.add + by, self.reg, self.stride)

    def times(self, n, plus=0):
        if self.reg is None:
            return self.add * n + plus
        return self.reg * (self.stride * n) + (self.add * n + plus)


def wait(eng, sem, per, c, k):
    v = c.times(per, k + 1)
    if isinstance(v, int) and v <= 0:
        return
    eng.wait_ge(sem, v)
    if not isinstance(v, int) and eng.engine in (POOL, SYNC):
        eng.nop(nofuse=True)


def then(eng, ins):
    eng.drain()


def build(nc, x, norm_w, in_proj_w, conv_w, dt_w, dt_b, A_log, B_w, C_w, D_skip, out_proj_w,
          gate_w, Wg, Wu, Wd, Sg, Su, Sd, out):
    x_rows = x.rearrange("b t d -> (b t) d")
    out_rows = out.rearrange("b t d -> (b t) d")

    x1_d = nc.dram_tensor("x1_scratch", (NTOK, DM), F32).ap()
    sh_d = nc.dram_tensor("shared_scratch", (NTOK, DM), F32).ap()
    xs_d = nc.dram_tensor("expert_in_scratch", (E * CAP, DM), F32).ap()
    b_d = nc.dram_tensor("b_scratch", (NCH * NS, CH), F32).ap()
    ys_d = nc.dram_tensor("expert_out_scratch", (NT * P, DM), F32).ap()

    with ExitStack() as top:
        def sem(name):
            return top.enter_context(nc.semaphore(name))

        def sbp(name, shape, dt=F32):
            return top.enter_context(nc.sbuf_tensor(name, shape, dt))

        ident = sbp("ident", [P, P])
        base = sbp("base", [P, E])
        posi = sbp("posi", [P, NTOK // P, TOPK], U32)
        posa = sbp("posa", [P, NTOK // P, TOPK])
        expa = sbp("expa", [P, NTOK // P, TOPK])
        gat = sbp("gat", [P, NTOK // P, TOPK])
        padi = sbp("padi", [P, E], U32)
        tab = sbp("tab", [1, 2, NT + 1], I32)

        phase1(nc, sem, x_rows, norm_w, in_proj_w, conv_w, dt_w, dt_b, A_log, B_w, C_w, D_skip,
               out_proj_w, gate_w, Sg, Su, Sd, b_d, x1_d, sh_d, xs_d, ident, base, posi, posa, expa, gat, padi, tab)
        phase2(nc, sem, Wg, Wu, Wd, x1_d, sh_d, xs_d, ys_d, out_rows, ident, posi, gat, tab)


def phase1(nc, sem, x_rows, norm_w, in_proj_w, conv_w, dt_w, dt_b, A_log, B_w, C_w, D_skip,
           out_proj_w, gate_w, Sg, Su, Sd, b_d, x1_d, sh_d, xs_d, ident, base, posi, posa, expa, gat, padi, tab):
    with ExitStack() as ctx:
        def sb(name, shape, dt=F32):
            return ctx.enter_context(nc.sbuf_tensor(name, shape, dt))

        def bank(name):
            return ctx.enter_context(nc.psum_tensor(name, [P, 512], F32))

        w_in = sb("w_in", [P, KD, 2 * DI])
        w_dt = sb("w_dt", [P, ND, DI])
        w_bc = sb("w_bc", [P, ND, 2 * NS])
        w_out = sb("w_out", [P, ND, DM])
        w_cv = sb("w_cv", [P, ND, TAPS])
        w_nm = sb("w_nm", [P, KD])
        b_dt = sb("b_dt", [P, ND])
        a_log = sb("a_log", [P, ND, NS])
        a_exp = sb("a_exp", [P, ND, NS])
        a_neg = sb("a_neg", [P, ND, NS])
        dskip = sb("dskip", [P, ND])
        w_gt = sb("w_gt", [P, KD, E])
        w_sg = sb("w_sg", [P, KD, SI])
        w_su = sb("w_su", [P, KD, SI])
        w_sd = sb("w_sd", [P, len(SIT), DM])
        ones = sb("ones", [P, P])
        below = sb("below", [P, P])
        iota_e = sb("iota_e", [P, E])
        iota_i = sb("iota_i", [P, E], I32)
        capi = sb("capi", [P, E], I32)
        xp = sb("xp", [P, J, DM])
        st = sb("st", [P, J, 6])
        mv = sb("mv", [P, J, 2])
        va = sb("va", [P, J])
        r0 = sb("r0", [P, J])
        tn = sb("tn", [P, J])
        nmr = sb("nmr", [P, J])
        xn = sb("xn", [P, J, DM])
        xnT = sb("xnT", [P, KD, CH])
        sg = sb("sg", [P, ND, CH])
        xin = sb("xin", [P, ND, TAPS - 1 + CH])
        xc = [sb(f"xc{i}", [P, ND, CH]) for i in range(2)]
        dt = [sb(f"dt{i}", [P, ND, CH]) for i in range(2)]
        u = [sb(f"u{i}", [P, ND, CH]) for i in range(2)]
        bT = sb("bT", [2 * NS, CH])
        bc = [sb(f"bc{i}", [P, J, 2 * NS]) for i in range(2)]
        NR, NB = 4, 4
        br = sb("br", [P, NR, CH])
        bb = sb("bb", [P, NB, CH])
        hh = sb("hh", [P, 2, ND, CH])
        hl = sb("hl", [P, NS, ND])
        yT = [sb(f"yT{i}", [P, J, DI]) for i in range(2)]
        xr = sb("xr", [P, J, DM])
        st2 = sb("st2", [P, J, 6])
        mv2 = sb("mv2", [P, J, 2])
        va2 = sb("va2", [P, J])
        r2 = sb("r2", [P, J])
        tn2 = sb("tn2", [P, J])
        nmr2 = sb("nmr2", [P, J])
        on = sb("on", [P, J, DM])
        xf = sb("xf", [P, J, DM])
        xfT = sb("xfT", [P, KD, CH])
        lg = sb("lg", [P, J, E])
        mx = sb("mx", [P, J, E])
        ix = sb("ix", [P, J, E], U32)
        ixf = sb("ixf", [P, J, TOPK])
        oh = sb("oh", [P, TOPK, J, E])
        mm_ = sb("mm_", [P, J + 1, E])
        dif = sb("dif", [P, J])
        e2 = sb("e2", [P, J])
        e2p = sb("e2p", [P, J])
        p1 = sb("p1", [P, J])
        pos8 = sb("pos8", [P, J, E])
        prd = sb("prd", [P, TOPK, J, E])
        posf = sb("posf", [P, J, TOPK])
        posl = sb("posl", [P, J, TOPK], U32)
        sgs = sb("sgs", [P, len(SIT), CH])
        sh = on
        cnt = sb("cnt", [P, E])
        cnti = sb("cnti", [P, E], I32)
        nti = sb("nti", [P, E], I32)
        ntf = sb("ntf", [P, E])
        one8 = sb("one8", [P, E])
        cum = sb("cum", [P, E])
        tot = sb("tot", [1, 1])
        off = sb("off", [P, E])
        capf = sb("capf", [P, E])
        adj = sb("adj", [P, NTOK // P * TOPK])
        tii = sb("tii", [1, NT + 1], I32)
        tif = sb("tif", [1, NT + 1])
        ge = sb("ge", [1, NT + 1])
        te = sb("te", [1, NT + 1])
        tp = sb("tp", [1, NT + 1])
        iop = sb("iop", [P, 1], I32)
        iopf = sb("iopf", [P, 1])
        padf = sb("padf", [P, E])
        zro = sb("zro", [P, DM])

        bA = [bank("bA0"), bank("bA1")]
        NA = len(bA)
        bH = [bank("bH0"), bank("bH1")]
        A = {n: bank(n) for n in ("A0", "A1", "A2", "A3")}
        full = {n: sem(f"full_{n}") for n in A}
        free = {n: sem(f"free_{n}") for n in A}

        s_w = sem("s_w"); s_c = sem("s_c"); s_id = sem("s_id"); s_cst = sem("s_cst"); s_an = sem("s_an")
        s_x = sem("s_x"); s_p0v = sem("s_p0v"); s_p0r = sem("s_p0r"); s_p0n = sem("s_p0n"); s_xn = sem("s_xn")
        s_t0 = sem("s_t0"); s_xc = sem("s_xc"); s_ln = sem("s_ln"); s_sil = sem("s_sil"); s_ssil = sem("s_ssil"); s_dt = sem("s_dt"); s_u = sem("s_u")
        s_bb = sem("s_bb"); s_bs = sem("s_bs"); s_bl = [sem(f"s_bl{i}") for i in range(NR)]; s_a = sem("s_a"); s_scan = sem("s_scan")
        s_ht = sem("s_ht"); s_y = sem("s_y"); s_hl = sem("s_hl")
        s_xr = sem("s_xr"); s_o1 = sem("s_o1"); s_o2 = sem("s_o2"); s_o3 = sem("s_o3"); s_x1 = sem("s_x1")
        s_l1 = sem("s_l1"); s_l2 = sem("s_l2"); s_l3 = sem("s_l3"); s_xf = sem("s_xf"); s_x1s = sem("s_x1s")
        s_m = sem("s_m"); s_e2 = sem("s_e2"); s_pos = sem("s_pos"); s_sc = sem("s_sc"); s_shs = sem("s_shs")
        s_pad = sem("s_pad"); s_padd = sem("s_padd")

        SP_, PE_, AC_, DV_, PO_ = "sync", "tensor", "scalar", "vector", "gpsimd"

        def bank_of(name):
            return A[USE[name][0]]

        def room(eng, name, c):
            b, k = USE[name]
            wait(eng, free[b], len(USES[b]), c, k)

        def filled(eng, name, c):
            b, k = USE[name]
            wait(eng, full[b], len(USES[b]), c, k)

        def emptied(eng, name, c):
            b, k = USE[name]
            wait(eng, free[b], len(USES[b]), c, k + 1)

        def all_emptied(eng, names, c):
            for name in {USE[n][0]: n for n in names}.values():
                emptied(eng, name, c)

        def fills(ins, name):
            ins.then_inc(full[USE[name][0]], 1)

        def empties(ins, name):
            ins.then_inc(free[USE[name][0]], 1)

        def rsqrt_tail(e, r, v, t):
            then(e, e.tensor_tensor(t[:], r[:], r[:], ALU.mult))
            then(e, e.tensor_tensor(t[:], t[:], v[:], ALU.mult))
            then(e, e.tensor_scalar(t[:], t[:], -0.5, 1.5, ALU.mult, ALU.add))
            then(e, e.tensor_tensor(r[:], r[:], t[:], ALU.mult))

        def already(e):
            pass

        def pre(c, par):
            s = defaultdict(list)

            def add(slot, eng, fn):
                s[(min(slot, SLOTS - 1), eng)].append(fn)

            def load_x(e):
                wait(e, s_xn, J, c.shift(-1), J - 1)
                e.dma_start(xp[:], x_rows[bass.ds(c.times(CH), CH), :].rearrange("(j p) d -> p j d", p=P)).then_inc(s_x, 16)
            add(0, SP_, load_x)

            def stats(e):
                wait(e, s_x, 16, c, 15)
                for j in range(J):
                    e.bn_stats(st[:, j, :], xp[:, j, :])
                e.drain()
                for j in range(J):
                    e.bn_aggr(mv[:, j, :], st[:, j, :])
                e.drain()
                wait(e, s_p0r, 1, c.shift(-1), 0)
                e.tensor_scalar(va[:], mv[:, :, 1], 1.0 + EPS_RMS, EPS_LN * EPS_RMS, ALU.mult, ALU.add).then_inc(s_p0v, 1)
            add(PLAN["stats"], DV_, stats)

            def root(e):
                wait(e, s_p0v, 1, c, 0)
                wait(e, s_xn, J, c.shift(-1), J - 1)
                then(e, e.activation(r0[:], va[:], ACT.Ln))
                e.activation(r0[:], r0[:], ACT.Exp, scale=-0.5).then_inc(s_p0r, 1)
            add(PLAN["root"], AC_, root)

            def newton(e):
                wait(e, s_p0r, 1, c, 0)
                wait(e, s_p0v, 1, c, 0)
                rsqrt_tail(e, r0, va, tn)
                e.scalar_tensor_tensor(out=nmr[:], in0=mv[:, :, 0], scalar=-1.0, in1=r0[:], op0=ALU.mult, op1=ALU.mult).then_inc(s_p0n, 1)
            add(PLAN["newton"], DV_, newton)

            def norm(e):
                wait(e, s_p0n, 1, c, 0)
                filled(e, "xnT1", c.shift(-1))
                for j in range(J):
                    e.activation(xn[:, j, :], xp[:, j, :], ACT.Identity, scale=r0[:, j:j + 1], bias=nmr[:, j:j + 1]).then_inc(s_xn, 1)
            add(PLAN["norm"], AC_, norm)

            def turn_x(k):
                def f(e):
                    b = f"xnT{k}"
                    wait(e, s_xn, J, c, J - 1)
                    room(e, b, c)
                    for j in range(J):
                        i = e.transpose(bank_of(b)[:, j * P:(j + 1) * P], xn[:, j, k * P:(k + 1) * P], ident[:])
                    fills(i, b)
                return f

            def keep_x(k):
                def f(e):
                    b = f"xnT{k}"
                    filled(e, b, c)
                    empties(e.copy(xnT[:, k, :], bank_of(b)[:]), b)
                return f
            for k in range(KD):
                add(PLAN["xT"][k], PE_, turn_x(k))
                add(PLAN["xT_keep"][k], AC_, keep_x(k))

            def product(slot, step, b, parts, ready):
                n = len(parts)
                for q, part in enumerate(parts):
                    def f(e, q=q, part=part):
                        if q == 0:
                            room(e, b, c)
                            ready(e)
                        i = part(e)
                        if q == n - 1:
                            fills(i, b)
                    add(slot + int(q * step), PE_, f)

            def x_kept(e):
                emptied(e, "xnT0", c)
                emptied(e, "xnT1", c)

            def p1_parts(b, off, d):
                return [lambda e, k=k: e.matmul(bank_of(b)[:], w_in[:, k, off + d * P:off + (d + 1) * P], xnT[:, k, :],
                                                start=(k == 0), stop=(k == KD - 1)) for k in range(KD)]

            def gate_act(d):
                def f(e):
                    filled(e, f"gate{d}", c)
                    if d == 0:
                        emptied(e, f"inner{ND - 1}", c.shift(-1))
                    empties(e.copy(sg[:, d, :], bank_of(f"gate{d}")[:]), f"gate{d}")
                return f

            def silu_act(e):
                all_emptied(e, [f"gate{d}" for d in range(ND)], c)
                e.activation(sg[:].rearrange("p d t -> p (d t)"), sg[:].rearrange("p d t -> p (d t)"), ACT.Silu).then_inc(s_sil, 1)
                e.preload_act_table_set(LOGEXP)

            def p1_dve(d):
                def f(e):
                    wait(e, s_xc, ND, c.shift(-1), d)
                    if par:
                        then(e, e.tensor_copy(xin[:, d, 0:TAPS - 1], xin[:, d, CH:CH + TAPS - 1]))
                    else:
                        then(e, e.memset(xin[:, d, 0:TAPS - 1], 0.0))
                    wait(e, s_sil, 1, c, 0)
                    filled(e, f"inner{d}", c)
                    empties(e.tensor_tensor(xin[:, d, TAPS - 1:], sg[:, d, :], bank_of(f"inner{d}")[:], ALU.mult), f"inner{d}")
                return f

            def tap0(d):
                def f(e):
                    emptied(e, f"inner{d}", c)
                    filled(e, "out1", c.shift(-2))
                    e.mul(xc[par][:, d, :], xin[:, d, 0:CH], w_cv[:, d, 0:1]).then_inc(s_t0, 1)
                return f

            def taps(d):
                def f(e):
                    wait(e, s_t0, ND, c, d)
                    for k in range(1, TAPS):
                        i = e.scalar_tensor_tensor(out=xc[par][:, d, :], in0=xin[:, d, k:k + CH], scalar=w_cv[:, d, k:k + 1],
                                                   in1=xc[par][:, d, :], op0=ALU.mult, op1=ALU.add)
                        if k < TAPS - 1:
                            then(e, i)
                    i.then_inc(s_xc, 1)
                return f
            for d in range(ND):
                product(PLAN["gate"][d], PLAN["step"], f"gate{d}", p1_parts(f"gate{d}", DI, d), x_kept if d == 0 else already)
                add(PLAN["gate_keep"][d], AC_, gate_act(d))
                product(PLAN["inner"][d], PLAN["step"], f"inner{d}", p1_parts(f"inner{d}", 0, d), already)
                add(PLAN["mul"][d], DV_, p1_dve(d))
                add(PLAN["tap0"][d], AC_, tap0(d))
                add(PLAN["taps"][d], DV_, taps(d))
            add(PLAN["silu"], AC_, silu_act)

            def conv_done(e):
                wait(e, s_xc, ND, c, ND - 1)

            bT_parts = [lambda e, k=k: e.matmul(bank_of("bT")[0:2 * NS, :], w_bc[:, k, :], xc[par][:, k, :],
                                                start=(k == 0), stop=(k == ND - 1)) for k in range(ND)]
            product(PLAN["bT"], PLAN["step"], "bT", bT_parts, conv_done)

            def bT_act(e):
                filled(e, "bT", c)
                wait(e, s_bs, 16, c.shift(-1), 15)
                empties(e.copy(bT[:], bank_of("bT")[0:2 * NS, :]), "bT")
            add(PLAN["bT_keep"], AC_, bT_act)

            def bT_store(e):
                emptied(e, "bT", c)
                e.dma_start(b_d[bass.ds(c.times(NS), NS), :], bT[0:NS, :]).then_inc(s_bs, 16)
            add(PLAN["bT_store"], SP_, bT_store)

            def bc_pe(e):
                room(e, "bc", c)
                e.nop(nofuse=True)
                for j in range(J):
                    i = e.transpose(bank_of("bc")[:, j * 2 * NS:(j + 1) * 2 * NS], bT[:, j * P:(j + 1) * P], ident[0:2 * NS, 0:2 * NS])
                fills(i, "bc")
            add(PLAN["bc"], PE_, bc_pe)

            def bc_act(e):
                filled(e, "bc", c)
                wait(e, s_y, SLOTS, c.shift(-2), SLOTS - 1)
                empties(e.copy(bc[par][:].rearrange("p j s -> p (j s)"), bank_of("bc")[:, 0:J * 2 * NS]), "bc")
            add(PLAN["bc_keep"], AC_, bc_act)

            def dt_parts(m):
                return [lambda e, k=k: e.matmul(bank_of(f"dt{m}")[:], w_dt[:, k, m * P:(m + 1) * P], xc[par][:, k, :],
                                                start=(k == 0), stop=(k == ND - 1)) for k in range(ND)]

            def dt_act(m):
                def f(e):
                    if m == 0:
                        wait(e, s_bb, SLOTS, c.shift(-2), SLOTS - 1)
                    filled(e, f"dt{m}", c)
                    e.activation(u[par][:, m, :], bank_of(f"dt{m}")[:], ACT.Relu, bias=b_dt[:, m:m + 1])
                    empties(e.activation(dt[par][:, m, :], bank_of(f"dt{m}")[:], ACT.Abs, bias=b_dt[:, m:m + 1]), f"dt{m}")
                    emptied(e, f"dt{m}", c)
                    then(e, e.activation(dt[par][:, m, :], dt[par][:, m, :], ACT.Exp, scale=-1.0))
                    e.activation(dt[par][:, m, :], dt[par][:, m, :], ACT.Ln, bias=1.0).then_inc(s_ln, 1)
                return f

            def dt_sum(m):
                def f(e):
                    wait(e, s_ln, ND, c, m)
                    e.tensor_tensor(dt[par][:, m, :], dt[par][:, m, :], u[par][:, m, :], ALU.add).then_inc(s_dt, 1)
                return f

            def dt_mul(m):
                def f(e):
                    wait(e, s_dt, ND, c, m)
                    wait(e, s_xc, ND, c, m)
                    e.tensor_tensor(u[par][:, m, :], dt[par][:, m, :], xc[par][:, m, :], ALU.mult).then_inc(s_u, 1)
                return f

            for m in range(ND):
                product(PLAN["dt"][m], PLAN["step"], f"dt{m}", dt_parts(m), conv_done if m == 0 else already)
                add(PLAN["dt_act"][m], AC_, dt_act(m))
                add(PLAN["dt_sum"][m], PO_, dt_sum(m))
                add(PLAN["dt_mul"][m], PO_, dt_mul(m))

            return s

        def post(c, par):
            s = defaultdict(list)

            def add(slot, eng, fn):
                s[(min(slot, SLOTS - 1), eng)].append(fn)

            def load_r(e):
                e.dma_start(xr[:], x_rows[bass.ds(c.times(CH), CH), :].rearrange("(j p) d -> p j d", p=P)).then_inc(s_xr, 16)
            add(1, SP_, load_r)

            def product(slot, step, b, parts, ready):
                n = len(parts)
                for q, part in enumerate(parts):
                    def f(e, q=q, part=part):
                        if q == 0:
                            room(e, b, c)
                            ready(e)
                        i = part(e)
                        if q == n - 1:
                            fills(i, b)
                    add(slot + int(q * step), PE_, f)

            def yb_pe(d):
                def f(e):
                    b = f"y{d}"
                    wait(e, s_y, SLOTS, c, SLOTS - 1)
                    room(e, b, c)
                    for j in range(J):
                        i = e.transpose(bank_of(b)[:, j * P:(j + 1) * P], yT[par][:, j, d * P:(d + 1) * P], ident[:])
                    fills(i, b)
                return f

            def yb_dve(d):
                def f(e):
                    b = f"y{d}"
                    filled(e, b, c)
                    empties(e.scalar_tensor_tensor(out=xc[par][:, d, :], in0=xc[par][:, d, :], scalar=dskip[:, d:d + 1], in1=bank_of(b)[:],
                                                   op0=ALU.mult, op1=ALU.add), b)
                return f
            for d in range(ND):
                add(PLAN["y"][d], PE_, yb_pe(d))
                add(PLAN["y_keep"][d], DV_, yb_dve(d))

            def y_ready(e):
                all_emptied(e, [f"y{d}" for d in range(ND)], c)

            def out_parts(q):
                return [lambda e, j=j, k=k: e.matmul(bank_of(f"out{q}")[:, (j % 2) * DM:(j % 2 + 1) * DM], xc[par][:, k, j * P:(j + 1) * P],
                                                     w_out[:, k, :], start=(k == 0), stop=(k == ND - 1))
                        for j in (2 * q, 2 * q + 1) for k in range(ND)]
            product(PLAN["out"][0], PLAN["step"] / 2, "out0", out_parts(0), y_ready)
            product(PLAN["out"][1], PLAN["step"] / 2, "out1", out_parts(1), already)

            def o_stats(e):
                for j in range(J):
                    filled(e, f"out{j // 2}", c)
                    e.bn_stats(st2[:, j, :], bank_of(f"out{j // 2}")[:, (j % 2) * DM:(j % 2 + 1) * DM])
                e.drain()
                for j in range(J):
                    e.bn_aggr(mv2[:, j, :], st2[:, j, :])
                e.drain()
                e.tensor_scalar(va2[:], mv2[:, :, 1], EPS_LN, None, ALU.add).then_inc(s_o1, 1)
            add(PLAN["o_stats"], DV_, o_stats)

            def o_root(e):
                wait(e, s_o1, 1, c, 0)
                then(e, e.activation(r2[:], va2[:], ACT.Ln))
                e.activation(r2[:], r2[:], ACT.Exp, scale=-0.5).then_inc(s_o2, 1)
            add(PLAN["o_root"], AC_, o_root)

            def o_newton(e):
                wait(e, s_o2, 1, c, 0)
                wait(e, s_o1, 1, c, 0)
                rsqrt_tail(e, r2, va2, tn2)
                e.scalar_tensor_tensor(out=nmr2[:], in0=mv2[:, :, 0], scalar=-1.0, in1=r2[:], op0=ALU.mult, op1=ALU.mult).then_inc(s_o3, 1)
            add(PLAN["o_newton"], DV_, o_newton)

            def o_norm(e):
                wait(e, s_o3, 1, c, 0)
                wait(e, s_shs, 16, c.shift(-1), 16)
                for j in range(J):
                    b = f"out{j // 2}"
                    i = e.activation(on[:, j, :], bank_of(b)[:, (j % 2) * DM:(j % 2 + 1) * DM], ACT.Identity,
                                     scale=r2[:, j:j + 1], bias=nmr2[:, j:j + 1])
                    if j % 2:
                        empties(i, b)
            add(PLAN["o_norm"], AC_, o_norm)

            def x1_pool(e):
                emptied(e, "out0", c)
                emptied(e, "out1", c)
                wait(e, s_xr, 16, c, 15)
                e.tensor_tensor(xr[:].rearrange("p j d -> p (j d)"), xr[:].rearrange("p j d -> p (j d)"),
                                on[:].rearrange("p j d -> p (j d)"), ALU.add).then_inc(s_x1, 1)
            add(PLAN["x1"], PO_, x1_pool)

            def x1_store(e):
                wait(e, s_x1, 1, c, 0)
                e.dma_start(x1_d[bass.ds(c.times(CH), CH), :].rearrange("(j p) d -> p j d", p=P), xr[:]).then_inc(s_x1s, 16)
            add(PLAN["x1_store"], SP_, x1_store)

            def l_stats(e):
                wait(e, s_x1, 1, c, 0)
                for j in range(J):
                    e.bn_stats(st2[:, j, :], xr[:, j, :])
                e.drain()
                emptied(e, "out1", c)
                e.nop(nofuse=True)
                for j in range(J):
                    e.bn_aggr(mv2[:, j, :], st2[:, j, :])
                e.drain()
                e.tensor_scalar(va2[:], mv2[:, :, 1], EPS_LN, None, ALU.add).then_inc(s_l1, 1)
            add(PLAN["l_stats"], DV_, l_stats)

            def l_root(e):
                wait(e, s_l1, 1, c, 0)
                then(e, e.activation(r2[:], va2[:], ACT.Ln))
                e.activation(r2[:], r2[:], ACT.Exp, scale=-0.5).then_inc(s_l2, 1)
            add(PLAN["l_root"], AC_, l_root)

            def l_newton(e):
                wait(e, s_l2, 1, c, 0)
                wait(e, s_l1, 1, c, 0)
                rsqrt_tail(e, r2, va2, tn2)
                e.scalar_tensor_tensor(out=nmr2[:], in0=mv2[:, :, 0], scalar=-1.0, in1=r2[:], op0=ALU.mult, op1=ALU.mult).then_inc(s_l3, 1)
            add(PLAN["l_newton"], DV_, l_newton)

            def l_norm(e):
                wait(e, s_l3, 1, c, 0)
                for j in range(J):
                    e.activation(xf[:, j, :], xr[:, j, :], ACT.Identity, scale=r2[:, j:j + 1], bias=nmr2[:, j:j + 1]).then_inc(s_xf, 1)
            add(PLAN["l_norm"], AC_, l_norm)

            def turn_f(k):
                def f(e):
                    b = f"xfT{k}"
                    wait(e, s_xf, J, c, J - 1)
                    room(e, b, c)
                    for j in range(J):
                        i = e.transpose(bank_of(b)[:, j * P:(j + 1) * P], xf[:, j, k * P:(k + 1) * P], ident[:])
                    fills(i, b)
                return f

            def keep_f(k):
                def f(e):
                    filled(e, f"xfT{k}", c)
                    empties(e.copy(xfT[:, k, :], bank_of(f"xfT{k}")[:]), f"xfT{k}")
                return f
            for k in range(KD):
                add(PLAN["fT"][k], PE_, turn_f(k))
                add(PLAN["fT_keep"][k], AC_, keep_f(k))

            def lg_pe(e):
                emptied(e, "xfT0", c)
                emptied(e, "xfT1", c)
                for j in range(J):
                    for k in range(KD):
                        i = e.matmul(bank_of("logit")[:, j * E:(j + 1) * E], xfT[:, k, j * P:(j + 1) * P], w_gt[:, k, :], start=(k == 0), stop=(k == KD - 1))
                fills(i, "logit")
            add(PLAN["logit"], PE_, lg_pe)

            def route(e):
                filled(e, "logit", c)
                empties(e.tensor_copy(lg[:].rearrange("p j e -> p (j e)"), bank_of("logit")[:, 0:J * E]), "logit")
                e.drain()
                for j in range(J):
                    e.max(mx[:, j, :], lg[:, j, :])
                e.drain()
                for j in range(J):
                    e.max_index(ix[:, j, :], mx[:, j, :], lg[:, j, :])
                e.tensor_tensor(dif[:], mx[:, :, 1], mx[:, :, 0], ALU.subtract)
                e.drain()
                e.tensor_copy(ixf[:], ix[:, :, 0:TOPK])
                e.drain()
                for k in range(TOPK):
                    for j in range(J):
                        e.tensor_scalar(oh[:, k, j, :], iota_e[:], ixf[:, j, k:k + 1], None, ALU.is_equal)
                e.drain()
                e.tensor_tensor(mm_[:, 0:J, :], oh[:, 0, :, :], oh[:, 1, :, :], ALU.add).then_inc(s_m, 1)
            add(PLAN["route"], DV_, route)

            def rank_pe(e):
                wait(e, s_m, 1, c, 0)
                room(e, "rank", c)
                m = mm_[:].rearrange("p j e -> p (j e)")
                e.matmul(bank_of("rank")[:, 0:(J + 1) * E], below[:], m, start=True, stop=False)
                for q in range(1, J + 1):
                    i = e.matmul(bank_of("rank")[:, q * E:(J + 1) * E], ones[:], m[:, 0:(J + 1 - q) * E], start=False, stop=(q == J))
                fills(i, "rank")
            add(PLAN["rank"], PE_, rank_pe)

            def e2_act(e):
                wait(e, s_m, 1, c, 0)
                e.activation(e2[:], dif[:], ACT.Exp).then_inc(s_e2, 1)
            add(PLAN["e2"], AC_, e2_act)

            def place(e):
                filled(e, "rank", c)
                for j in range(J):
                    e.tensor_tensor(pos8[:, j, :], bank_of("rank")[:, j * E:(j + 1) * E], base[:], ALU.add)
                e.drain()
                empties(e.tensor_tensor(base[:], base[:], bank_of("rank")[:, J * E:(J + 1) * E], ALU.add), "rank")
                wait(e, s_e2, 1, c, 0)
                e.tensor_scalar(e2p[:], e2[:], 1.0, None, ALU.add)
                for k in range(TOPK):
                    e.tensor_tensor(prd[:, k, :, :], oh[:, k, :, :], pos8[:], ALU.mult)
                e.drain()
                e.reciprocal(p1[:], e2p[:])
                for k in range(TOPK):
                    e.tensor_reduce(posf[:, :, k], prd[:, k, :, :], AX.X, ALU.add)
                e.drain()
                e.tensor_copy(gat[:, bass.ds(c.times(J), J), 0], p1[:])
                e.tensor_tensor(gat[:, bass.ds(c.times(J), J), 1], e2[:], p1[:], ALU.mult)
                e.tensor_copy(posa[:, bass.ds(c.times(J), J), :], posf[:])
                e.tensor_copy(expa[:, bass.ds(c.times(J), J), :], ixf[:])
                e.tensor_copy(posl[:], posf[:]).then_inc(s_pos, 1)
            add(PLAN["place"], DV_, place)

            def scatter(j):
                def f(e):
                    wait(e, s_pos, 1, c, 0)
                    wait(e, s_xf, J, c, J - 1)
                    for k in range(TOPK):
                        e.indirect_dma_start(out=xs_d, out_offset=bass.IndirectOffsetOnAxis(ap=posl[:, j, k:k + 1], axis=0),
                                             in_=xf[:, j, :], in_offset=None).then_inc(s_sc, 16)
                return f
            for j in range(J):
                add(PLAN["scatter"][j], PO_, scatter(j))

            def sh_parts(b, w, t):
                i0, n = SIT[t]
                return [lambda e, k=k: e.matmul(bank_of(b)[0:n, :], w[:, k, i0:i0 + n], xfT[:, k, :], start=(k == 0), stop=(k == KD - 1))
                        for k in range(KD)]

            def sh_act(t):
                def f(e):
                    n = SIT[t][1]
                    filled(e, f"sg{t}", c)
                    empties(e.copy(sgs[0:n, t, :], bank_of(f"sg{t}")[0:n, :]), f"sg{t}")
                return f

            def sh_silu(e):
                all_emptied(e, [f"sg{t}" for t in range(len(SIT))], c)
                for t, (i0, n) in enumerate(SIT):
                    e.activation(sgs[0:n, t, :], sgs[0:n, t, :], ACT.Silu).then_inc(s_ssil, 1)
                e.preload_act_table_set(LOGEXP)

            def sh_dve(t):
                def f(e):
                    n = SIT[t][1]
                    wait(e, s_ssil, len(SIT), c, t)
                    filled(e, f"su{t}", c)
                    empties(e.tensor_tensor(sgs[0:n, t, :], sgs[0:n, t, :], bank_of(f"su{t}")[0:n, :], ALU.mult), f"su{t}")
                return f
            for t in range(len(SIT)):
                product(PLAN["sg"][t], PLAN["step"], f"sg{t}", sh_parts(f"sg{t}", w_sg, t), already)
                add(PLAN["sg_keep"][t], AC_, sh_act(t))
                product(PLAN["su"][t], PLAN["step"], f"su{t}", sh_parts(f"su{t}", w_su, t), already)
                add(PLAN["sh_mul"][t], DV_, sh_dve(t))
            add(PLAN["sh_silu"], AC_, sh_silu)

            def h_ready(e):
                emptied(e, f"su{len(SIT) - 1}", c)

            def sd_parts(q):
                return [lambda e, j=j, t=t: e.matmul(bank_of(f"sd{q}")[:, (j % 2) * DM:(j % 2 + 1) * DM], sgs[0:SIT[t][1], t, j * P:(j + 1) * P],
                                                     w_sd[0:SIT[t][1], t, :], start=(t == 0), stop=(t == len(SIT) - 1))
                        for j in (2 * q, 2 * q + 1) for t in range(len(SIT))]

            def sd_act(q):
                def f(e):
                    b = f"sd{q}"
                    filled(e, b, c)
                    wait(e, s_x1, 1, c, 0)
                    empties(e.copy(sh[:, 2 * q:2 * q + 2, :].rearrange("p j d -> p (j d)"), bank_of(b)[:]), b)
                return f
            for q in range(2):
                product(PLAN["sd"][q], PLAN["step"] / 2, f"sd{q}", sd_parts(q), h_ready if q == 0 else already)
                add(PLAN["sd_keep"][q], AC_, sd_act(q))

            def sh_store(e):
                emptied(e, "sd0", c)
                emptied(e, "sd1", c)
                e.dma_start(sh_d[bass.ds(c.times(CH), CH), :].rearrange("(j p) d -> p j d", p=P), sh[:]).then_inc(s_shs, 16)
            add(PLAN["sh_store"], SP_, sh_store)

            def done_sp(e):
                wait(e, s_xf, J, c, J - 1)
                wait(e, s_x1s, 16, c, 15)
            add(SLOTS - 1, SP_, done_sp)

            def done_rows(e):
                wait(e, s_sc, 16 * J * TOPK, c, 16 * J * TOPK - 1)
                filled(e, "xfT1", c)
            add(SLOTS - 1, PO_, done_rows)
            add(SLOTS - 1, DV_, done_rows)
            add(SLOTS - 1, AC_, done_rows)
            return s

        def main_act(e, c, par, k):
            n, d = divmod(k, ND)
            if n == 0:
                wait(e, s_dt, ND, c, d)
            wait(e, s_scan, SLOTS, c, k - NA)
            e.activation(bA[k % NA][:], dt[par][:, d, :], ACT.Exp, scale=a_neg[:, d, n:n + 1]).then_inc(s_a, 1)

        def main_pool(e, c, par, k):
            n, d = divmod(k, ND)
            if n == 0:
                wait(e, s_u, ND, c, d)
            if d == 0:
                wait(e, s_bl[n % NR], 16 * NS // NR, c, 16 * (n // NR) + 15)
            wait(e, s_scan, SLOTS, c, k - NB)
            e.tensor_tensor(bb[:, k % NB, :], u[par][:, d, :], br[:, n % NR, :], ALU.mult).then_inc(s_bb, 1)

        def load_b(e, c, n):
            if n == 0:
                wait(e, s_bs, 16, c, 15)
            wait(e, s_bb, SLOTS, c, (n - NR) * ND + ND - 1)
            row = b_d[bass.ds(c.times(NS, n), 1), :].broadcast_to([P, CH])
            e.dma_start(br[:, n % NR, :], row).then_inc(s_bl[n % NR], 16)

        def keep_last(e, c, n):
            wait(e, s_scan, SLOTS, c, n * ND + ND - 1)
            e.tensor_copy(hl[:, n, :], hh[:, n % 2, :, CH - 1]).then_inc(s_hl, 1)

        def main_pe(e, c, par, k, first):
            n, d = divmod(k, ND)
            if not first:
                if d == 0:
                    wait(e, s_scan, SLOTS, c, k - 1)
                wait(e, s_y, SLOTS, c, k - ND - 2)
                for q in range(ND):
                    i = e.transpose(bH[d % 2][:, q * P:(q + 1) * P], hh[:, (n - 1) % 2, q, d * P:(d + 1) * P], ident[:])
                i.then_inc(s_ht, 1)

        def main_dve(e, c, par, k, first, scan=True):
            n, d = divmod(k, ND)
            if scan:
                wait(e, s_a, SLOTS, c, k)
                wait(e, s_bb, SLOTS, c, k)
                if d == 0:
                    wait(e, s_ht, SLOTS, c, k - ND - 1)
                if par:
                    if k == 0:
                        e.wait_ge(s_hl, c.times(NS // 2, NS // 2))
                else:
                    if d == 0 and n >= 2:
                        e.wait_ge(s_hl, c.times(NS // 2, n - 1))
                e.tensor_tensor_scan(hh[:, n % 2, d, :], bA[k % NA][:], bb[:, k % NB, :], hl[:, n, d:d + 1] if par else 0.0,
                                     ALU.mult, ALU.add).then_inc(s_scan, 1)
            if not first:
                wait(e, s_ht, SLOTS, c, k - ND)
                if n == 0:
                    cm, yy = bc[1 - par][:, d, 2 * NS - 1:2 * NS], yT[1 - par]
                else:
                    cm, yy = bc[par][:, d, NS + n - 1:NS + n], yT[par]
                if n == 1:
                    if d == 0:
                        emptied(e, "bc", c)
                    e.tensor_scalar(yy[:, d, :], bH[d % 2][:], cm, None, ALU.mult).then_inc(s_y, 1)
                else:
                    wait(e, s_y, SLOTS, c, k - 2 * ND)
                    e.scalar_tensor_tensor(out=yy[:, d, :], in0=bH[d % 2][:], scalar=cm, in1=yy[:, d, :],
                                           op0=ALU.mult, op1=ALU.add).then_inc(s_y, 1)

        def main_sync(e, c, par, k):
            if k % ND == 0:
                load_b(e, c, k // ND)

        AHEAD = {AC_: (main_act, PLAN["ahead_act"]), PO_: (main_pool, PLAN["ahead_pool"]), SP_: (main_sync, (NR - 1) * ND)}

        def chunk(e, name, c, par, first=False, last=False):
            side = []
            if not last:
                side.append(pre(c.shift(1), 1 - par))
            if not first:
                side.append(post(c.shift(-1), 1 - par))
            for k in range(SLOTS):
                f = first and k < ND
                if name in AHEAD:
                    fn, by = AHEAD[name]
                    if k + by < SLOTS:
                        fn(e, c, par, k + by)
                    elif not last:
                        fn(e, c.shift(1), 1 - par, k + by - SLOTS)
                elif name == PE_:
                    main_pe(e, c, par, k, f)
                elif name == DV_:
                    main_dve(e, c, par, k, f)
                if name == PO_ and par == 0 and k % ND == ND - 1 and k > ND:
                    keep_last(e, c, k // ND - 1)
                for s in side:
                    for fn in s[(k, name)]:
                        fn(e)
            if name == PO_ and par == 0:
                keep_last(e, c, NS - 1)
            if last:
                for d in range(ND):
                    if name == PE_:
                        main_pe(e, c.shift(1), 1 - par, d, False)
                    if name == DV_:
                        main_dve(e, c.shift(1), 1 - par, d, False, scan=False)

        def run(e, name):
            s = pre(Chunk(0), 0)
            for k in range(SLOTS):
                for fn in s[(k, name)]:
                    fn(e)
            if name in AHEAD:
                fn, by = AHEAD[name]
                for k in range(by):
                    fn(e, Chunk(0), 0, k)
            chunk(e, name, Chunk(0), 0, first=True)
            with e.Fori(0, (NCH - 2) // 2) as i:
                chunk(e, name, Chunk(1, i), 1)
                chunk(e, name, Chunk(2, i), 0)
            chunk(e, name, Chunk(NCH - 1), 1, last=True)
            s = post(Chunk(NCH - 1), 1)
            for k in range(SLOTS):
                for fn in s[(k, name)]:
                    fn(e)

        def table(e):
            def link(i):
                then(e, i)
            emptied(e, "rank", Chunk(NCH - 1))
            link(e.tensor_copy(iopf[:], iop[:]))
            link(e.tensor_scalar(padf[:], base[:], iopf[:, 0:1], None, ALU.add))
            e.tensor_copy(padi[:], padf[:]).then_inc(s_pad, 1)
            link(e.tensor_scalar(capf[:], iota_e[:], float(CAP), None, ALU.mult))
            link(e.tensor_tensor(cnt[:], base[:], capf[:], ALU.subtract))
            link(e.tensor_scalar(cnti[:], cnt[:], float(P - 1), None, ALU.add))
            link(e.tensor_single_scalar(nti[:], cnti[:], P.bit_length() - 1, ALU.arith_shift_right))
            link(e.tensor_copy(ntf[:], nti[:]))
            link(e.tensor_tensor_scan(cum[:], one8[:], ntf[:], 0.0, ALU.mult, ALU.add))
            link(e.tensor_scalar(tot[:], cum[0:1, E - 1:E], -1.0, None, ALU.add))
            link(e.tensor_copy(tif[:], tii[:]))
            link(e.tensor_scalar(tif[:], tif[:], tot[:, 0:1], None, ALU.min))
            link(e.tensor_scalar(te[:], tif[:], 0.0, None, ALU.mult))
            link(e.tensor_copy(tp[:], tif[:]))
            for x_ in range(E - 1):
                link(e.tensor_scalar(ge[:], tif[:], cum[0:1, x_:x_ + 1], None, ALU.is_ge))
                link(e.tensor_tensor(te[:], te[:], ge[:], ALU.add))
                link(e.tensor_scalar(ge[:], ge[:], ntf[0:1, x_:x_ + 1], None, ALU.mult))
                link(e.tensor_tensor(tp[:], tp[:], ge[:], ALU.subtract))
            link(e.tensor_copy(tab[:, 0, :], te[:]))
            link(e.tensor_scalar(tp[:], tp[:], float(P), None, ALU.mult))
            link(e.tensor_scalar(te[:], te[:], float(CAP), None, ALU.mult))
            link(e.tensor_tensor(tp[:], te[:], tp[:], ALU.add))
            link(e.tensor_copy(tab[:, 1, :], tp[:]))
            link(e.tensor_tensor(off[:], cum[:], ntf[:], ALU.subtract))
            link(e.tensor_scalar(off[:], off[:], float(P), None, ALU.mult))
            link(e.tensor_tensor(off[:], off[:], capf[:], ALU.subtract))
            pa, ea = (t[:].rearrange("p t k -> p (t k)") for t in (posa, expa))
            for x_ in range(E):
                link(e.tensor_scalar(adj[:], ea, float(x_), off[:, x_:x_ + 1], ALU.is_equal, ALU.mult))
                link(e.tensor_tensor(pa, pa, adj[:], ALU.add))
            link(e.tensor_copy(posi[:].rearrange("p t k -> p (t k)"), pa))

        block = ctx.enter_context(nc.Block())

        NW = 16 + 2
        @block.sync
        def _(e):
            def ld(dst, src, **kw):
                e.dma_start(dst, src, **kw).then_inc(s_w, 16)
            ld(w_in[:], in_proj_w.rearrange("(k p) n -> p k n", p=P))
            ld(w_nm[:], norm_w.rearrange("(k p) -> p k", p=P), allow_slow_non_contiguous=True)
            ld(w_cv[:], conv_w.rearrange("(k p) a t -> p k (a t)", p=P))
            ld(w_dt[:], dt_w.rearrange("(k p) n -> p k n", p=P))
            ld(w_bc[:, :, 0:NS], B_w.rearrange("(k p) n -> p k n", p=P))
            ld(w_bc[:, :, NS:2 * NS], C_w.rearrange("(k p) n -> p k n", p=P))
            ld(b_dt[:], dt_b.rearrange("(k p) -> p k", p=P), allow_slow_non_contiguous=True)
            ld(a_log[:], A_log.rearrange("(k p) n -> p k n", p=P))
            ld(dskip[:], D_skip.rearrange("(k p) -> p k", p=P), allow_slow_non_contiguous=True)
            ld(w_out[:], out_proj_w.rearrange("(k p) n -> p k n", p=P))
            ld(w_gt[:], gate_w.rearrange("(k p) n -> p k n", p=P))
            ld(w_sg[:], Sg.rearrange("(k p) n -> p k n", p=P))
            ld(w_su[:], Su.rearrange("(k p) n -> p k n", p=P))
            for t, (i0, n) in enumerate(SIT):
                ld(w_sd[0:n, t, :], Sd[i0:i0 + n, :])
            run(e, SP_)
            e.wait_ge(s_x1s, 16 * NCH)
            e.wait_ge(s_shs, 16 * NCH + 1)

        NWD = 13 + len(SIT)

        @block.gpsimd
        def _(e):
            def sel(t, op, fill, base_, pattern, cm):
                return e.affine_select(out=t, in_=t, compare_op=op, fill=fill, base=base_, pattern=pattern, channel_multiplier=cm)
            e.memset(ident[:], 0.0).then_inc(s_c, 1)
            e.memset(below[:], 1.0).then_inc(s_c, 1)
            e.memset(ones[:], 1.0).then_inc(s_c, 1)
            e.memset(zro[:], 0.0).then_inc(s_c, 1)
            e.memset(one8[:], 1.0).then_inc(s_c, 1)
            e.memset(mm_[:, J, :], 0.0).then_inc(s_c, 1)
            e.iota(iota_i[:], [[1, E]], base=0, channel_multiplier=0).then_inc(s_c, 1)
            e.iota(capi[:], [[CAP, E]], base=0, channel_multiplier=0).then_inc(s_c, 1)
            e.iota(iop[:], [[0, 1]], base=0, channel_multiplier=1).then_inc(s_c, 1)
            e.iota(tii[:], [[1, NT + 1]], base=0, channel_multiplier=0).then_inc(s_c, 1)
            for s_ in [*free.values(), s_shs]:
                e.nop(nofuse=True).then_inc(s_, 1)
            e.wait_ge(s_c, 10)
            sel(ident[:], ALU.not_equal, 1.0, 0, [[-1, P]], 1).then_inc(s_id, 1)
            sel(below[:], ALU.is_gt, 0.0, 0, [[1, P]], -1).then_inc(s_id, 1)
            e.wait_ge(s_id, 2)
            e.wait_ge(s_cst, 3)
            run(e, PO_)
            e.wait_ge(s_pad, 1)
            for x_ in range(E):
                e.indirect_dma_start(out=xs_d, out_offset=bass.IndirectOffsetOnAxis(ap=padi[:, x_:x_ + 1], axis=0),
                                     in_=zro[:], in_offset=None).then_inc(s_padd, 16)
            e.wait_ge(s_padd, 16 * E)
            e.wait_ge(s_sc, 16 * J * TOPK * NCH)

        @block.scalar
        def _(e):
            e.wait_ge(s_w, 16 * NWD)
            e.activation(a_exp[:], a_log[:], ACT.Exp).then_inc(s_an, 1)
            e.wait_ge(s_an, 1)
            e.mul(a_neg[:], a_exp[:], -1.0).then_inc(s_an, 1)
            e.wait_ge(s_an, 2)
            e.preload_act_table_set(LOGEXP)
            run(e, AC_)

        @block.tensor
        def _(e):
            e.wait_ge(s_id, 2)
            e.wait_ge(s_cst, 3)
            run(e, PE_)

        @block.vector
        def _(e):
            e.wait_ge(s_c, 10)
            e.wait_ge(s_w, 16 * NWD)
            for k in range(KD):
                i = e.tensor_scalar(w_in[:, k, :], w_in[:, k, :], w_nm[:, k:k + 1], None, ALU.mult)
            i.then_inc(s_cst, 1)
            e.tensor_copy(iota_e[:], iota_i[:]).then_inc(s_cst, 1)
            e.tensor_copy(base[:], capi[:]).then_inc(s_cst, 1)
            e.wait_ge(s_cst, 3)
            run(e, DV_)
            table(e)



def phase2(nc, sem, Wg, Wu, Wd, x1_d, sh_d, xs_d, ys_d, out_rows, ident, posi, gat, tab):
    with ExitStack() as ctx:
        def sb(name, shape, dt=F32):
            return ctx.enter_context(nc.sbuf_tensor(name, shape, dt))

        def bank(name):
            return ctx.enter_context(nc.psum_tensor(name, [P, 512], F32))

        NF = len(FIT)
        w_g = sb("w_g", [P, E * KD * FI])
        w_u = sb("w_u", [P, E * KD * FI])
        w_d = sb("w_d", [P, E * NF * DM])
        xt = sb("xt", [P, 2, DM])
        xtT = sb("xtT", [P, 2, KD, P])
        sgm = sb("sgm", [P, 2, FI])
        hm = sb("hm", [P, 2, FI])
        hT = sb("hT", [P, 2, NF, P])
        yt = sb("yt", [P, 2, DM])

        bX = bank("bX"); bG = [bank("bG0"), bank("bG1")]; bU = [bank("bU0"), bank("bU1")]
        bHA = bank("bHA"); bHB = bank("bHB"); bD = bank("bD")

        s_wt = sem("s_wt")
        s_in = [sem("s_in0"), sem("s_in1")]
        s_tx = sem("s_tx"); s_kx = sem("s_kx"); s_g = sem("s_g"); s_gu = sem("s_gu"); s_si = sem("s_si"); s_h = sem("s_h")
        s_th = sem("s_th"); s_ka = sem("s_ka"); s_kb = sem("s_kb"); s_dn = sem("s_dn"); s_yt = sem("s_yt"); s_ys = sem("s_ys")
        NB4 = 4

        def after(e, s_, t, back=0, per=1):
            wait(e, s_, per, t.shift(-back), per - 1)

        def arrived(e, t, par):
            v = t.times(8, 16 - 8 * par)
            e.wait_ge(s_in[par], v)

        def tile_in(e, t, par):
            after(e, s_tx, t, 2)
            row = e.value_load(tab[0:1, 1, bass.ds(t.times(1), 1)], min_val=0, max_val=E * CAP - P)
            e.dma_start(xt[:, par, :], xs_d[bass.ds(row, P), :]).then_inc(s_in[par], 16)

        def tile_out(e, t, par):
            after(e, s_yt, t)
            after(e, s_ys, t, 1, 16)
            e.dma_start(ys_d[bass.ds(t.times(P), P), :], yt[:, par, :]).then_inc(s_ys, 16)

        def turn_in(e, t, par):
            arrived(e, t, par)
            after(e, s_kx, t, 1)
            for k in range(KD):
                i = e.transpose(bX[:, k * P:(k + 1) * P], xt[:, par, k * P:(k + 1) * P], ident[:])
            i.then_inc(s_tx, 1)

        def expert(e, t):
            return e.value_load(tab[0:1, 0, bass.ds(t.times(1), 1)], min_val=0, max_val=E - 1)

        def inner(e, ex, par, w, banks, s_):
            for f in range(2):
                for k in range(KD):
                    i = e.matmul(banks[f][:, 0:FH], xtT[:, par, k, :], w[:, bass.ds(ex * (KD * FI) + (k * FI + f * FH), FH)],
                                 start=(k == 0), stop=(k == KD - 1))
            i.then_inc(s_, 1)

        def gate(e, t, par):
            ex = expert(e, t)
            e.wait_ge(s_wt, ex * 64 + 64)
            e.nop(nofuse=True)
            after(e, s_kx, t)
            after(e, s_si, t, 1)
            inner(e, ex, par, w_g, bG, s_g)

        def up(e, t, par):
            ex = expert(e, t)
            after(e, s_h, t, 1)
            inner(e, ex, par, w_u, bU, s_gu)

        def turn_h(e, t, par):
            after(e, s_h, t)
            after(e, s_ka, t, 1)
            after(e, s_kb, t, 1)
            for q, (i0, n) in enumerate(FIT):
                b, o = (bHA, q) if q < NB4 else (bHB, q - NB4)
                i = e.transpose(b[0:n, o * P:(o + 1) * P], hm[:, par, i0:i0 + n], ident[:])
            i.then_inc(s_th, 1)

        def down(e, t, par):
            ex = expert(e, t)
            after(e, s_ka, t)
            after(e, s_kb, t)
            after(e, s_yt, t, 1)
            for q, (i0, n) in enumerate(FIT):
                i = e.matmul(bD[:, 0:DM], hT[0:n, par, q, :], w_d[0:n, bass.ds(ex * (NF * DM) + q * DM, DM)],
                             start=(q == 0), stop=(q == NF - 1))
            i.then_inc(s_dn, 1)

        def act_keep_x(e, t, par):
            after(e, s_tx, t)
            after(e, s_gu, t, 2)
            e.copy(xtT[:, par, :, :].rearrange("p k q -> p (k q)"), bX[:, 0:KD * P]).then_inc(s_kx, 1)

        def act_silu(e, t, par):
            after(e, s_g, t)
            after(e, s_h, t, 2)
            for f in range(2):
                i = e.activation(sgm[:, par, f * FH:(f + 1) * FH], bG[f][:, 0:FH], ACT.Silu)
            i.then_inc(s_si, 1)

        def act_keep_h(e, t, par):
            after(e, s_th, t)
            after(e, s_dn, t, 2)
            e.copy(hT[:, par, 0:NB4, :].rearrange("p k q -> p (k q)"), bHA[:]).then_inc(s_ka, 1)

        def dve_mul(e, t, par):
            after(e, s_si, t)
            after(e, s_gu, t)
            after(e, s_th, t, 2)
            for f in range(2):
                i = e.tensor_tensor(hm[:, par, f * FH:(f + 1) * FH], sgm[:, par, f * FH:(f + 1) * FH], bU[f][:, 0:FH], ALU.mult)
            i.then_inc(s_h, 1)

        def dve_keep_h(e, t, par):
            after(e, s_th, t)
            after(e, s_dn, t, 2)
            for q in range(NB4, NF):
                n = FIT[q][1]
                i = e.tensor_copy(hT[0:n, par, q, :], bHB[0:n, (q - NB4) * P:(q - NB4 + 1) * P])
            i.then_inc(s_kb, 1)

        def dve_keep_y(e, t, par):
            after(e, s_dn, t)
            after(e, s_ys, t, 2, 16)
            e.tensor_copy(yt[:, par, :], bD[:, 0:DM]).then_inc(s_yt, 1)

        def stream(e, work, n, ring, start):
            lags = [lag for _, lag in work]

            def step(t):
                for fn, lag in work:
                    if t.reg is not None or 0 <= t.add - lag < n:
                        fn(e, t.shift(-lag), (t.add - lag) % ring)

            loops = (n + min(lags) - start) // ring
            for t in range(min(lags), start):
                step(Chunk(t))
            with e.Fori(0, loops) as i:
                for k in range(ring):
                    step(Chunk(start + k, i, ring))
            for t in range(start + loops * ring, n + max(lags)):
                step(Chunk(t))

        def tiles(e, work):
            stream(e, work, NT, 2, 3)

        UT = 2
        NU = NTOK // P // UT
        R = 4
        gidx = sb("gidx", [P, R, UT, TOPK], U32)
        gwt = sb("gwt", [P, R, UT, TOPK])
        yg = sb("yg", [P, R, TOPK, UT, DM])
        x1u = sb("x1u", [P, R, UT, DM])
        shu = sb("shu", [P, R, UT, DM])
        ou = sb("ou", [P, R, UT, DM])
        st = sb("st3", [P, UT, 6])
        mv = sb("mv3", [P, R, UT, 2])
        va = sb("va3", [P, R, UT])
        rr = sb("rr3", [P, R, UT])
        tn = sb("tn3", [P, UT])
        nm = sb("nm3", [P, R, UT])
        s_gi = sem("s_gi")
        s_yg = [sem(f"s_yg{b}") for b in range(R)]
        s_xu = [sem(f"s_xu{b}") for b in range(R)]
        s_out = [sem(f"s_out{b}") for b in range(R)]
        s_f1 = sem("s_f1"); s_f2 = sem("s_f2"); s_f3 = sem("s_f3"); s_f4 = sem("s_f4"); s_f5 = sem("s_f5")

        def landed(e, sems, per, u, b):
            v = u.times(per // R, per - per * b // R)
            if isinstance(v, int) and v <= 0:
                return
            e.wait_ge(sems[b], v)
            if not isinstance(v, int) and e.engine in (POOL, SYNC):
                e.nop(nofuse=True)

        def u_gather(e, u, b):
            wait(e, s_f1, 1, u.shift(-R), 0)
            e.tensor_copy(gidx[:, b, :, :], posi[:, bass.ds(u.times(UT), UT), :]).then_inc(s_gi, 1)
            e.tensor_copy(gwt[:, b, :, :], gat[:, bass.ds(u.times(UT), UT), :]).then_inc(s_gi, 1)
            wait(e, s_gi, 2, u, 1)
            for k in range(TOPK):
                for q in range(UT):
                    e.indirect_dma_start(out=yg[:, b, k, q, :], out_offset=None, in_=ys_d,
                                         in_offset=bass.IndirectOffsetOnAxis(ap=gidx[:, b, q, k:k + 1], axis=0)).then_inc(s_yg[b], 16)

        def u_load(e, u, b):
            wait(e, s_f5, 1, u.shift(-R), 0)
            rows = lambda d: d[bass.ds(u.times(UT * P), UT * P), :].rearrange("(j p) d -> p j d", p=P)
            e.dma_start(x1u[:, b, :, :], rows(x1_d)).then_inc(s_xu[b], 16)
            e.dma_start(shu[:, b, :, :], rows(sh_d)).then_inc(s_xu[b], 16)

        def u_store(e, u, b):
            wait(e, s_f5, 1, u, 0)
            rows = out_rows[bass.ds(u.times(UT * P), UT * P), :].rearrange("(j p) d -> p j d", p=P)
            e.dma_start(rows, ou[:, b, :, :]).then_inc(s_out[b], 16)

        def u_sum(e, u, b):
            landed(e, s_xu, 32, u, b)
            wait(e, s_gi, 2, u, 1)
            landed(e, s_yg, 16 * UT * TOPK, u, b)
            for k in range(TOPK):
                for q in range(UT):
                    e.scalar_tensor_tensor(out=shu[:, b, q, :], in0=yg[:, b, k, q, :], scalar=gwt[:, b, q, k:k + 1],
                                           in1=shu[:, b, q, :], op0=ALU.mult, op1=ALU.add)
                e.drain()
            for q in range(UT):
                e.bn_stats(st[:, q, :], shu[:, b, q, :])
            e.drain()
            for q in range(UT):
                e.bn_aggr(mv[:, b, q, :], st[:, q, :])
            e.drain()
            e.tensor_scalar(va[:, b, :], mv[:, b, :, 1], EPS_LN, None, ALU.add).then_inc(s_f1, 1)

        def u_root(e, u, b):
            wait(e, s_f1, 1, u, 0)
            e.activation(rr[:, b, :], va[:, b, :], ACT.Ln)
            e.drain()
            e.activation(rr[:, b, :], rr[:, b, :], ACT.Exp, scale=-0.5).then_inc(s_f2, 1)

        def u_newton(e, u, b):
            wait(e, s_f2, 1, u, 0)
            r = rr[:, b, :]
            for ins in (lambda: e.tensor_tensor(tn[:], r, r, ALU.mult),
                        lambda: e.tensor_tensor(tn[:], tn[:], va[:, b, :], ALU.mult),
                        lambda: e.tensor_scalar(tn[:], tn[:], -0.5, 1.5, ALU.mult, ALU.add),
                        lambda: e.tensor_tensor(r, r, tn[:], ALU.mult)):
                ins()
                e.drain()
            e.scalar_tensor_tensor(out=nm[:, b, :], in0=mv[:, b, :, 0], scalar=-1.0, in1=r, op0=ALU.mult, op1=ALU.mult).then_inc(s_f3, 1)

        def u_norm(e, u, b):
            wait(e, s_f3, 1, u, 0)
            landed(e, s_out, 16, u.shift(-R), b)
            for q in range(UT):
                i = e.activation(ou[:, b, q, :], shu[:, b, q, :], ACT.Identity, scale=rr[:, b, q:q + 1], bias=nm[:, b, q:q + 1])
            i.then_inc(s_f4, 1)

        def u_add(e, u, b):
            wait(e, s_f4, 1, u, 0)
            e.tensor_tensor(ou[:, b, :, :].rearrange("p j d -> p (j d)"), x1u[:, b, :, :].rearrange("p j d -> p (j d)"),
                            ou[:, b, :, :].rearrange("p j d -> p (j d)"), ALU.add).then_inc(s_f5, 1)

        block = ctx.enter_context(nc.Block())

        @block.sync
        def _(e):
            for x_ in range(E):
                n = NF - 1
                o = x_ * KD * FI
                e.dma_start(w_g[:, o:o + KD * FI].rearrange("p (k n) -> p k n", k=KD), Wg[x_].rearrange("(k p) n -> p k n", p=P)).then_inc(s_wt, 16)
                e.dma_start(w_u[:, o:o + KD * FI].rearrange("p (k n) -> p k n", k=KD), Wu[x_].rearrange("(k p) n -> p k n", p=P)).then_inc(s_wt, 16)
                o = x_ * NF * DM
                e.dma_start(w_d[:, o:o + n * DM].rearrange("p (k n) -> p k n", k=n), Wd[x_][0:n * P, :].rearrange("(k p) n -> p k n", p=P)).then_inc(s_wt, 16)
                e.dma_start(w_d[0:FI - n * P, o + n * DM:o + NF * DM], Wd[x_][n * P:FI, :]).then_inc(s_wt, 16)
                e.wait_ge(s_wt, 64 * (x_ + 1))
            stream(e, [(u_store, 0), (u_load, -R)], NU, R, 0)
            for b in range(R):
                e.wait_ge(s_out[b], 16 * NU // R)

        @block.gpsimd
        def _(e):
            tiles(e, [(tile_in, -1), (tile_out, 1)])
            e.wait_ge(s_ys, 16 * NT)
            stream(e, [(u_gather, 0)], NU, R, R)

        @block.tensor
        def _(e):
            tiles(e, [(gate, 0), (turn_h, 1), (up, 0), (turn_in, -1), (down, 1)])

        @block.scalar
        def _(e):
            tiles(e, [(act_silu, 0), (act_keep_h, 1), (act_keep_x, -1)])
            e.preload_act_table_set(LOGEXP)
            stream(e, [(u_root, 0), (u_norm, 1)], NU, R, R + 1)

        @block.vector
        def _(e):
            tiles(e, [(dve_keep_h, 1), (dve_mul, 0), (dve_keep_y, 1)])
            stream(e, [(u_sum, 0), (u_newton, 1), (u_add, 2)], NU, R, 2)


_INS = ["L0_attn_x", "L0_attn_norm_w", "L0_attn_in_proj_w", "L0_attn_conv_w", "L0_attn_dt_w", "L0_attn_dt_b",
        "L0_attn_A_log", "L0_attn_B_w", "L0_attn_C_w", "L0_attn_D_skip", "L0_attn_out_proj_w",
        "L0_ffn_gate_w", "L0_ffn_Wg", "L0_ffn_Wu", "L0_ffn_Wd", "L0_ffn_Sg", "L0_ffn_Su", "L0_ffn_Sd"]


def kernel(**inputs):
    import numpy as _np
    import concourse.bacc as _bacc
    from concourse import mybir as _mybir
    from concourse.bass_utils import run_bass_kernel_spmd as _run

    nc = _bacc.Bacc("TRN2", target_bir_lowering=False, num_devices=1)
    arrays, args = {}, []
    for name in _INS:
        a = _np.ascontiguousarray(inputs[name])
        arrays[f"in_{name}_dram"] = a
        args.append(nc.dram_tensor(f"in_{name}_dram", a.shape, _mybir.dt.from_np(a.dtype), kind="ExternalInput").ap())
    args.append(nc.dram_tensor("out_0_dram", inputs["L0_attn_x"].shape, _mybir.dt.float32, kind="ExternalOutput").ap())
    build(nc, *args)
    r = _run(nc, [arrays], core_ids=[0])
    return r.results[0]["out_0_dram"]
```

```python
from collections import defaultdict
from contextlib import ExitStack

import numpy as np
import concourse.bass as bass
from concourse import mybir

F32 = mybir.dt.float32
I32 = mybir.dt.int32
U32 = mybir.dt.uint32
ALU = mybir.AluOpType
ACT = mybir.ActivationFunctionType
AX = mybir.AxisListType
POOL = mybir.EngineType.Pool
SYNC = mybir.EngineType.SP

P = 128
DM = 256
DI = 512
NS = 16
TAPS = 4
E = 8
TOPK = 2
FI = 704
SI = 352
NTOK = 4096
CH = 512
NCH = NTOK // CH
J = CH // P
KD = DM // P
ND = DI // P
SLOTS = NS * ND
CAP = NTOK + P
NT = NTOK * TOPK // P + E - 1
EPS_LN = 1e-5
EPS_RMS = 1e-6
SIT = [(t * P, min(P, SI - t * P)) for t in range((SI + P - 1) // P)]
FIT = [(t * P, min(P, FI - t * P)) for t in range((FI + P - 1) // P)]
FH = FI // 2
USES = {"A0": ("xnT0", "gate0", "gate2", "inner0", "cv0", "inner2", "cv2", "bT", "bc", "dt1", "dt3"),
        "A1": ("xnT1", "gate1", "gate3", "inner1", "cv1", "inner3", "cv3", "dt0", "dt2"),
        "A2": ("y0", "y2", "out0", "xfT0", "logit", "sg0", "sg2", "su1", "sd0"),
        "A3": ("y1", "y3", "out1", "xfT1", "rank", "sg1", "su0", "su2", "sd1")}
USE = {name: (b, k) for b, names in USES.items() for k, name in enumerate(names)}


PLAN = dict(
    stats=[0, 0, 1], root=0, newton=[3, 3, 4, 5, 6], norm=8, xT=[10, 12], xT_keep=[15, 15],
    gate=[16, 18, 20, 22], gate_keep=[18, 21, 22, 24], silu=24,
    inner=[23, 25, 30, 32], head=[22, 23, 31, 31], mul=[26, 27, 32, 34], conv=[27, 28, 33, 35], conv_keep=[29, 31, 36, 38],
    bT=39, bT_keep=44, bT_store=48, bc=45, bc_keep=44,
    dt=[42, 46, 49, 52], dt_act=[46, 51, 53, 56], dt_exp=[46, 51, 53, 56], dt_ln=[47, 51, 54, 57], dt_sum=[48, 52, 55, 58], dt_mul=[49, 52, 58, 59],
    y=[4, 4, 5, 6], y_keep=[4, 4, 5, 5], out=[7, 12], o_stats=[14, 15, 16], o_root=16, o_newton=[16, 18, 19, 20, 22], o_norm=23, x1=23, x1_store=31,
    l_stats=[25, 26, 27], l_root=25, l_newton=[27, 28, 29, 30, 31], l_norm=33, fT=[37, 38], fT_keep=[39, 39],
    logit=43, route=[46, 48, 49, 49, 50], rank=51, e2=52, place=[51, 52, 54, 54], scatter=[55, 59, 61, 61],
    sg=[47, 53, 55], sg_keep=[51, 55, 57], sh_silu=57, su=[56, 58, 58], sh_mul=[57, 59, 59],
    sd=[63, 63], sd_keep=[62, 62], sh_store=63,
    step=1, ahead_act=3, ahead_pool=3)
LOGEXP = "natural_log_exp_and_others"


class Chunk:

    def __init__(self, add, reg=None, stride=2):
        self.add, self.reg, self.stride = add, reg, stride

    def shift(self, by):
        return Chunk(self.add + by, self.reg, self.stride)

    def times(self, n, plus=0):
        if self.reg is None:
            return self.add * n + plus
        return self.reg * (self.stride * n) + (self.add * n + plus)


def wait(eng, sem, per, c, k):
    v = c.times(per, k + 1)
    if isinstance(v, int) and v <= 0:
        return
    eng.wait_ge(sem, v)
    if not isinstance(v, int) and eng.engine in (POOL, SYNC):
        eng.nop(nofuse=True)


def then(eng, ins):
    eng.drain()


def build(nc, x, norm_w, in_proj_w, conv_w, dt_w, dt_b, A_log, B_w, C_w, D_skip, out_proj_w,
          gate_w, Wg, Wu, Wd, Sg, Su, Sd, out):
    x_rows = x.rearrange("b t d -> (b t) d")
    out_rows = out.rearrange("b t d -> (b t) d")

    x1_d = nc.dram_tensor("x1_scratch", (NTOK, DM), F32).ap()
    sh_d = nc.dram_tensor("shared_scratch", (NTOK, DM), F32).ap()
    xs_d = nc.dram_tensor("expert_in_scratch", (E * CAP, DM), F32).ap()
    b_d = nc.dram_tensor("b_scratch", (NCH * NS, CH), F32).ap()
    ys_d = nc.dram_tensor("expert_out_scratch", (NT * P, DM), F32).ap()

    with ExitStack() as top:
        def sem(name):
            return top.enter_context(nc.semaphore(name))

        def sbp(name, shape, dt=F32):
            return top.enter_context(nc.sbuf_tensor(name, shape, dt))

        ident = sbp("ident", [P, P])
        base = sbp("base", [P, E])
        posi = sbp("posi", [P, NTOK // P, TOPK], U32)
        posa = sbp("posa", [P, NTOK // P, TOPK])
        expa = sbp("expa", [P, NTOK // P, TOPK])
        gat = sbp("gat", [P, NTOK // P, TOPK])
        padi = sbp("padi", [P, E], U32)
        iota_e = sbp("iota_e", [P, E])
        off = sbp("off", [P, E])
        tab = sbp("tab", [1, 2, NT + 1], I32)

        phase1(nc, sem, x_rows, norm_w, in_proj_w, conv_w, dt_w, dt_b, A_log, B_w, C_w, D_skip,
               out_proj_w, gate_w, Sg, Su, Sd, b_d, x1_d, sh_d, xs_d, ident, base, posi, posa, expa, gat, padi, iota_e, off, tab)
        phase2(nc, sem, Wg, Wu, Wd, x1_d, sh_d, xs_d, ys_d, out_rows, ident, iota_e, off, posa, expa, posi, gat, tab)


def phase1(nc, sem, x_rows, norm_w, in_proj_w, conv_w, dt_w, dt_b, A_log, B_w, C_w, D_skip,
           out_proj_w, gate_w, Sg, Su, Sd, b_d, x1_d, sh_d, xs_d, ident, base, posi, posa, expa, gat, padi, iota_e, off, tab):
    with ExitStack() as ctx:
        def sb(name, shape, dt=F32):
            return ctx.enter_context(nc.sbuf_tensor(name, shape, dt))

        def bank(name):
            return ctx.enter_context(nc.psum_tensor(name, [P, 512], F32))

        w_in = sb("w_in", [P, KD, 2 * DI])
        w_dt = sb("w_dt", [P, ND, DI])
        w_bc = sb("w_bc", [P, ND, 2 * NS])
        w_out = sb("w_out", [P, ND, DM])
        w_cv = sb("w_cv", [P, ND, TAPS])
        w_nm = sb("w_nm", [P, KD])
        w_tap = sb("w_tap", [P, ND, TAPS, P])
        b_dt = sb("b_dt", [P, ND])
        a_log = sb("a_log", [P, ND, NS])
        a_exp = sb("a_exp", [P, ND, NS])
        a_neg = sb("a_neg", [P, ND, NS])
        dskip = sb("dskip", [P, ND])
        w_gt = sb("w_gt", [P, KD, E])
        w_sg = sb("w_sg", [P, KD, SI])
        w_su = sb("w_su", [P, KD, SI])
        w_sd = sb("w_sd", [P, len(SIT), DM])
        ones = sb("ones", [P, P])
        below = sb("below", [P, P])
        iota_i = sb("iota_i", [P, E], I32)
        capi = sb("capi", [P, E], I32)
        xp = sb("xp", [P, J, DM])
        st = sb("st", [P, J, 6])
        mv = sb("mv", [P, J, 2])
        va = sb("va", [P, J])
        r0 = sb("r0", [P, J])
        tn = sb("tn", [P, J])
        nmr = sb("nmr", [P, J])
        xn = sb("xn", [P, J, DM])
        xnT = sb("xnT", [P, KD, CH])
        sg = sb("sg", [P, ND, CH])
        xin = sb("xin", [P, ND, TAPS - 1 + CH])
        xc = [sb(f"xc{i}", [P, ND, CH]) for i in range(2)]
        dt = [sb(f"dt{i}", [P, ND, CH]) for i in range(2)]
        u = [sb(f"u{i}", [P, ND, CH]) for i in range(2)]
        bT = sb("bT", [2 * NS, CH])
        bc = [sb(f"bc{i}", [P, J, 2 * NS]) for i in range(2)]
        NR, NB = 4, 4
        br = sb("br", [P, NR, CH])
        bb = sb("bb", [P, NB, CH])
        hh = sb("hh", [P, 2, ND, CH])
        hl = sb("hl", [P, NS, ND])
        yT = [sb(f"yT{i}", [P, J, DI]) for i in range(2)]
        xr = sb("xr", [P, J, DM])
        st2 = sb("st2", [P, J, 6])
        mv2 = sb("mv2", [P, J, 2])
        va2 = sb("va2", [P, J])
        r2 = sb("r2", [P, J])
        tn2 = sb("tn2", [P, J])
        nmr2 = sb("nmr2", [P, J])
        on = sb("on", [P, J, DM])
        xf = sb("xf", [P, J, DM])
        xfT = sb("xfT", [P, KD, CH])
        lg = sb("lg", [P, J, E])
        mx = sb("mx", [P, J, E])
        ix = sb("ix", [P, J, E], U32)
        ixf = sb("ixf", [P, J, TOPK])
        oh = sb("oh", [P, TOPK, J, E])
        mm_ = sb("mm_", [P, J + 1, E])
        dif = sb("dif", [P, J])
        e2 = sb("e2", [P, J])
        e2p = sb("e2p", [P, J])
        p1 = sb("p1", [P, J])
        pos8 = sb("pos8", [P, J, E])
        prd = sb("prd", [P, TOPK, J, E])
        posf = sb("posf", [P, J, TOPK])
        posl = sb("posl", [P, J, TOPK], U32)
        sgs = sb("sgs", [P, len(SIT), CH])
        sh = on
        cnt = sb("cnt", [P, E])
        cnti = sb("cnti", [P, E], I32)
        nti = sb("nti", [P, E], I32)
        ntf = sb("ntf", [P, E])
        one8 = sb("one8", [P, E])
        cum = sb("cum", [P, E])
        tot = sb("tot", [1, 1])
        capf = sb("capf", [P, E])
        tii = sb("tii", [1, NT + 1], I32)
        tif = sb("tif", [1, NT + 1])
        ge = sb("ge", [1, NT + 1, E - 1])
        gn = sb("gn", [1, NT + 1, E - 1])
        te = sb("te", [1, NT + 1])
        tp = sb("tp", [1, NT + 1])
        iop = sb("iop", [P, 1], I32)
        iopf = sb("iopf", [P, 1])
        padf = sb("padf", [P, E])
        zro = sb("zro", [P, DM])

        NA = 4
        bA = [sb(f"bA{i}", [P, CH]) for i in range(NA)]
        bH = [bank(f"bH{i}") for i in range(ND)]
        A = {n: bank(n) for n in ("A0", "A1", "A2", "A3")}
        full = {n: sem(f"full_{n}") for n in A}
        free = {n: sem(f"free_{n}") for n in A}

        s_w = sem("s_w"); s_w2 = sem("s_w2"); s_c = sem("s_c"); s_id = sem("s_id"); s_cst = sem("s_cst"); s_an = sem("s_an")
        s_x = sem("s_x"); s_p0v = sem("s_p0v"); s_p0r = sem("s_p0r"); s_p0n = sem("s_p0n"); s_xn = sem("s_xn")
        s_ln = sem("s_ln"); s_sil = sem("s_sil"); s_ssil = sem("s_ssil"); s_dt = sem("s_dt"); s_u = sem("s_u")
        s_bb = sem("s_bb"); s_bs = sem("s_bs"); s_bl = [sem(f"s_bl{i}") for i in range(NR)]; s_a = sem("s_a"); s_scan = sem("s_scan")
        s_ht = sem("s_ht"); s_y = sem("s_y"); s_hl = sem("s_hl")
        s_xr = sem("s_xr"); s_o1 = sem("s_o1"); s_o2 = sem("s_o2"); s_o3 = sem("s_o3"); s_x1 = sem("s_x1")
        s_l1 = sem("s_l1"); s_l2 = sem("s_l2"); s_l3 = sem("s_l3"); s_xf = sem("s_xf"); s_x1s = sem("s_x1s")
        s_hd = sem("s_hd"); s_ex = sem("s_ex")
        s_cx = sem("s_cx"); s_nx = sem("s_nx"); s_co = sem("s_co"); s_no = sem("s_no"); s_cl = sem("s_cl"); s_nl = sem("s_nl")
        s_cr = sem("s_cr"); s_cp = sem("s_cp")
        s_m = sem("s_m"); s_e2 = sem("s_e2"); s_pos = sem("s_pos"); s_sc = sem("s_sc"); s_scd = sem("s_scd"); s_shs = sem("s_shs")
        s_pad = sem("s_pad"); s_padd = sem("s_padd")

        SP_, PE_, AC_, DV_, PO_ = "sync", "tensor", "scalar", "vector", "gpsimd"

        def bank_of(name):
            return A[USE[name][0]]

        def room(eng, name, c):
            b, k = USE[name]
            wait(eng, free[b], len(USES[b]), c, k)

        def filled(eng, name, c):
            b, k = USE[name]
            wait(eng, full[b], len(USES[b]), c, k)

        def emptied(eng, name, c):
            b, k = USE[name]
            wait(eng, free[b], len(USES[b]), c, k + 1)

        def all_emptied(eng, names, c):
            for name in {USE[n][0]: n for n in names}.values():
                emptied(eng, name, c)

        def fills(ins, name):
            ins.then_inc(full[USE[name][0]], 1)

        def empties(ins, name):
            ins.then_inc(free[USE[name][0]], 1)

        def chain(add, c, slots, s_, steps):
            n = len(steps) - 1
            for k, step in enumerate(steps):
                def f(e, k=k, step=step):
                    if k:
                        wait(e, s_, n, c, k - 1)
                        e.nop(nofuse=True)
                    i = step(e)
                    if k < n:
                        i.then_inc(s_, 1)
                add(slots[k], DV_, f)

        def mean_steps(ready, rows, st_, m, v, scale, shift, between, s_v):
            def parts(e):
                for j in range(J):
                    ready(e, j)
                    i = e.bn_stats(st_[:, j, :], rows(j))
                return i

            def join(e):
                between(e)
                for j in range(J):
                    i = e.bn_aggr(m[:, j, :], st_[:, j, :])
                return i

            def var(e):
                e.tensor_scalar(v[:], m[:, :, 1], scale, shift, ALU.mult, ALU.add).then_inc(s_v, 1)
            return [parts, join, var]

        def root_steps(ready, m, v, r, t, nm, s_f):
            def square(e):
                ready(e)
                return e.tensor_tensor(t[:], r[:], r[:], ALU.mult)

            def nmr_(e):
                e.scalar_tensor_tensor(out=nm[:], in0=m[:, :, 0], scalar=-1.0, in1=r[:], op0=ALU.mult, op1=ALU.mult).then_inc(s_f, 1)
            return [square,
                    lambda e: e.tensor_tensor(t[:], t[:], v[:], ALU.mult),
                    lambda e: e.tensor_scalar(t[:], t[:], -0.5, 1.5, ALU.mult, ALU.add),
                    lambda e: e.tensor_tensor(r[:], r[:], t[:], ALU.mult),
                    nmr_]

        def already(e):
            pass

        def pre(c, par):
            s = defaultdict(list)

            def add(slot, eng, fn):
                s[(min(slot, SLOTS - 1), eng)].append(fn)

            def load_x(e):
                wait(e, s_xn, J, c.shift(-1), J - 1)
                e.dma_start(xp[:], x_rows[bass.ds(c.times(CH), CH), :].rearrange("(j p) d -> p j d", p=P)).then_inc(s_x, 16)
            add(0, SP_, load_x)

            def x_ready(e, j):
                if j == 0:
                    wait(e, s_x, 16, c, 15)

            chain(add, c, PLAN["stats"], s_cx, mean_steps(x_ready, lambda j: xp[:, j, :], st, mv, va, 1.0 + EPS_RMS, EPS_LN * EPS_RMS,
                                                          lambda e: None, s_p0v))

            def root(e):
                wait(e, s_p0v, 1, c, 0)
                wait(e, s_xn, J, c.shift(-1), J - 1)
                then(e, e.activation(r0[:], va[:], ACT.Ln))
                e.activation(r0[:], r0[:], ACT.Exp, scale=-0.5).then_inc(s_p0r, 1)
            add(PLAN["root"], AC_, root)

            chain(add, c, PLAN["newton"], s_nx, root_steps(lambda e: wait(e, s_p0r, 1, c, 0), mv, va, r0, tn, nmr, s_p0n))

            def norm(e):
                wait(e, s_p0n, 1, c, 0)
                filled(e, "xnT1", c.shift(-1))
                for j in range(J):
                    e.activation(xn[:, j, :], xp[:, j, :], ACT.Identity, scale=r0[:, j:j + 1], bias=nmr[:, j:j + 1]).then_inc(s_xn, 1)
            add(PLAN["norm"], AC_, norm)

            def turn_x(k):
                def f(e):
                    b = f"xnT{k}"
                    wait(e, s_xn, J, c, J - 1)
                    room(e, b, c)
                    for j in range(J):
                        i = e.transpose(bank_of(b)[:, j * P:(j + 1) * P], xn[:, j, k * P:(k + 1) * P], ident[:])
                    fills(i, b)
                return f

            def keep_x(k):
                def f(e):
                    b = f"xnT{k}"
                    filled(e, b, c)
                    empties(e.copy(xnT[:, k, :], bank_of(b)[:]), b)
                return f
            for k in range(KD):
                add(PLAN["xT"][k], PE_, turn_x(k))
                add(PLAN["xT_keep"][k], AC_, keep_x(k))

            def product(slot, step, b, parts, ready):
                n = len(parts)
                for q, part in enumerate(parts):
                    def f(e, q=q, part=part):
                        if q == 0:
                            room(e, b, c)
                            ready(e)
                        i = part(e)
                        if q == n - 1:
                            fills(i, b)
                    add(slot + int(q * step), PE_, f)

            def x_kept(e):
                emptied(e, "xnT0", c)
                emptied(e, "xnT1", c)

            def p1_parts(b, off, d):
                return [lambda e, k=k: e.matmul(bank_of(b)[:], w_in[:, k, off + d * P:off + (d + 1) * P], xnT[:, k, :],
                                                start=(k == 0), stop=(k == KD - 1)) for k in range(KD)]

            def gate_act(d):
                def f(e):
                    filled(e, f"gate{d}", c)
                    if d == 0:
                        emptied(e, f"inner{ND - 1}", c.shift(-1))
                    empties(e.copy(sg[:, d, :], bank_of(f"gate{d}")[:]), f"gate{d}")
                return f

            def silu_act(e):
                all_emptied(e, [f"gate{d}" for d in range(ND)], c)
                e.activation(sg[:].rearrange("p d t -> p (d t)"), sg[:].rearrange("p d t -> p (d t)"), ACT.Silu).then_inc(s_sil, 1)
                e.preload_act_table_set(LOGEXP)

            def head(d):
                def f(e):
                    filled(e, f"cv{d}", c.shift(-1))
                    if par:
                        e.tensor_copy(xin[:, d, 0:TAPS - 1], xin[:, d, CH:CH + TAPS - 1]).then_inc(s_hd, 1)
                    else:
                        e.memset(xin[:, d, 0:TAPS - 1], 0.0).then_inc(s_hd, 1)
                return f

            def p1_dve(d):
                def f(e):
                    wait(e, s_hd, ND, c, d)
                    wait(e, s_sil, 1, c, 0)
                    filled(e, f"inner{d}", c)
                    empties(e.tensor_tensor(xin[:, d, TAPS - 1:], sg[:, d, :], bank_of(f"inner{d}")[:], ALU.mult), f"inner{d}")
                return f

            def conv_parts(d):
                return [lambda e, k=k: e.matmul(bank_of(f"cv{d}")[:], w_tap[:, d, k, :], xin[:, d, k:k + CH],
                                                start=(k == 0), stop=(k == TAPS - 1)) for k in range(TAPS)]

            def gated(d):
                def f(e):
                    wait(e, s_hd, ND, c, d)
                    emptied(e, f"inner{d}", c)
                return f

            def conv_keep(d):
                def f(e):
                    filled(e, f"cv{d}", c)
                    filled(e, "out1", c.shift(-2))
                    empties(e.copy(xc[par][:, d, :], bank_of(f"cv{d}")[:]), f"cv{d}")
                return f
            for d in range(ND):
                product(PLAN["gate"][d], PLAN["step"], f"gate{d}", p1_parts(f"gate{d}", DI, d), x_kept if d == 0 else already)
                add(PLAN["gate_keep"][d], AC_, gate_act(d))
                product(PLAN["inner"][d], PLAN["step"], f"inner{d}", p1_parts(f"inner{d}", 0, d), already)
                add(PLAN["head"][d], DV_, head(d))
                add(PLAN["mul"][d], DV_, p1_dve(d))
                product(PLAN["conv"][d], PLAN["step"], f"cv{d}", conv_parts(d), gated(d))
                add(PLAN["conv_keep"][d], AC_, conv_keep(d))
            add(PLAN["silu"], AC_, silu_act)

            def conv_done(e):
                all_emptied(e, [f"cv{d}" for d in range(ND)], c)

            bT_parts = [lambda e, k=k: e.matmul(bank_of("bT")[0:2 * NS, :], w_bc[:, k, :], xc[par][:, k, :],
                                                start=(k == 0), stop=(k == ND - 1)) for k in range(ND)]
            product(PLAN["bT"], PLAN["step"], "bT", bT_parts, conv_done)

            def bT_act(e):
                filled(e, "bT", c)
                wait(e, s_bs, 16, c.shift(-1), 15)
                empties(e.copy(bT[:], bank_of("bT")[0:2 * NS, :]), "bT")
            add(PLAN["bT_keep"], AC_, bT_act)

            def bT_store(e):
                emptied(e, "bT", c)
                e.dma_start(b_d[bass.ds(c.times(NS), NS), :], bT[0:NS, :]).then_inc(s_bs, 16)
            add(PLAN["bT_store"], SP_, bT_store)

            def bc_pe(e):
                room(e, "bc", c)
                e.nop(nofuse=True)
                for j in range(J):
                    i = e.transpose(bank_of("bc")[:, j * 2 * NS:(j + 1) * 2 * NS], bT[:, j * P:(j + 1) * P], ident[0:2 * NS, 0:2 * NS])
                fills(i, "bc")
            add(PLAN["bc"], PE_, bc_pe)

            def bc_act(e):
                filled(e, "bc", c)
                wait(e, s_y, SLOTS, c.shift(-2), SLOTS - 1)
                empties(e.copy(bc[par][:].rearrange("p j s -> p (j s)"), bank_of("bc")[:, 0:J * 2 * NS]), "bc")
            add(PLAN["bc_keep"], AC_, bc_act)

            def dt_parts(m):
                return [lambda e, k=k: e.matmul(bank_of(f"dt{m}")[:], w_dt[:, k, m * P:(m + 1) * P], xc[par][:, k, :],
                                                start=(k == 0), stop=(k == ND - 1)) for k in range(ND)]

            def dt_act(m):
                def f(e):
                    if m == 0:
                        wait(e, s_bb, SLOTS, c.shift(-2), SLOTS - 1)
                    filled(e, f"dt{m}", c)
                    e.activation(u[par][:, m, :], bank_of(f"dt{m}")[:], ACT.Relu, bias=b_dt[:, m:m + 1])
                    empties(e.activation(dt[par][:, m, :], bank_of(f"dt{m}")[:], ACT.Abs, bias=b_dt[:, m:m + 1]), f"dt{m}")
                return f

            def dt_exp(m):
                def f(e):
                    emptied(e, f"dt{m}", c)
                    e.activation(dt[par][:, m, :], dt[par][:, m, :], ACT.Exp, scale=-1.0).then_inc(s_ex, 1)
                return f

            def dt_ln(m):
                def f(e):
                    wait(e, s_ex, ND, c, m)
                    e.activation(dt[par][:, m, :], dt[par][:, m, :], ACT.Ln, bias=1.0).then_inc(s_ln, 1)
                return f

            def dt_sum(m):
                def f(e):
                    wait(e, s_ln, ND, c, m)
                    e.tensor_tensor(dt[par][:, m, :], dt[par][:, m, :], u[par][:, m, :], ALU.add).then_inc(s_dt, 1)
                return f

            def dt_mul(m):
                def f(e):
                    wait(e, s_dt, ND, c, m)
                    emptied(e, f"cv{m}", c)
                    e.tensor_tensor(u[par][:, m, :], dt[par][:, m, :], xc[par][:, m, :], ALU.mult).then_inc(s_u, 1)
                return f

            for m in range(ND):
                product(PLAN["dt"][m], PLAN["step"], f"dt{m}", dt_parts(m), conv_done if m == 0 else already)
                add(PLAN["dt_act"][m], AC_, dt_act(m))
                add(PLAN["dt_exp"][m], AC_, dt_exp(m))
                add(PLAN["dt_ln"][m], AC_, dt_ln(m))
                add(PLAN["dt_sum"][m], PO_, dt_sum(m))
                add(PLAN["dt_mul"][m], PO_, dt_mul(m))

            return s

        def post(c, par):
            s = defaultdict(list)

            def add(slot, eng, fn):
                s[(min(slot, SLOTS - 1), eng)].append(fn)

            def load_r(e):
                e.dma_start(xr[:], x_rows[bass.ds(c.times(CH), CH), :].rearrange("(j p) d -> p j d", p=P)).then_inc(s_xr, 16)
            add(1, SP_, load_r)

            def product(slot, step, b, parts, ready):
                n = len(parts)
                for q, part in enumerate(parts):
                    def f(e, q=q, part=part):
                        if q == 0:
                            room(e, b, c)
                            ready(e)
                        i = part(e)
                        if q == n - 1:
                            fills(i, b)
                    add(slot + int(q * step), PE_, f)

            def yb_pe(d):
                def f(e):
                    b = f"y{d}"
                    wait(e, s_y, SLOTS, c, SLOTS - 1)
                    room(e, b, c)
                    for j in range(J):
                        i = e.transpose(bank_of(b)[:, j * P:(j + 1) * P], yT[par][:, j, d * P:(d + 1) * P], ident[:])
                    fills(i, b)
                return f

            def yb_dve(d):
                def f(e):
                    b = f"y{d}"
                    filled(e, b, c)
                    empties(e.scalar_tensor_tensor(out=xc[par][:, d, :], in0=xc[par][:, d, :], scalar=dskip[:, d:d + 1], in1=bank_of(b)[:],
                                                   op0=ALU.mult, op1=ALU.add), b)
                return f
            for d in range(ND):
                add(PLAN["y"][d], PE_, yb_pe(d))
                add(PLAN["y_keep"][d], DV_, yb_dve(d))

            def y_ready(e):
                all_emptied(e, [f"y{d}" for d in range(ND)], c)

            def out_parts(q):
                return [lambda e, j=j, k=k: e.matmul(bank_of(f"out{q}")[:, (j % 2) * DM:(j % 2 + 1) * DM], xc[par][:, k, j * P:(j + 1) * P],
                                                     w_out[:, k, :], start=(k == 0), stop=(k == ND - 1))
                        for j in (2 * q, 2 * q + 1) for k in range(ND)]
            product(PLAN["out"][0], PLAN["step"] / 2, "out0", out_parts(0), y_ready)
            product(PLAN["out"][1], PLAN["step"] / 2, "out1", out_parts(1), already)

            chain(add, c, PLAN["o_stats"], s_co,
                  mean_steps(lambda e, j: filled(e, f"out{j // 2}", c) if j % 2 == 0 else None,
                             lambda j: bank_of(f"out{j // 2}")[:, (j % 2) * DM:(j % 2 + 1) * DM], st2, mv2, va2, 1.0, EPS_LN,
                             lambda e: None, s_o1))

            def o_root(e):
                wait(e, s_o1, 1, c, 0)
                then(e, e.activation(r2[:], va2[:], ACT.Ln))
                e.activation(r2[:], r2[:], ACT.Exp, scale=-0.5).then_inc(s_o2, 1)
            add(PLAN["o_root"], AC_, o_root)

            chain(add, c, PLAN["o_newton"], s_no, root_steps(lambda e: wait(e, s_o2, 1, c, 0), mv2, va2, r2, tn2, nmr2, s_o3))

            def o_norm(e):
                wait(e, s_o3, 1, c, 0)
                wait(e, s_shs, 16, c.shift(-1), 16)
                for j in range(J):
                    b = f"out{j // 2}"
                    i = e.activation(on[:, j, :], bank_of(b)[:, (j % 2) * DM:(j % 2 + 1) * DM], ACT.Identity,
                                     scale=r2[:, j:j + 1], bias=nmr2[:, j:j + 1])
                    if j % 2:
                        empties(i, b)
            add(PLAN["o_norm"], AC_, o_norm)

            def x1_pool(e):
                emptied(e, "out0", c)
                emptied(e, "out1", c)
                wait(e, s_xr, 16, c, 15)
                e.tensor_tensor(xr[:].rearrange("p j d -> p (j d)"), xr[:].rearrange("p j d -> p (j d)"),
                                on[:].rearrange("p j d -> p (j d)"), ALU.add).then_inc(s_x1, 1)
            add(PLAN["x1"], PO_, x1_pool)

            def x1_store(e):
                wait(e, s_x1, 1, c, 0)
                e.dma_start(x1_d[bass.ds(c.times(CH), CH), :].rearrange("(j p) d -> p j d", p=P), xr[:]).then_inc(s_x1s, 16)
            add(PLAN["x1_store"], SP_, x1_store)

            chain(add, c, PLAN["l_stats"], s_cl,
                  mean_steps(lambda e, j: wait(e, s_x1, 1, c, 0) if j == 0 else None,
                             lambda j: xr[:, j, :], st2, mv2, va2, 1.0, EPS_LN,
                             lambda e: (emptied(e, "out1", c), e.nop(nofuse=True)),
                             s_l1))

            def l_root(e):
                wait(e, s_l1, 1, c, 0)
                then(e, e.activation(r2[:], va2[:], ACT.Ln))
                e.activation(r2[:], r2[:], ACT.Exp, scale=-0.5).then_inc(s_l2, 1)
            add(PLAN["l_root"], AC_, l_root)

            chain(add, c, PLAN["l_newton"], s_nl, root_steps(lambda e: wait(e, s_l2, 1, c, 0), mv2, va2, r2, tn2, nmr2, s_l3))

            def scattered(e):
                wait(e, s_scd, 1, c.shift(-1), 1)

            def scatter_done(e):
                wait(e, s_sc, 16 * J * TOPK, c, 16 * J * TOPK - 1)
                e.nop(nofuse=True).then_inc(s_scd, 1)
            add(SLOTS - 1, PO_, scatter_done)

            def l_norm(e):
                scattered(e)
                wait(e, s_l3, 1, c, 0)
                for j in range(J):
                    e.activation(xf[:, j, :], xr[:, j, :], ACT.Identity, scale=r2[:, j:j + 1], bias=nmr2[:, j:j + 1]).then_inc(s_xf, 1)
            add(PLAN["l_norm"], AC_, l_norm)

            def turn_f(k):
                def f(e):
                    b = f"xfT{k}"
                    wait(e, s_xf, J, c, J - 1)
                    room(e, b, c)
                    for j in range(J):
                        i = e.transpose(bank_of(b)[:, j * P:(j + 1) * P], xf[:, j, k * P:(k + 1) * P], ident[:])
                    fills(i, b)
                return f

            def keep_f(k):
                def f(e):
                    filled(e, f"xfT{k}", c)
                    empties(e.copy(xfT[:, k, :], bank_of(f"xfT{k}")[:]), f"xfT{k}")
                return f
            for k in range(KD):
                add(PLAN["fT"][k], PE_, turn_f(k))
                add(PLAN["fT_keep"][k], AC_, keep_f(k))

            def lg_pe(e):
                emptied(e, "xfT0", c)
                emptied(e, "xfT1", c)
                for j in range(J):
                    for k in range(KD):
                        i = e.matmul(bank_of("logit")[:, j * E:(j + 1) * E], xfT[:, k, j * P:(j + 1) * P], w_gt[:, k, :], start=(k == 0), stop=(k == KD - 1))
                fills(i, "logit")
            add(PLAN["logit"], PE_, lg_pe)

            def take(e):
                filled(e, "logit", c)
                i = e.tensor_copy(lg[:].rearrange("p j e -> p (j e)"), bank_of("logit")[:, 0:J * E])
                empties(i, "logit")
                emptied(e, "logit", c)
                e.nop(nofuse=True)
                for j in range(J):
                    i = e.max(mx[:, j, :], lg[:, j, :])
                return i

            def which(e):
                for j in range(J):
                    i = e.max_index(ix[:, j, :], mx[:, j, :], lg[:, j, :])
                return i

            def as_float(e):
                e.tensor_tensor(dif[:], mx[:, :, 1], mx[:, :, 0], ALU.subtract)
                return e.tensor_copy(ixf[:], ix[:, :, 0:TOPK])

            def one_hot(e):
                for k in range(TOPK):
                    i = e.tensor_tensor(oh[:, k, :, :], iota_e[:].unsqueeze(1).broadcast_to([P, J, E]),
                                        ixf[:, :, k:k + 1].broadcast_to([P, J, E]), ALU.is_equal)
                return i

            def taken(e):
                e.tensor_tensor(mm_[:, 0:J, :], oh[:, 0, :, :], oh[:, 1, :, :], ALU.add).then_inc(s_m, 1)
            chain(add, c, PLAN["route"], s_cr, [take, which, as_float, one_hot, taken])

            def rank_pe(e):
                wait(e, s_m, 1, c, 0)
                room(e, "rank", c)
                m = mm_[:].rearrange("p j e -> p (j e)")
                e.matmul(bank_of("rank")[:, 0:(J + 1) * E], below[:], m, start=True, stop=False)
                for q in range(1, J + 1):
                    i = e.matmul(bank_of("rank")[:, q * E:(J + 1) * E], ones[:], m[:, 0:(J + 1 - q) * E], start=False, stop=(q == J))
                fills(i, "rank")
            add(PLAN["rank"], PE_, rank_pe)

            def e2_act(e):
                wait(e, s_m, 1, c, 0)
                e.activation(e2[:], dif[:], ACT.Exp).then_inc(s_e2, 1)
            add(PLAN["e2"], AC_, e2_act)

            def place(e):
                filled(e, "rank", c)
                return e.tensor_tensor(pos8[:], bank_of("rank")[:, 0:J * E].rearrange("p (j e) -> p j e", e=E),
                                       base[:].unsqueeze(1).broadcast_to([P, J, E]), ALU.add)

            def of_choice(e):
                empties(e.tensor_tensor(base[:], base[:], bank_of("rank")[:, J * E:(J + 1) * E], ALU.add), "rank")
                wait(e, s_e2, 1, c, 0)
                e.tensor_scalar(e2p[:], e2[:], 1.0, None, ALU.add)
                for k in range(TOPK):
                    i = e.tensor_tensor(prd[:, k, :, :], oh[:, k, :, :], pos8[:], ALU.mult)
                return i

            def row_of_choice(e):
                e.reciprocal(p1[:], e2p[:])
                for k in range(TOPK):
                    i = e.tensor_reduce(posf[:, :, k], prd[:, k, :, :], AX.X, ALU.add)
                return i

            def keep_place(e):
                scattered(e)
                e.tensor_copy(gat[:, bass.ds(c.times(J), J), 0], p1[:])
                e.tensor_tensor(gat[:, bass.ds(c.times(J), J), 1], e2[:], p1[:], ALU.mult)
                e.tensor_copy(posa[:, bass.ds(c.times(J), J), :], posf[:])
                e.tensor_copy(expa[:, bass.ds(c.times(J), J), :], ixf[:])
                e.tensor_copy(posl[:], posf[:]).then_inc(s_pos, 1)
            chain(add, c, PLAN["place"], s_cp, [place, of_choice, row_of_choice, keep_place])

            def scatter(j):
                def f(e):
                    wait(e, s_pos, 1, c, 0)
                    wait(e, s_xf, J, c, J - 1)
                    for k in range(TOPK):
                        e.indirect_dma_start(out=xs_d, out_offset=bass.IndirectOffsetOnAxis(ap=posl[:, j, k:k + 1], axis=0),
                                             in_=xf[:, j, :], in_offset=None).then_inc(s_sc, 16)
                return f
            for j in range(J):
                add(PLAN["scatter"][j], PO_, scatter(j))

            def sh_parts(b, w, t):
                i0, n = SIT[t]
                return [lambda e, k=k: e.matmul(bank_of(b)[0:n, :], w[:, k, i0:i0 + n], xfT[:, k, :], start=(k == 0), stop=(k == KD - 1))
                        for k in range(KD)]

            def sh_act(t):
                def f(e):
                    n = SIT[t][1]
                    filled(e, f"sg{t}", c)
                    empties(e.copy(sgs[0:n, t, :], bank_of(f"sg{t}")[0:n, :]), f"sg{t}")
                return f

            def sh_silu(e):
                all_emptied(e, [f"sg{t}" for t in range(len(SIT))], c)
                for t, (i0, n) in enumerate(SIT):
                    e.activation(sgs[0:n, t, :], sgs[0:n, t, :], ACT.Silu).then_inc(s_ssil, 1)
                e.preload_act_table_set(LOGEXP)

            def sh_dve(t):
                def f(e):
                    n = SIT[t][1]
                    wait(e, s_ssil, len(SIT), c, t)
                    filled(e, f"su{t}", c)
                    empties(e.tensor_tensor(sgs[0:n, t, :], sgs[0:n, t, :], bank_of(f"su{t}")[0:n, :], ALU.mult), f"su{t}")
                return f
            for t in range(len(SIT)):
                product(PLAN["sg"][t], PLAN["step"], f"sg{t}", sh_parts(f"sg{t}", w_sg, t), already)
                add(PLAN["sg_keep"][t], AC_, sh_act(t))
                product(PLAN["su"][t], PLAN["step"], f"su{t}", sh_parts(f"su{t}", w_su, t), already)
                add(PLAN["sh_mul"][t], DV_, sh_dve(t))
            add(PLAN["sh_silu"], AC_, sh_silu)

            def h_ready(e):
                emptied(e, f"su{len(SIT) - 1}", c)

            def sd_parts(q):
                return [lambda e, j=j, t=t: e.matmul(bank_of(f"sd{q}")[:, (j % 2) * DM:(j % 2 + 1) * DM], sgs[0:SIT[t][1], t, j * P:(j + 1) * P],
                                                     w_sd[0:SIT[t][1], t, :], start=(t == 0), stop=(t == len(SIT) - 1))
                        for j in (2 * q, 2 * q + 1) for t in range(len(SIT))]

            def sd_act(q):
                def f(e):
                    b = f"sd{q}"
                    filled(e, b, c)
                    wait(e, s_x1, 1, c, 0)
                    empties(e.copy(sh[:, 2 * q:2 * q + 2, :].rearrange("p j d -> p (j d)"), bank_of(b)[:]), b)
                return f
            for q in range(2):
                product(PLAN["sd"][q], PLAN["step"] / 2, f"sd{q}", sd_parts(q), h_ready if q == 0 else already)
                add(PLAN["sd_keep"][q], AC_, sd_act(q))

            def sh_store(e):
                emptied(e, "sd0", c)
                emptied(e, "sd1", c)
                e.dma_start(sh_d[bass.ds(c.times(CH), CH), :].rearrange("(j p) d -> p j d", p=P), sh[:]).then_inc(s_shs, 16)
            add(PLAN["sh_store"], AC_, sh_store)

            def done_sp(e):
                wait(e, s_xf, J, c, J - 1)
                wait(e, s_x1s, 16, c, 15)
            add(SLOTS - 1, SP_, done_sp)
            return s

        def main_act(e, c, par, k):
            n, d = divmod(k, ND)
            if n == 0:
                wait(e, s_dt, ND, c, d)
            wait(e, s_scan, SLOTS, c, k - NA)
            e.activation(bA[k % NA][:], dt[par][:, d, :], ACT.Exp, scale=a_neg[:, d, n:n + 1]).then_inc(s_a, 1)

        def main_pool(e, c, par, k):
            n, d = divmod(k, ND)
            if n == 0:
                wait(e, s_u, ND, c, d)
            if d == 0:
                wait(e, s_bl[n % NR], 16 * NS // NR, c, 16 * (n // NR) + 15)
            wait(e, s_scan, SLOTS, c, k - NB)
            e.tensor_tensor(bb[:, k % NB, :], u[par][:, d, :], br[:, n % NR, :], ALU.mult).then_inc(s_bb, 1)

        def load_b(e, c, n):
            if n == 0:
                wait(e, s_bs, 16, c, 15)
            wait(e, s_bb, SLOTS, c, (n - NR) * ND + ND - 1)
            row = b_d[bass.ds(c.times(NS, n), 1), :].broadcast_to([P, CH])
            e.dma_start(br[:, n % NR, :], row).then_inc(s_bl[n % NR], 16)

        def keep_last(e, c, n):
            wait(e, s_scan, SLOTS, c, n * ND + ND - 1)
            e.tensor_copy(hl[:, n, :], hh[:, n % 2, :, CH - 1]).then_inc(s_hl, 1)

        def main_pe(e, c, par, k, first):
            n, d = divmod(k, ND)
            if not first:
                if d == 0:
                    wait(e, s_scan, SLOTS, c, k - 1)
                wait(e, s_y, SLOTS, c, k - 2 * ND)
                for q in range(ND):
                    i = e.transpose(bH[d][:, q * P:(q + 1) * P], hh[:, (n - 1) % 2, q, d * P:(d + 1) * P], ident[:])
                i.then_inc(s_ht, 1)

        def main_dve(e, c, par, k, first, scan=True):
            n, d = divmod(k, ND)
            if scan:
                wait(e, s_a, SLOTS, c, k)
                wait(e, s_bb, SLOTS, c, k)
                if d == 0:
                    wait(e, s_ht, SLOTS, c, k - ND - 1)
                if par:
                    if k == 0:
                        e.wait_ge(s_hl, c.times(NS // 2, NS // 2))
                else:
                    if d == 0 and n >= 2:
                        e.wait_ge(s_hl, c.times(NS // 2, n - 1))
                e.tensor_tensor_scan(hh[:, n % 2, d, :], bA[k % NA][:], bb[:, k % NB, :], hl[:, n, d:d + 1] if par else 0.0,
                                     ALU.mult, ALU.add).then_inc(s_scan, 1)
            if not first:
                wait(e, s_ht, SLOTS, c, k - ND)
                if n == 0:
                    cm, yy = bc[1 - par][:, d, 2 * NS - 1:2 * NS], yT[1 - par]
                else:
                    cm, yy = bc[par][:, d, NS + n - 1:NS + n], yT[par]
                if n == 1:
                    if d == 0:
                        emptied(e, "bc", c)
                    e.tensor_scalar(yy[:, d, :], bH[d][:], cm, None, ALU.mult).then_inc(s_y, 1)
                else:
                    wait(e, s_y, SLOTS, c, k - 2 * ND)
                    e.scalar_tensor_tensor(out=yy[:, d, :], in0=bH[d][:], scalar=cm, in1=yy[:, d, :],
                                           op0=ALU.mult, op1=ALU.add).then_inc(s_y, 1)

        def main_sync(e, c, par, k):
            if k % ND == 0:
                load_b(e, c, k // ND)

        AHEAD = {AC_: (main_act, PLAN["ahead_act"]), PO_: (main_pool, PLAN["ahead_pool"]), SP_: (main_sync, (NR - 1) * ND)}

        def chunk(e, name, c, par, first=False, last=False):
            side = []
            if not last:
                side.append(pre(c.shift(1), 1 - par))
            if not first:
                side.append(post(c.shift(-1), 1 - par))
            for k in range(SLOTS):
                f = first and k < ND
                if name == SP_:
                    for s in side:
                        for fn in s[(k, name)]:
                            fn(e)
                if name in AHEAD:
                    fn, by = AHEAD[name]
                    if k + by < SLOTS:
                        fn(e, c, par, k + by)
                    elif not last:
                        fn(e, c.shift(1), 1 - par, k + by - SLOTS)
                elif name == PE_:
                    main_pe(e, c, par, k, f)
                elif name == DV_:
                    main_dve(e, c, par, k, f)
                if name == PO_ and par == 0 and k % ND == ND - 1 and k > ND:
                    keep_last(e, c, k // ND - 1)
                for s in side if name != SP_ else ():
                    for fn in s[(k, name)]:
                        fn(e)
            if name == PO_ and par == 0:
                keep_last(e, c, NS - 1)
            if last:
                for d in range(ND):
                    if name == PE_:
                        main_pe(e, c.shift(1), 1 - par, d, False)
                    if name == DV_:
                        main_dve(e, c.shift(1), 1 - par, d, False, scan=False)

        def table_ends(e):
            emptied(e, "rank", Chunk(NCH - 1))
            e.tensor_copy(iopf[:], iop[:])
            e.tensor_scalar(capf[:], iota_e[:], float(CAP), None, ALU.mult)
            e.tensor_copy(tif[:], tii[:])
            e.drain()
            e.tensor_scalar(padf[:], base[:], iopf[:, 0:1], None, ALU.add)
            e.tensor_tensor(cnt[:], base[:], capf[:], ALU.subtract)
            e.drain()
            e.tensor_copy(padi[:], padf[:]).then_inc(s_pad, 1)
            e.tensor_scalar(cnti[:], cnt[:], float(P - 1), None, ALU.add)
            e.drain()
            e.tensor_single_scalar(nti[:], cnti[:], P.bit_length() - 1, ALU.arith_shift_right)
            e.drain()
            e.tensor_copy(ntf[:], nti[:])
            e.drain()
            e.tensor_tensor_scan(cum[:], one8[:], ntf[:], 0.0, ALU.mult, ALU.add)
            e.drain()
            e.tensor_scalar(tot[:], cum[0:1, E - 1:E], -1.0, None, ALU.add)
            e.tensor_tensor(off[:], cum[:], ntf[:], ALU.subtract)
            e.drain()
            e.tensor_scalar(tif[:], tif[:], tot[:, 0:1], None, ALU.min)
            e.tensor_scalar(off[:], off[:], float(P), None, ALU.mult)
            e.drain()
            e.tensor_tensor(off[:], off[:], capf[:], ALU.subtract)

        def table_tiles(e):
            each = [1, NT + 1, E - 1]
            e.drain()
            e.tensor_tensor(ge[:], tif[:].unsqueeze(2).broadcast_to(each), cum[0:1, 0:E - 1].unsqueeze(1).broadcast_to(each), ALU.is_ge)
            e.drain()
            e.tensor_reduce(te[:], ge[:], AX.X, ALU.add)
            e.tensor_tensor(gn[:], ge[:], ntf[0:1, 0:E - 1].unsqueeze(1).broadcast_to(each), ALU.mult)
            e.drain()
            e.tensor_copy(tab[:, 0, :], te[:])
            e.tensor_reduce(tp[:], gn[:], AX.X, ALU.add)
            e.drain()
            e.tensor_scalar(te[:], te[:], float(CAP), None, ALU.mult)
            e.tensor_tensor(tp[:], tif[:], tp[:], ALU.subtract)
            e.drain()
            e.scalar_tensor_tensor(out=tab[:, 1, :], in0=tp[:], scalar=float(P), in1=te[:], op0=ALU.mult, op1=ALU.add)

        def ld(e, s_, dst, src, **kw):
            e.dma_start(dst, src, **kw).then_inc(s_, 16)

        def late_weights(e):
            ld(e, s_w2, w_dt[:], dt_w.rearrange("(k p) n -> p k n", p=P))
            ld(e, s_w2, w_out[:], out_proj_w.rearrange("(k p) n -> p k n", p=P))
            ld(e, s_w2, w_gt[:], gate_w.rearrange("(k p) n -> p k n", p=P))
            ld(e, s_w2, w_sg[:], Sg.rearrange("(k p) n -> p k n", p=P))
            ld(e, s_w2, w_su[:], Su.rearrange("(k p) n -> p k n", p=P))
            for t, (i0, n) in enumerate(SIT):
                ld(e, s_w2, w_sd[0:n, t, :], Sd[i0:i0 + n, :])

        def run(e, name):
            s = pre(Chunk(0), 0)
            for k in range(SLOTS):
                if name == SP_ and k == 1:
                    late_weights(e)
                if name == PE_ and k == min(PLAN["bT"], PLAN["dt"][0]):
                    e.wait_ge(s_w2, 16 * (5 + len(SIT)))
                for fn in s[(k, name)]:
                    fn(e)
            if name in AHEAD:
                fn, by = AHEAD[name]
                for k in range(by):
                    fn(e, Chunk(0), 0, k)
            chunk(e, name, Chunk(0), 0, first=True)
            with e.Fori(0, (NCH - 2) // 2) as i:
                chunk(e, name, Chunk(1, i), 1)
                chunk(e, name, Chunk(2, i), 0)
            chunk(e, name, Chunk(NCH - 1), 1, last=True)
            s = post(Chunk(NCH - 1), 1)
            for k in range(SLOTS):
                for fn in s[(k, name)]:
                    fn(e)
                if name == DV_ and k == PLAN["place"][-1]:
                    table_ends(e)
                if name == DV_ and k == PLAN["sh_mul"][-1]:
                    table_tiles(e)

        block = ctx.enter_context(nc.Block())

        @block.sync
        def _(e):
            ld(e, s_w, w_in[:], in_proj_w.rearrange("(k p) n -> p k n", p=P))
            ld(e, s_w, w_nm[:], norm_w.rearrange("(k p) -> p k", p=P), allow_slow_non_contiguous=True)
            ld(e, s_w, w_cv[:], conv_w.rearrange("(k p) a t -> p k (a t)", p=P))
            ld(e, s_w, w_bc[:, :, 0:NS], B_w.rearrange("(k p) n -> p k n", p=P))
            ld(e, s_w, w_bc[:, :, NS:2 * NS], C_w.rearrange("(k p) n -> p k n", p=P))
            ld(e, s_w, b_dt[:], dt_b.rearrange("(k p) -> p k", p=P), allow_slow_non_contiguous=True)
            ld(e, s_w, a_log[:], A_log.rearrange("(k p) n -> p k n", p=P))
            ld(e, s_w, dskip[:], D_skip.rearrange("(k p) -> p k", p=P), allow_slow_non_contiguous=True)
            run(e, SP_)
            e.wait_ge(s_x1s, 16 * NCH)
            e.wait_ge(s_shs, 16 * NCH + 1)

        @block.gpsimd
        def _(e):
            def sel(t, op, fill, base_, pattern, cm):
                return e.affine_select(out=t, in_=t, compare_op=op, fill=fill, base=base_, pattern=pattern, channel_multiplier=cm)
            e.memset(ident[:], 0.0).then_inc(s_c, 1)
            e.memset(below[:], 1.0).then_inc(s_c, 1)
            e.memset(ones[:], 1.0).then_inc(s_c, 1)
            e.memset(zro[:], 0.0).then_inc(s_c, 1)
            e.memset(one8[:], 1.0).then_inc(s_c, 1)
            e.memset(mm_[:, J, :], 0.0).then_inc(s_c, 1)
            e.iota(iota_i[:], [[1, E]], base=0, channel_multiplier=0).then_inc(s_c, 1)
            e.iota(capi[:], [[CAP, E]], base=0, channel_multiplier=0).then_inc(s_c, 1)
            e.iota(iop[:], [[0, 1]], base=0, channel_multiplier=1).then_inc(s_c, 1)
            e.iota(tii[:], [[1, NT + 1]], base=0, channel_multiplier=0).then_inc(s_c, 1)
            for s_ in [*free.values(), s_shs, s_scd]:
                e.nop(nofuse=True).then_inc(s_, 1)
            e.wait_ge(s_c, 10)
            sel(ident[:], ALU.not_equal, 1.0, 0, [[-1, P]], 1).then_inc(s_id, 1)
            sel(below[:], ALU.is_gt, 0.0, 0, [[1, P]], -1).then_inc(s_id, 1)
            e.wait_ge(s_id, 2)
            e.wait_ge(s_cst, 4)
            run(e, PO_)
            e.wait_ge(s_pad, 1)
            for x_ in range(E):
                e.indirect_dma_start(out=xs_d, out_offset=bass.IndirectOffsetOnAxis(ap=padi[:, x_:x_ + 1], axis=0),
                                     in_=zro[:], in_offset=None).then_inc(s_padd, 16)
            e.wait_ge(s_padd, 16 * E)
            e.wait_ge(s_sc, 16 * J * TOPK * NCH)

        @block.scalar
        def _(e):
            e.wait_ge(s_w, 16 * 8)
            e.activation(a_exp[:], a_log[:], ACT.Exp).then_inc(s_an, 1)
            e.wait_ge(s_an, 1)
            e.mul(a_neg[:], a_exp[:], -1.0).then_inc(s_an, 1)
            e.wait_ge(s_an, 2)
            e.preload_act_table_set(LOGEXP)
            run(e, AC_)

        @block.tensor
        def _(e):
            e.wait_ge(s_id, 2)
            e.wait_ge(s_cst, 4)
            run(e, PE_)

        @block.vector
        def _(e):
            e.wait_ge(s_c, 10)
            e.wait_ge(s_w, 16 * 8)
            for k in range(KD):
                i = e.tensor_scalar(w_in[:, k, :], w_in[:, k, :], w_nm[:, k:k + 1], None, ALU.mult)
            i.then_inc(s_cst, 1)
            e.tensor_copy(iota_e[:], iota_i[:]).then_inc(s_cst, 1)
            e.tensor_copy(base[:], capi[:]).then_inc(s_cst, 1)
            e.wait_ge(s_id, 2)
            for d in range(ND):
                for k in range(TAPS):
                    i = e.tensor_scalar(w_tap[:, d, k, :], ident[:], w_cv[:, d, k:k + 1], None, ALU.mult)
            i.then_inc(s_cst, 1)
            e.wait_ge(s_cst, 4)
            run(e, DV_)



def phase2(nc, sem, Wg, Wu, Wd, x1_d, sh_d, xs_d, ys_d, out_rows, ident, iota_e, off, posa, expa, posi, gat, tab):
    with ExitStack() as ctx:
        def sb(name, shape, dt=F32):
            return ctx.enter_context(nc.sbuf_tensor(name, shape, dt))

        def bank(name):
            return ctx.enter_context(nc.psum_tensor(name, [P, 512], F32))

        NF = len(FIT)
        w_g = sb("w_g", [P, E * KD * FI])
        w_u = sb("w_u", [P, E * KD * FI])
        w_d = sb("w_d", [P, E * NF * DM])
        xt = sb("xt", [P, 2, DM])
        xtT = sb("xtT", [P, 2, KD, P])
        sgm = sb("sgm", [P, 2, FI])
        hm = sb("hm", [P, 2, FI])
        hT = sb("hT", [P, 2, NF, P])
        yt = sb("yt", [P, 2, DM])

        bX = bank("bX"); bG = [bank("bG0"), bank("bG1")]; bU = [bank("bU0"), bank("bU1")]
        bHA = bank("bHA"); bHB = bank("bHB"); bD = bank("bD")

        s_wt = sem("s_wt")
        s_in = [sem("s_in0"), sem("s_in1")]
        s_tx = sem("s_tx"); s_kx = sem("s_kx"); s_g = sem("s_g"); s_gu = sem("s_gu"); s_si = sem("s_si"); s_h = sem("s_h")
        s_th = sem("s_th"); s_ka = sem("s_ka"); s_kb = sem("s_kb"); s_dn = sem("s_dn"); s_yt = sem("s_yt"); s_ys = sem("s_ys")
        NB4 = 4

        def after(e, s_, t, back=0, per=1):
            wait(e, s_, per, t.shift(-back), per - 1)

        def arrived(e, t, par):
            v = t.times(8, 16 - 8 * par)
            e.wait_ge(s_in[par], v)

        def tile_in(e, t, par):
            after(e, s_tx, t, 2)
            row = e.value_load(tab[0:1, 1, bass.ds(t.times(1), 1)], min_val=0, max_val=E * CAP - P)
            e.dma_start(xt[:, par, :], xs_d[bass.ds(row, P), :]).then_inc(s_in[par], 16)

        def tile_out(e, t, par):
            after(e, s_yt, t)
            after(e, s_ys, t, 1, 16)
            e.dma_start(ys_d[bass.ds(t.times(P), P), :], yt[:, par, :]).then_inc(s_ys, 16)

        def turn_in(e, t, par):
            arrived(e, t, par)
            after(e, s_kx, t, 1)
            for k in range(KD):
                i = e.transpose(bX[:, k * P:(k + 1) * P], xt[:, par, k * P:(k + 1) * P], ident[:])
            i.then_inc(s_tx, 1)

        def expert(e, t):
            return e.value_load(tab[0:1, 0, bass.ds(t.times(1), 1)], min_val=0, max_val=E - 1)

        def inner(e, ex, par, w, banks, s_):
            for f in range(2):
                for k in range(KD):
                    i = e.matmul(banks[f][:, 0:FH], xtT[:, par, k, :], w[:, bass.ds(ex * (KD * FI) + (k * FI + f * FH), FH)],
                                 start=(k == 0), stop=(k == KD - 1))
            i.then_inc(s_, 1)

        held = {}

        def gate(e, t, par):
            if t.reg is not None or t.add > 0:
                held["last"] = expert(e, t.shift(-1))
            ex = held["this"] = expert(e, t)
            e.wait_ge(s_wt, ex * 64 + 64)
            e.nop(nofuse=True)
            after(e, s_kx, t)
            after(e, s_si, t, 1)
            inner(e, ex, par, w_g, bG, s_g)

        def up(e, t, par):
            ex = held["this"]
            after(e, s_h, t, 1)
            inner(e, ex, par, w_u, bU, s_gu)

        def turn_h(e, t, par):
            after(e, s_h, t)
            after(e, s_ka, t, 1)
            after(e, s_kb, t, 1)
            for q, (i0, n) in enumerate(FIT):
                b, o = (bHA, q) if q < NB4 else (bHB, q - NB4)
                i = e.transpose(b[0:n, o * P:(o + 1) * P], hm[:, par, i0:i0 + n], ident[:])
            i.then_inc(s_th, 1)

        def down(e, t, par):
            ex = held.pop("last") if "last" in held else expert(e, t)
            after(e, s_ka, t)
            after(e, s_kb, t)
            after(e, s_yt, t, 1)
            for q, (i0, n) in enumerate(FIT):
                i = e.matmul(bD[:, 0:DM], hT[0:n, par, q, :], w_d[0:n, bass.ds(ex * (NF * DM) + q * DM, DM)],
                             start=(q == 0), stop=(q == NF - 1))
            i.then_inc(s_dn, 1)

        def act_keep_x(e, t, par):
            after(e, s_tx, t)
            after(e, s_gu, t, 2)
            e.copy(xtT[:, par, :, :].rearrange("p k q -> p (k q)"), bX[:, 0:KD * P]).then_inc(s_kx, 1)

        def act_silu(e, t, par):
            after(e, s_g, t)
            after(e, s_h, t, 2)
            for f in range(2):
                i = e.activation(sgm[:, par, f * FH:(f + 1) * FH], bG[f][:, 0:FH], ACT.Silu)
            i.then_inc(s_si, 1)

        def act_keep_h(e, t, par):
            after(e, s_th, t)
            after(e, s_dn, t, 2)
            e.copy(hT[:, par, 0:NB4, :].rearrange("p k q -> p (k q)"), bHA[:]).then_inc(s_ka, 1)

        def dve_mul(e, t, par):
            after(e, s_si, t)
            after(e, s_gu, t)
            after(e, s_th, t, 2)
            for f in range(2):
                i = e.tensor_tensor(hm[:, par, f * FH:(f + 1) * FH], sgm[:, par, f * FH:(f + 1) * FH], bU[f][:, 0:FH], ALU.mult)
            i.then_inc(s_h, 1)

        def dve_keep_h(e, t, par):
            after(e, s_th, t)
            after(e, s_dn, t, 2)
            for q in range(NB4, NF):
                n = FIT[q][1]
                i = e.tensor_copy(hT[0:n, par, q, :], bHB[0:n, (q - NB4) * P:(q - NB4 + 1) * P])
            i.then_inc(s_kb, 1)

        def dve_keep_y(e, t, par):
            after(e, s_dn, t)
            after(e, s_ys, t, 2, 16)
            e.tensor_copy(yt[:, par, :], bD[:, 0:DM]).then_inc(s_yt, 1)

        def stream(e, work, n, ring, start):
            lags = [lag for _, lag in work]

            def step(t):
                for fn, lag in work:
                    if t.reg is not None or 0 <= t.add - lag < n:
                        fn(e, t.shift(-lag), (t.add - lag) % ring)

            loops = (n + min(lags) - start) // ring
            for t in range(min(lags), start):
                step(Chunk(t))
            with e.Fori(0, loops) as i:
                for k in range(ring):
                    step(Chunk(start + k, i, ring))
            for t in range(start + loops * ring, n + max(lags)):
                step(Chunk(t))

        def tiles(e, work):
            stream(e, work, NT, 2, 3)

        UT = 2
        NU = NTOK // P // UT
        R = 4
        gidx = sb("gidx", [P, R, UT, TOPK], U32)
        gwt = sb("gwt", [P, R, UT, TOPK])
        yg = sb("yg", [P, R, TOPK, UT, DM])
        x1u = sb("x1u", [P, R, UT, DM])
        shu = sb("shu", [P, R, UT, DM])
        ou = sb("ou", [P, R, UT, DM])
        st = sb("st3", [P, UT, 6])
        mv = sb("mv3", [P, R, UT, 2])
        va = sb("va3", [P, R, UT])
        rr = sb("rr3", [P, R, UT])
        tn = sb("tn3", [P, UT])
        nm = sb("nm3", [P, R, UT])
        s_gi = sem("s_gi"); s_rows = sem("s_rows")
        s_yg = [sem(f"s_yg{b}") for b in range(R)]
        s_xu = [sem(f"s_xu{b}") for b in range(R)]
        s_out = [sem(f"s_out{b}") for b in range(R)]
        s_f1 = sem("s_f1"); s_f2 = sem("s_f2"); s_f3 = sem("s_f3"); s_f4 = sem("s_f4"); s_f5 = sem("s_f5")

        def landed(e, sems, per, u, b):
            v = u.times(per // R, per - per * b // R)
            if isinstance(v, int) and v <= 0:
                return
            e.wait_ge(sems[b], v)
            if not isinstance(v, int) and e.engine in (POOL, SYNC):
                e.nop(nofuse=True)

        def u_gather(e, u, b):
            wait(e, s_f1, 1, u.shift(-R), 0)
            e.tensor_copy(gidx[:, b, :, :], posi[:, bass.ds(u.times(UT), UT), :]).then_inc(s_gi, 1)
            e.tensor_copy(gwt[:, b, :, :], gat[:, bass.ds(u.times(UT), UT), :]).then_inc(s_gi, 1)
            wait(e, s_gi, 2, u, 1)
            for k in range(TOPK):
                for q in range(UT):
                    e.indirect_dma_start(out=yg[:, b, k, q, :], out_offset=None, in_=ys_d,
                                         in_offset=bass.IndirectOffsetOnAxis(ap=gidx[:, b, q, k:k + 1], axis=0)).then_inc(s_yg[b], 16)

        def u_load(e, u, b):
            wait(e, s_f5, 1, u.shift(-R), 0)
            rows = lambda d: d[bass.ds(u.times(UT * P), UT * P), :].rearrange("(j p) d -> p j d", p=P)
            e.dma_start(x1u[:, b, :, :], rows(x1_d)).then_inc(s_xu[b], 16)
            e.dma_start(shu[:, b, :, :], rows(sh_d)).then_inc(s_xu[b], 16)

        def u_store(e, u, b):
            wait(e, s_f5, 1, u, 0)
            rows = out_rows[bass.ds(u.times(UT * P), UT * P), :].rearrange("(j p) d -> p j d", p=P)
            e.dma_start(rows, ou[:, b, :, :]).then_inc(s_out[b], 16)

        def u_step(e, u, b):
            now = u.reg is not None or u.add < NU
            before = u.reg is not None or 1 <= u.add <= NU
            b1, u1 = (b - 1) % R, u.shift(-1)
            r = rr[:, b1, :]

            def weigh(k):
                for q in range(UT):
                    e.scalar_tensor_tensor(out=shu[:, b, q, :], in0=yg[:, b, k, q, :], scalar=gwt[:, b, q, k:k + 1],
                                           in1=shu[:, b, q, :], op0=ALU.mult, op1=ALU.add)

            if now:
                landed(e, s_xu, 32, u, b)
                wait(e, s_gi, 2, u, 1)
                landed(e, s_yg, 16 * UT * TOPK, u, b)
                weigh(0)
                e.drain()
                weigh(1)
            if before:
                wait(e, s_f2, 1, u1, 0)
                e.tensor_tensor(tn[:], r, r, ALU.mult)
            e.drain()
            if now:
                for q in range(UT):
                    e.bn_stats(st[:, q, :], shu[:, b, q, :])
            if before:
                e.tensor_tensor(tn[:], tn[:], va[:, b1, :], ALU.mult)
            e.drain()
            if now:
                for q in range(UT):
                    e.bn_aggr(mv[:, b, q, :], st[:, q, :])
            if before:
                e.tensor_scalar(tn[:], tn[:], -0.5, 1.5, ALU.mult, ALU.add)
            e.drain()
            if now:
                e.tensor_scalar(va[:, b, :], mv[:, b, :, 1], EPS_LN, None, ALU.add).then_inc(s_f1, 1)
            if before:
                e.tensor_tensor(r, r, tn[:], ALU.mult)
                e.drain()
                e.scalar_tensor_tensor(out=nm[:, b1, :], in0=mv[:, b1, :, 0], scalar=-1.0, in1=r, op0=ALU.mult, op1=ALU.mult).then_inc(s_f3, 1)
            if u.reg is not None or u.add >= 2:
                u_add(e, u.shift(-2), (b - 2) % R)

        def u_steps(e):
            start = 2
            loops = (NU - start) // R
            for t in range(start):
                u_step(e, Chunk(t), t % R)
            with e.Fori(0, loops) as i:
                for k in range(R):
                    u_step(e, Chunk(start + k, i, R), (start + k) % R)
            for t in range(start + loops * R, NU + 2):
                u_step(e, Chunk(t), t % R)

        def u_root(e, u, b):
            wait(e, s_f1, 1, u, 0)
            e.activation(rr[:, b, :], va[:, b, :], ACT.Ln)
            e.drain()
            e.activation(rr[:, b, :], rr[:, b, :], ACT.Exp, scale=-0.5).then_inc(s_f2, 1)

        def u_norm(e, u, b):
            wait(e, s_f3, 1, u, 0)
            landed(e, s_out, 16, u.shift(-R), b)
            for q in range(UT):
                i = e.activation(ou[:, b, q, :], shu[:, b, q, :], ACT.Identity, scale=rr[:, b, q:q + 1], bias=nm[:, b, q:q + 1])
            i.then_inc(s_f4, 1)

        def u_add(e, u, b):
            wait(e, s_f4, 1, u, 0)
            e.tensor_tensor(ou[:, b, :, :].rearrange("p j d -> p (j d)"), x1u[:, b, :, :].rearrange("p j d -> p (j d)"),
                            ou[:, b, :, :].rearrange("p j d -> p (j d)"), ALU.add).then_inc(s_f5, 1)

        adj = sb("adj", [P, NTOK // P * TOPK])

        def output_rows(e):
            pa, ea = (t[:].rearrange("p t k -> p (t k)") for t in (posa, expa))
            each = [P, NTOK // P * TOPK, E]
            adj8 = yg[:, 0, 0, :, :].rearrange("p q (t e) -> p (q t) e", e=E)
            e.tensor_tensor(adj8, ea.unsqueeze(2).broadcast_to(each), iota_e[:].unsqueeze(1).broadcast_to(each), ALU.is_equal)
            e.drain()
            e.tensor_tensor(adj8, adj8, off[:].unsqueeze(1).broadcast_to(each), ALU.mult)
            e.drain()
            e.tensor_reduce(adj[:], adj8, AX.X, ALU.add)
            e.drain()
            e.tensor_tensor(pa, pa, adj[:], ALU.add)
            e.drain()
            e.tensor_copy(posi[:].rearrange("p t k -> p (t k)"), pa).then_inc(s_rows, 1)

        block = ctx.enter_context(nc.Block())

        @block.sync
        def _(e):
            for x_ in range(E):
                n = NF - 1
                o = x_ * KD * FI
                e.dma_start(w_g[:, o:o + KD * FI].rearrange("p (k n) -> p k n", k=KD), Wg[x_].rearrange("(k p) n -> p k n", p=P)).then_inc(s_wt, 16)
                e.dma_start(w_u[:, o:o + KD * FI].rearrange("p (k n) -> p k n", k=KD), Wu[x_].rearrange("(k p) n -> p k n", p=P)).then_inc(s_wt, 16)
                o = x_ * NF * DM
                e.dma_start(w_d[:, o:o + n * DM].rearrange("p (k n) -> p k n", k=n), Wd[x_][0:n * P, :].rearrange("(k p) n -> p k n", p=P)).then_inc(s_wt, 16)
                e.dma_start(w_d[0:FI - n * P, o + n * DM:o + NF * DM], Wd[x_][n * P:FI, :]).then_inc(s_wt, 16)
                e.wait_ge(s_wt, 64 * (x_ + 1))
            stream(e, [(u_store, 0), (u_load, -R)], NU, R, 0)
            for b in range(R):
                e.wait_ge(s_out[b], 16 * NU // R)

        @block.gpsimd
        def _(e):
            tiles(e, [(tile_in, -1), (tile_out, 1)])
            e.wait_ge(s_ys, 16 * NT)
            e.wait_ge(s_rows, 1)
            stream(e, [(u_gather, 0)], NU, R, R)

        @block.tensor
        def _(e):
            tiles(e, [(gate, 0), (turn_h, 1), (up, 0), (turn_in, -1), (down, 1)])

        @block.scalar
        def _(e):
            tiles(e, [(act_silu, 0), (act_keep_h, 1), (act_keep_x, -1)])
            e.preload_act_table_set(LOGEXP)
            stream(e, [(u_root, 0), (u_norm, 1)], NU, R, R + 1)

        @block.vector
        def _(e):
            output_rows(e)
            tiles(e, [(dve_keep_h, 1), (dve_mul, 0), (dve_keep_y, 1)])
            u_steps(e)


_INS = ["L0_attn_x", "L0_attn_norm_w", "L0_attn_in_proj_w", "L0_attn_conv_w", "L0_attn_dt_w", "L0_attn_dt_b",
        "L0_attn_A_log", "L0_attn_B_w", "L0_attn_C_w", "L0_attn_D_skip", "L0_attn_out_proj_w",
        "L0_ffn_gate_w", "L0_ffn_Wg", "L0_ffn_Wu", "L0_ffn_Wd", "L0_ffn_Sg", "L0_ffn_Su", "L0_ffn_Sd"]


def kernel(**inputs):
    import numpy as _np
    import concourse.bacc as _bacc
    from concourse import mybir as _mybir
    from concourse.bass_utils import run_bass_kernel_spmd as _run

    nc = _bacc.Bacc("TRN2", target_bir_lowering=False, num_devices=1)
    arrays, args = {}, []
    for name in _INS:
        a = _np.ascontiguousarray(inputs[name])
        arrays[f"in_{name}_dram"] = a
        args.append(nc.dram_tensor(f"in_{name}_dram", a.shape, _mybir.dt.from_np(a.dtype), kind="ExternalInput").ap())
    args.append(nc.dram_tensor("out_0_dram", inputs["L0_attn_x"].shape, _mybir.dt.float32, kind="ExternalOutput").ap())
    build(nc, *args)
    r = _run(nc, [arrays], core_ids=[0])
    return r.results[0]["out_0_dram"]
```
